# Optimizing a Trainium2 kernel written in Bass

```python
import numpy as np
import jax
import jax.numpy as jnp

def _softmax(x, axis=-1):
    return jax.nn.softmax(x, axis=axis)

def _gelu(x):
    return jax.nn.gelu(x, approximate=True)

def _silu(x):
    return jax.nn.silu(x)

def _sigmoid(x):
    return jax.nn.sigmoid(x)

def _layernorm(x, axis=-1, eps=1e-05):
    m = jnp.mean(x, axis=axis, keepdims=True)
    v = jnp.var(x, axis=axis, keepdims=True)
    return (x - m) / jnp.sqrt(v + eps)

def _scatter_add(tgt, idx, src, axis=0):
    return tgt.at[idx].add(src)

def _segment_sum(src, seg, n):
    return jax.ops.segment_sum(src, seg, n)
kernel_name = 'mk_xattn_ffn_d2_seqx_r8_6c09df'

def setup_inputs(seed: int=0):
    np.random.seed(seed)
    _w = jnp.asarray

    def _rec_inputs():
        import jax
        import jax.numpy as jnp
        _rk = jax.random.key(seed)
        x = -0.0002928 + 1 * jax.random.normal(jax.random.fold_in(_rk, 1), (4, 512, 128), jnp.float32)
        _lenS = 512 - jax.random.randint(jax.random.fold_in(_rk, 7), (4,), 0, max(1, 512 // 4) + 1, jnp.int32)
        _lenS2 = 77 - jax.random.randint(jax.random.fold_in(_rk, 8), (4,), 0, max(1, 77 // 4) + 1, jnp.int32)
        _ctx_1024P = jax.random.normal(jax.random.fold_in(_rk, 11), (4, 16, 128), jnp.float32)
        _ctx_1024c = jax.random.dirichlet(jax.random.fold_in(_rk, 511), 0.3 * jnp.ones((16,), jnp.float32), (4, 77))
        _ctx_1024t = jnp.einsum('bsk,bkd->bsd', _ctx_1024c, _ctx_1024P)
        _ctx_1024t = _ctx_1024t * jax.lax.rsqrt(jnp.mean(jnp.square(_ctx_1024t)) + 1e-12) * 0.953939
        ctx_1024 = -1.39393e-06 + 0.999914 * (_ctx_1024t + 0.3 * jax.random.normal(jax.random.fold_in(_rk, 611), (4, 77, 128), jnp.float32))
        _validS = jnp.arange(512)[None, :] < _lenS[:, None]
        _validS2 = jnp.arange(77)[None, :] < _lenS2[:, None]
        _causal = jnp.tril(jnp.ones((512, 512), dtype=bool))
        mask_Bx1xSxS2_ik1 = jnp.where(jnp.broadcast_to(_validS2[:, None, None, :], (4, 1, 512, 77)), 1, 0).astype(jnp.int32)
        mask_BxSxS2_bk1 = jnp.broadcast_to(_validS2[:, None, :], (4, 512, 77))
        return (x, ctx_1024, mask_Bx1xSxS2_ik1, mask_BxSxS2_bk1)
    x, ctx_1024, mask_Bx1xSxS2_ik1, mask_BxSxS2_bk1 = _rec_inputs()

    def _L0_xattn_setup():
        import jax, jax.numpy as jnp
        import numpy as np
        EMBED = 128
        HEADS = 16
        HEAD_DIM = EMBED // HEADS
        key = jax.random.key(seed)
        ks = jax.random.split(key, 9)
        N, Q, K = (2, 256, 256)
        queries = jax.random.normal(ks[0], (N, Q, EMBED), dtype=jnp.float32)
        keys_ = jax.random.normal(ks[1], (N, K, EMBED), dtype=jnp.float32)
        values = jax.random.normal(ks[2], (N, K, EMBED), dtype=jnp.float32)
        mask = jax.random.randint(ks[3], (N, 1, Q, K), 0, 2, dtype=jnp.int32)
        s = 1.0 / np.sqrt(EMBED)
        Wq = jax.random.normal(ks[4], (EMBED, EMBED), dtype=jnp.float32) * s
        Wk = jax.random.normal(ks[5], (EMBED, EMBED), dtype=jnp.float32) * s
        Wv = jax.random.normal(ks[6], (EMBED, EMBED), dtype=jnp.float32) * s
        Wo = jax.random.normal(ks[7], (EMBED, EMBED), dtype=jnp.float32) * s
        bo = jax.random.normal(ks[8], (EMBED,), dtype=jnp.float32) * s
        return {'queries': queries, 'keys': keys_, 'values': values, 'mask': mask, 'Wq': Wq, 'Wk': Wk, 'Wv': Wv, 'Wo': Wo, 'bo': bo}
    _L0_xattn_all = _L0_xattn_setup()
    _L0_xattn_in = {k: v for k, v in _L0_xattn_all.items() if k in ('Wq', 'Wk', 'Wv', 'Wo', 'bo')}
    del _L0_xattn_all

    def _L0_ffn_setup():
        import jax, jax.numpy as jnp
        import numpy as np
        D_MODEL, D_FF, N_EXPERTS, TOP_K = (128, 256, 8, 2)
        B, S = (2, 256)
        key = jax.random.key(seed)
        k1, k2, k3, k4 = jax.random.split(key, 4)
        scale = 0.02
        return {'x': jax.random.normal(k1, (B, S, D_MODEL), dtype=jnp.float32), 'gate_w': jax.random.normal(k2, (D_MODEL, N_EXPERTS), dtype=jnp.float32) * scale, 'w1': jax.random.normal(k3, (N_EXPERTS, D_MODEL, D_FF), dtype=jnp.float32) * scale, 'w2': jax.random.normal(k4, (N_EXPERTS, D_FF, D_MODEL), dtype=jnp.float32) * scale}
    _L0_ffn_all = _L0_ffn_setup()
    _L0_ffn_in = {k: v for k, v in _L0_ffn_all.items() if k in ('gate_w', 'w1', 'w2')}
    del _L0_ffn_all

    def _L1_xattn_setup():
        import jax, jax.numpy as jnp
        import numpy as np
        B, S, E, H = (2, 256, 128, 16)
        HD = E // H
        NEG = -1e+24
        key = jax.random.key(seed)
        ks = jax.random.split(key, 20)
        sc_e = 1.0 / np.sqrt(E)
        inp = {'q_matrix': jax.random.normal(ks[0], (B, S, E), jnp.float32), 'k_matrix': jax.random.normal(ks[1], (B, S, E), jnp.float32), 'v_matrix': jax.random.normal(ks[2], (B, S, E), jnp.float32), 'mask': jax.random.randint(ks[3], (B, S, S), 0, 2).astype(bool), 'Wq': jax.random.normal(ks[4], (E, E), jnp.float32) * sc_e, 'bq': jnp.zeros((E,), jnp.float32), 'Wk': jax.random.normal(ks[5], (E, E), jnp.float32) * sc_e, 'bk': jnp.zeros((E,), jnp.float32), 'Wv': jax.random.normal(ks[6], (E, E), jnp.float32) * sc_e, 'bv': jnp.zeros((E,), jnp.float32), 'Whq': jax.random.normal(ks[7], (H, E, HD), jnp.float32) * sc_e, 'bhq': jnp.zeros((H, HD), jnp.float32), 'Whk': jax.random.normal(ks[8], (H, E, HD), jnp.float32) * sc_e, 'bhk': jnp.zeros((H, HD), jnp.float32), 'Whv': jax.random.normal(ks[9], (H, E, HD), jnp.float32) * sc_e, 'bhv': jnp.zeros((H, HD), jnp.float32), 'Wo': jax.random.normal(ks[10], (E, E), jnp.float32) * sc_e, 'bo': jnp.zeros((E,), jnp.float32)}
        return inp
    _L1_xattn_all = _L1_xattn_setup()
    _L1_xattn_in = {k: v for k, v in _L1_xattn_all.items() if k in ('Wq', 'bq', 'Wk', 'bk', 'Wv', 'bv', 'Whq', 'bhq', 'Whk', 'bhk', 'Whv', 'bhv', 'Wo', 'bo')}
    del _L1_xattn_all

    def _L1_ffn_setup():
        import jax, jax.numpy as jnp
        import numpy as np
        EPS_LN = 1e-05
        EPS_GATE = 1e-08

        def layer_norm(x, gamma, beta):
            mu = jnp.mean(x, axis=-1, keepdims=True)
            var = jnp.mean(jnp.square(x - mu), axis=-1, keepdims=True)
            return (x - mu) * jax.lax.rsqrt(var + EPS_LN) * gamma + beta
        key = jax.random.key(seed)
        ks = jax.random.split(key, 8)
        B, S, D, E, H = (4, 512, 128, 4, 256)
        s_in = 1.0 / np.sqrt(D)
        s_h = 1.0 / np.sqrt(H)
        return {'h': jax.random.normal(ks[0], (B, S, D), dtype=jnp.float32), 'router_w': jax.random.uniform(ks[1], (E, D), jnp.float32, -s_in, s_in), 'rn_g': jnp.ones((D,), jnp.float32), 'rn_b': jnp.zeros((D,), jnp.float32), 'w1': jax.random.uniform(ks[2], (E, D, H), jnp.float32, -s_in, s_in), 'ln_g': jnp.ones((E, H), jnp.float32), 'ln_b': jnp.zeros((E, H), jnp.float32), 'w2': jax.random.uniform(ks[3], (E, H, D), jnp.float32, -s_h, s_h), 'on_g': jnp.ones((D,), jnp.float32), 'on_b': jnp.zeros((D,), jnp.float32)}
    _L1_ffn_all = _L1_ffn_setup()
    _L1_ffn_in = {k: v for k, v in _L1_ffn_all.items() if k in ('router_w', 'rn_g', 'rn_b', 'w1', 'ln_g', 'ln_b', 'w2', 'on_g', 'on_b')}
    del _L1_ffn_all
    return {'x': x, 'ctx_1024': ctx_1024, 'mask_Bx1xSxS2_ik1': mask_Bx1xSxS2_ik1, 'mask_BxSxS2_bk1': mask_BxSxS2_bk1, 'L0_xattn_Wq': _L0_xattn_in['Wq'], 'L0_xattn_Wk': _L0_xattn_in['Wk'], 'L0_xattn_Wv': _L0_xattn_in['Wv'], 'L0_xattn_Wo': _L0_xattn_in['Wo'], 'L0_xattn_bo': _L0_xattn_in['bo'], 'L0_ffn_gate_w': _L0_ffn_in['gate_w'], 'L0_ffn_w1': _L0_ffn_in['w1'], 'L0_ffn_w2': _L0_ffn_in['w2'], 'L1_xattn_Wq': _L1_xattn_in['Wq'], 'L1_xattn_bq': _L1_xattn_in['bq'], 'L1_xattn_Wk': _L1_xattn_in['Wk'], 'L1_xattn_bk': _L1_xattn_in['bk'], 'L1_xattn_Wv': _L1_xattn_in['Wv'], 'L1_xattn_bv': _L1_xattn_in['bv'], 'L1_xattn_Whq': _L1_xattn_in['Whq'], 'L1_xattn_bhq': _L1_xattn_in['bhq'], 'L1_xattn_Whk': _L1_xattn_in['Whk'], 'L1_xattn_bhk': _L1_xattn_in['bhk'], 'L1_xattn_Whv': _L1_xattn_in['Whv'], 'L1_xattn_bhv': _L1_xattn_in['bhv'], 'L1_xattn_Wo': _L1_xattn_in['Wo'], 'L1_xattn_bo': _L1_xattn_in['bo'], 'L1_ffn_router_w': _L1_ffn_in['router_w'], 'L1_ffn_rn_g': _L1_ffn_in['rn_g'], 'L1_ffn_rn_b': _L1_ffn_in['rn_b'], 'L1_ffn_w1': _L1_ffn_in['w1'], 'L1_ffn_ln_g': _L1_ffn_in['ln_g'], 'L1_ffn_ln_b': _L1_ffn_in['ln_b'], 'L1_ffn_w2': _L1_ffn_in['w2'], 'L1_ffn_on_g': _L1_ffn_in['on_g'], 'L1_ffn_on_b': _L1_ffn_in['on_b']}

def reference(x, ctx_1024, mask_Bx1xSxS2_ik1, mask_BxSxS2_bk1, L0_xattn_Wq, L0_xattn_Wk, L0_xattn_Wv, L0_xattn_Wo, L0_xattn_bo, L0_ffn_gate_w, L0_ffn_w1, L0_ffn_w2, L1_xattn_Wq, L1_xattn_bq, L1_xattn_Wk, L1_xattn_bk, L1_xattn_Wv, L1_xattn_bv, L1_xattn_Whq, L1_xattn_bhq, L1_xattn_Whk, L1_xattn_bhk, L1_xattn_Whv, L1_xattn_bhv, L1_xattn_Wo, L1_xattn_bo, L1_ffn_router_w, L1_ffn_rn_g, L1_ffn_rn_b, L1_ffn_w1, L1_ffn_ln_g, L1_ffn_ln_b, L1_ffn_w2, L1_ffn_on_g, L1_ffn_on_b):
    import jax
    import jax.numpy as jnp

    def _L0_xattn_ref(queries, keys, values, mask, Wq, Wk, Wv, Wo, bo):
        import jax, jax.numpy as jnp
        import numpy as np
        EMBED = 128
        HEADS = 16
        HEAD_DIM = EMBED // HEADS
        N, Qlen, _ = queries.shape
        Klen = keys.shape[1]
        q = (queries @ Wq.T).reshape(N, Qlen, HEADS, HEAD_DIM)
        k = (keys @ Wk.T).reshape(N, Klen, HEADS, HEAD_DIM)
        v = (values @ Wv.T).reshape(N, Klen, HEADS, HEAD_DIM)
        energy = jnp.einsum('nqhd,nkhd->nhqk', q, k)
        energy = jnp.where(mask == 0, jnp.float32(-1e+20), energy)
        attention = jax.nn.softmax(energy / jnp.sqrt(jnp.float32(EMBED)), axis=3)
        out = jnp.einsum('nhqk,nkhd->nqhd', attention, v).reshape(N, Qlen, EMBED)
        return out @ Wo.T + bo

    def _L0_ffn_ref(x, gate_w, w1, w2):
        import jax, jax.numpy as jnp
        import numpy as np
        D_MODEL, D_FF, N_EXPERTS, TOP_K = (128, 256, 8, 2)
        B, S = (2, 256)
        router_logits = jnp.einsum('bsd,de->bse', x, gate_w)
        top_logits, top_idx = jax.lax.top_k(router_logits, TOP_K)
        top_w = jax.nn.softmax(top_logits, axis=-1)
        combine = jnp.sum(jax.nn.one_hot(top_idx, N_EXPERTS, dtype=x.dtype) * top_w[..., None], axis=-2)
        h = jax.nn.silu(jnp.einsum('bsd,edf->ebsf', x, w1))
        y = jnp.einsum('ebsf,efd->ebsd', h, w2)
        out = jnp.einsum('ebsd,bse->bsd', y, combine)
        return out

    def _L1_xattn_ref(q_matrix, k_matrix, v_matrix, mask, Wq, bq, Wk, bk, Wv, bv, Whq, bhq, Whk, bhk, Whv, bhv, Wo, bo):
        import jax, jax.numpy as jnp
        import numpy as np
        B, S, E, H = (2, 256, 128, 16)
        HD = E // H
        NEG = -1e+24
        qg = q_matrix @ Wq + bq
        kg = k_matrix @ Wk + bk
        vg = v_matrix @ Wv + bv
        qh = jnp.einsum('bse,hed->bhsd', qg, Whq) + bhq[None, :, None, :]
        kh = jnp.einsum('bse,hed->bhsd', kg, Whk) + bhk[None, :, None, :]
        vh = jnp.einsum('bse,hed->bhsd', vg, Whv) + bhv[None, :, None, :]
        scores = jnp.einsum('bhsd,bhtd->bhst', qh, kh) / jnp.sqrt(jnp.float32(HD))
        scores = jnp.where(mask[:, None, :, :], NEG, scores)
        weights = jax.nn.softmax(scores, axis=-1)
        out = jnp.einsum('bhst,bhtd->bhsd', weights, vh)
        x = out.transpose(0, 2, 1, 3).reshape(out.shape[0], out.shape[2], E)
        return x @ Wo + bo

    def _L1_ffn_ref(h, router_w, rn_g, rn_b, w1, ln_g, ln_b, w2, on_g, on_b):
        import jax, jax.numpy as jnp
        import numpy as np
        EPS_LN = 1e-05
        EPS_GATE = 1e-08

        def layer_norm(x, gamma, beta):
            mu = jnp.mean(x, axis=-1, keepdims=True)
            var = jnp.mean(jnp.square(x - mu), axis=-1, keepdims=True)
            return (x - mu) * jax.lax.rsqrt(var + EPS_LN) * gamma + beta
        D = h.shape[-1]
        h_norm = layer_norm(h, rn_g, rn_b)
        g = jax.nn.softmax(jnp.einsum('bsd,ed->bse', h_norm, router_w), axis=-1)
        top2_w, top2_idx = jax.lax.top_k(g, 2)
        top2_w = top2_w / (jnp.sum(top2_w, axis=-1, keepdims=True) + EPS_GATE)
        hid = jnp.einsum('bsd,edh->bseh', h, w1)
        hid = jax.nn.relu(layer_norm(hid, ln_g, ln_b))
        expert_out = jnp.einsum('bseh,ehd->bsed', hid, w2)
        idx = jnp.broadcast_to(top2_idx[..., None], top2_idx.shape + (D,))
        top2_out = jnp.take_along_axis(expert_out, idx, axis=-2)
        out = jnp.sum(top2_out * top2_w[..., None], axis=-2)
        return layer_norm(out, on_g, on_b)
    x = x + _L0_xattn_ref(_layernorm(x, axis=-1), ctx_1024, ctx_1024, mask_Bx1xSxS2_ik1, L0_xattn_Wq, L0_xattn_Wk, L0_xattn_Wv, L0_xattn_Wo, L0_xattn_bo)
    x = x + _L0_ffn_ref(_layernorm(x, axis=-1), L0_ffn_gate_w, L0_ffn_w1, L0_ffn_w2)
    x = x + _L1_xattn_ref(_layernorm(x, axis=-1), ctx_1024, ctx_1024, mask_BxSxS2_bk1, L1_xattn_Wq, L1_xattn_bq, L1_xattn_Wk, L1_xattn_bk, L1_xattn_Wv, L1_xattn_bv, L1_xattn_Whq, L1_xattn_bhq, L1_xattn_Whk, L1_xattn_bhk, L1_xattn_Whv, L1_xattn_bhv, L1_xattn_Wo, L1_xattn_bo)
    x = x + _L1_ffn_ref(_layernorm(x, axis=-1), L1_ffn_router_w, L1_ffn_rn_g, L1_ffn_rn_b, L1_ffn_w1, L1_ffn_ln_g, L1_ffn_ln_b, L1_ffn_w2, L1_ffn_on_g, L1_ffn_on_b)
    return x

_drawn_inputs = setup_inputs


def setup_inputs(seed=0):
    import zlib

    import numpy as np

    out = dict(_drawn_inputs(seed))
    spreads = {'L1_xattn_bq': (0.0, 0.1),
     'L1_xattn_bk': (0.0, 0.1),
     'L1_xattn_bv': (0.0, 0.1),
     'L1_xattn_bhq': (0.0, 0.1),
     'L1_xattn_bhk': (0.0, 0.1),
     'L1_xattn_bhv': (0.0, 0.1),
     'L1_xattn_bo': (0.0, 0.1),
     'L1_ffn_rn_g': (1.0, 0.2),
     'L1_ffn_rn_b': (0.0, 0.1),
     'L1_ffn_ln_g': (1.0, 0.2),
     'L1_ffn_ln_b': (0.0, 0.1),
     'L1_ffn_on_g': (1.0, 0.2),
     'L1_ffn_on_b': (0.0, 0.1)}
    factors = {}
    for name, (base, spread) in spreads.items():
        noise = np.random.default_rng([zlib.crc32(name.encode()), seed]).standard_normal(out[name].shape)
        drawn = base * np.exp(spread * noise) if base else spread * noise
        out[name] = jnp.asarray(drawn.astype(out[name].dtype))
    for name, factor in factors.items():
        out[name] = (out[name] * factor).astype(out[name].dtype)
    return out
```

```python
from contextlib import ExitStack

import concourse.bass as bass
from concourse import mybir

F32 = mybir.dt.float32
F32R = mybir.dt.float32r
BF16 = mybir.dt.bfloat16
I32 = mybir.dt.int32
U8 = mybir.dt.uint8
U32 = mybir.dt.uint32
ALU = mybir.AluOpType
ACT = mybir.ActivationFunctionType
AX_X = mybir.AxisListType.X

P = 128
B, S, D = 4, 512, 128
NT = S // P
KEYS = 77
H, HD = 16, 8
HALF = H // 2
HK = HALF * KEYS
NCH = -(-HK // P)
HKP = NCH * P
QH = HALF // 2
QW = QH * KEYS
E0, FF0 = 8, 256
E1, FF1 = 4, 256
CROW = 96
CK = CROW + H
BIG = 2.0 ** 100
LOWEST = -3.0e38
EPS = 1e-5
EPS_GATE = 1e-8
SCALE = (float(D) ** -0.5, float(HD) ** -0.5)
TURNS = B // 2


class Unit:
    def __init__(self, at, kind, layer, par):
        self.at, self.kind, self.layer, self.par = at, kind, layer, par


UNITS = [Unit(2 * n + par, kind, layer, par)
         for n, (kind, layer) in enumerate([("attn", 0), ("moe0", 0), ("attn", 1), ("moe1", 1)])
         for par in range(2)]


def head_of(u):
    if u is None:
        return [[] for _ in range(9)]
    if u.kind == "attn":
        return [[("mask", u, 0), ("ln", u, 0), ("attn_bias", u, 0), ("values_in", u, 0),
                 ("keys", u, 0), ("keys", u, 1)],
                [("mask_T", u, 0)], [("xhat_T", u, 0)], [("row_valid", u, 0)],
                [("query", u, 0)], [("query", u, 1)], [("values", u, 0)], [("values", u, 1)], []]
    if u.kind == "moe0":
        return [[("ln", u, 0)], [("xhat_T", u, 0)], [("gate", u, 0)], [("route", u, 0)], [], [], [], [], []]
    return [[("ln", u, 0), ("ln2", u, 0)], [("xhat_T", u, 0)], [("gate", u, 0)],
            [("fold", u, 0), ("route", u, 0)], [], [], [], [], []]


def body_of(u, gap):
    if u.kind == "attn":
        out = [("peak", u, s) for s in range(2 * NT)]
        out += [("peak_T", u, 0)] + gap[0]
        n = 2 * NCH
        at = {2: 1, 4: 2, 5: 3, 6: 4, 7: 5, 8: 6, 9: 7}
        for j in range(n):
            out += [("scores", u, j)]
            if j:
                out += [("weigh", u, j - 1)]
            if j == NCH:
                out += [("norm", u, 0)]
            if j in at:
                out += gap[at[j]]
        out += [("weigh", u, n - 1), ("norm", u, 1)] + gap[8] + [("attn_out", u, 0)]
        return out
    if u.kind == "moe0":
        out = []
        for e in range(E0):
            out += [("up0", u, 2 * e), ("up0", u, 2 * e + 1)]
            if e:
                out += [("down0", u, e - 1)]
            out += gap[e]
        return out + gap[8] + [("down0", u, E0 - 1)]
    out = [("up1", u, s) for s in range(NT)] + gap[0]
    out += [("turn1", u, 0), ("turn1", u, 1)] + gap[1]
    out += [("up1", u, NT), ("up1", u, NT + 1), ("down1", u, 0)] + gap[2]
    out += [("turn1", u, 2), ("turn1", u, 3), ("up1", u, NT + 2), ("up1", u, NT + 3)] + gap[3]
    out += [("down1", u, 1)] + gap[4] + [("turn1", u, 4), ("turn1", u, 5)] + gap[5]
    out += [("turn1", u, 6), ("turn1", u, 7), ("down1", u, 2)] + gap[6] + [("down1", u, 3)]
    return out + gap[7] + gap[8] + [("finish", u, 0)]


def order_of_turn():
    out = [step for piece in head_of(UNITS[0]) for step in piece]
    for u in UNITS:
        out += body_of(u, head_of(UNITS[u.at + 1] if u.at + 1 < len(UNITS) else None))
    return out


ORDER = order_of_turn()
SHORT = ("mask_T", "xhat_T", "row_valid", "query", "values", "gate", "peak_T", "attn_out")


POOL_LAST = {"ln": "ln_rstd", "ln2": "ln2_rstd", "attn_bias": "bias_added", "keys": "keys_lo",
             "query": "query_ready", "up1": "hid_rstd", "finish": "out_bias"}


def rank(kinds, u, arg):
    kinds = (kinds,) if isinstance(kinds, str) else kinds
    n = 0
    for k, v, a in ORDER:
        n += k in kinds
        if k in kinds and v is u and a == arg:
            return n
    raise KeyError((kinds, u.at, arg))


def per_turn(kinds):
    kinds = (kinds,) if isinstance(kinds, str) else kinds
    return sum(k in kinds for k, _, _ in ORDER)


def build(nc: bass.Bass, a, out):
    ctx = ExitStack()
    with ctx:
        def sb(name, shape, dt=F32):
            return ctx.enter_context(nc.sbuf_tensor(name, shape, dt))

        def sem(name):
            return ctx.enter_context(nc.semaphore(name))

        rows_sb = sb("rows_sb", [29, P])
        NB_LNG, NB_LNB, NB_RNG, NB_RNB, NB_B, NB_HB, NB_RW = 0, 8, 16, 17, 18, 21, 25
        cols = sb("cols", [P, 29])
        flat_sb = sb("flat_sb", [1, 4, P])
        bhv_sb = sb("bhv_sb", [1, P])
        spread = sb("spread", [P, 4, P])
        w_T = sb("w_T", [P, 3, P])
        w_head = sb("w_head", [P, 3, P])
        ctx_nat = sb("ctx_nat", [KEYS, B, P])
        ctx_hi = sb("ctx_hi", [P, B * KEYS], F32R)
        ctx_lo = sb("ctx_lo", [P, B * KEYS], F32R)
        ctx_T = sb("ctx_T", [P, B * KEYS])
        k_full = sb("k_full", [P, B * KEYS])
        router_in = sb("router_in", [P, 2, E1])
        gate_nat = sb("gate_nat", [P, E0])

        ones = sb("ones", [P, P])
        ones_r = sb("ones_r", [KEYS, P], F32R)
        ident = sb("ident", [P, P])
        ident_b = sb("ident_b", [P, P], BF16)
        pick = sb("pick", [CK, 2, HKP], F32R)
        own_v = sb("own_v", [P, NCH, HALF * HD])
        own_k2 = sb("own_k2", [P, 2, HALF])
        own_k = sb("own_k", [P, HALF])
        iota8 = sb("iota8", [P, E0])
        neg_half = sb("neg_half", [P, NT])
        eps_t = sb("eps_t", [P, 1])
        wqk_hi = sb("wqk_hi", [P, 2, 2, 2, P], F32R)
        wqk_lo = sb("wqk_lo", [P, 2, 2, 2, P], F32R)
        qk_bias = sb("qk_bias", [P, 2, 2, 2])
        wv = sb("wv", [P, 2, P])
        v_bias = sb("v_bias", [1, P])
        wo = sb("wo", [P, 2, P])
        k_hi = sb("k_hi", [P, 2, 2, B, KEYS], F32R)
        k_lo = sb("k_lo", [P, 2, 2, B, KEYS], F32R)
        v_all = sb("v_all", [KEYS, 2, B, P])
        gate0_hi = sb("gate0_hi", [P, E0], F32R)
        gate0_lo = sb("gate0_lo", [P, E0], F32R)
        gate1 = sb("gate1", [P, E1])
        gate1_hi = sb("gate1_hi", [P, E1], F32R)
        gate1_lo = sb("gate1_lo", [P, E1], F32R)
        gate1_sum = sb("gate1_sum", [P, 2, E1])
        up0_hi = sb("up0_hi", [P, E0 * FF0], F32R)
        up0_lo = sb("up0_lo", [P, E0 * FF0], F32R)
        dn0 = sb("dn0", [P, E0, 2, P])
        up1_hi = sb("up1_hi", [P, E1 * FF1], F32R)
        up1_lo = sb("up1_lo", [P, E1 * FF1], F32R)
        dn1 = sb("dn1", [P, E1, 2, P])

        x_in = sb("x_in", [P, 2, NT, P])
        mask_in = [sb("mask0_in", [P, 2, NT, KEYS], I32), sb("mask1_in", [P, 2, NT, KEYS], U8)]
        x = sb("x", [P, 2, NT, P])
        x_bias = sb("x_bias", [P, 2, NT, P])
        bn = sb("bn", [P, NT, 6])
        stat = sb("stat", [P, NT, 2])
        var_e = sb("var_e", [P, NT])
        rstd = sb("rstd", [P, NT])
        bn2 = sb("bn2", [P, NT, 6])
        stat2 = sb("stat2", [P, NT, 2])
        var_e2 = sb("var_e2", [P, NT])
        rstd2 = sb("rstd2", [P, NT])
        xhat = sb("xhat", [P, NT, P])
        xT_hi = sb("xT_hi", [P, 2, S], F32R)
        xT_lo = sb("xT_lo", [P, 2, S], F32R)
        mask_q = sb("mask_q", [P, 2, NT, KEYS], BF16)
        shift = sb("shift", [CK, 2, S], F32R)
        valid = sb("valid", [P, S])
        q_full = sb("q_full", [P, 2, S])
        q_st = sb("q_st", [P, 2, 2, S], F32R)
        k_st = sb("k_st", [P, 2, 2, 2, HKP], F32R)
        v_now = sb("v_now", [KEYS, P])
        v_st = sb("v_st", [P, 2, 2, NCH, P])
        neg_max = sb("neg_max", [P, NT, H])
        prob = sb("prob", [P, 3, S])
        inv = sb("inv", [HALF * HD, 2, S])
        heads_T = sb("heads_T", [P, S])
        logit = sb("logit", [P, NT, 8])
        top = sb("top", [P, NT, 8])
        top_at = sb("top_at", [P, NT, 8], U32)
        top_f = sb("top_f", [P, NT, 2])
        lead = sb("lead", [P, NT, 8])
        lead_e = sb("lead_e", [P, NT, 8])
        gsum = sb("gsum", [P, NT])
        gden = sb("gden", [P, NT])
        ginv = sb("ginv", [P, NT])
        gw = sb("gw", [P, NT, 2])
        pair = sb("pair", [P, NT, 2, 8])
        comb = sb("comb", [P, 2, NT, 8])
        hid_T = sb("hid_T", [P, 2, 2, S])
        hbn = sb("hbn", [P, NT, 2, 6])
        hstat = sb("hstat", [P, NT, 2, 2])
        hvar = sb("hvar", [P, NT, 2])
        hrstd = sb("hrstd", [P, NT, 2])
        hshift = sb("hshift", [P, NT, 2])
        hnorm = sb("hnorm", [P, 2, NT, 2 * FF1])
        acc = sb("acc", [P, NT, P])
        fold = sb("fold", [P, NT, E1])
        y = sb("y", [P, B, NT, P])

        w_nat = prob[:].rearrange("p a c -> p (a c)")[:, 0:7 * P].rearrange("p (i c) -> p i c", i=7)
        pick_f = hid_T[0:CK].rearrange("p a b c -> p (a b c)")[:, 0:2 * HKP].rearrange("p (i c) -> p i c", i=2)
        up0_f = hnorm[:, 0].rearrange("p a c -> p (a c)")
        up1_f = hnorm[:, 1].rearrange("p a c -> p (a c)")[:, 0:E1 * FF1]

        ps = ctx.enter_context(nc.psum_tensor("ps", [P, 8, 512], F32))
        SH = 7
        PV = (6, 0)

        ld_rows, ld_flat, ld_w, ld_head, ld_ctx = (sem(n) for n in ("ld_rows", "ld_flat", "ld_w", "ld_head", "ld_ctx"))
        ld_gate, ld_up0, ld_dn, ld_up1 = (sem(n) for n in ("ld_gate", "ld_up0", "ld_dn", "ld_up1"))
        const_made, const_cast = sem("const_made"), sem("const_cast")
        setup_full, setup_free, setup_dve = sem("setup_full"), sem("setup_free"), sem("setup_dve")
        up_hi_made = sem("up_hi_made")
        turn_done = sem("turn_done")

        counts = {}

        sems = {}
        for name, kinds in {
            "mask_ready": ("mask",), "ln_bn": ("ln",), "ln_stats": ("ln",), "ln_var": ("ln",), "ln_rstd": ("ln",),
            "xhat_ready": ("ln",), "ln2_bn": ("ln2",), "ln2_stats": ("ln2",), "ln2_var": ("ln2",),
            "ln2_rstd": ("ln2",), "bias_added": ("attn_bias",), "values_ready": ("values_in",),
            "keys_hi": ("keys",), "keys_lo": ("keys",), "short_full": SHORT, "short_free": SHORT,
            "xT_hi_ready": ("xhat_T",), "query_hi": ("query",), "query_ready": ("query",),
            "peak_full": ("peak",), "peak_done": ("peak",), "scores_full": ("scores",), "exp_done": ("scores",),
            "weigh_done": ("weigh",), "inv_ready": ("norm",), "norm_done": ("norm",),
            "fold_scaled": ("fold",), "fold_mean": ("fold",), "fold_added": ("fold",), "fold_done": ("fold",),
            "gate_den_eps": ("fold",), "top_ready": ("route",), "lead_ready": ("route",), "lead_exp": ("route",),
            "gate_den": ("route",), "gate_inv": ("route",), "pair_is": ("route",), "pair_ready": ("route",),
            "comb_ready": ("route",),
            "up0_full": ("up0",), "silu_done": ("up0",), "down0_full": ("down0",), "down0_done": ("down0",),
            "up1_full": ("up1",), "hid_bn": ("up1",), "hid_stats": ("up1",), "hid_var": ("up1",), "hid_rstd": ("up1",),
            "hid_mr": ("up1",), "hid_shift": ("up1",), "hid_norm": ("up1",), "turn1_full": ("turn1",), "relu_done": ("turn1",),
            "down1_full": ("down1",), "down1_done": ("down1",),
            "out_bn": ("finish",), "out_stats": ("finish",), "out_var": ("finish",), "out_rstd": ("finish",), "out_bias": ("finish",),
            "out_hat": ("finish",), "out_gain": ("finish",), "out_ready": ("finish",),
        }.items():
            sems[name] = sem(name)
            counts[name] = kinds
        go = {name: sem(f"go_{name}") for name in ("act", "dve", "pe", "sp")}
        turn_loaded = sem("turn_loaded")
        stored = sem("stored")

        def wait(eng, name, u, arg, back=0):
            kinds = counts[name]
            own = [k for k, v, g in ORDER if v is u and g == arg and k in kinds]
            n = rank_any(kinds, u, arg, own[0]) - back
            if n >= 1:
                eng.wait_ge(sems[name], n)

        def rank_any(kinds, u, arg, own):
            n = 0
            for k, v, g in ORDER:
                n += k in kinds
                if k == own and v is u and g == arg:
                    return n
            raise KeyError((kinds, u.at, arg))

        def short(name, kind, eng, u, arg, back=0):
            n = rank_any(SHORT, u, arg, kind) - back
            if n >= 1:
                eng.wait_ge(sems[name], n)

        def sem_number(s):
            return s.num

        def start_turn(eng, name):
            eng.wait_ge(go[name], 1)
            eng.sem_clear(go[name])

        def x_of(u):
            return x_in if u.kind == "attn" and u.layer == 0 else x

        def spread_over(row, n):
            return row.unsqueeze(1).broadcast_to([row.shape[0], n, row.shape[1]])

        block = ctx.enter_context(nc.Block())

        @block.sync
        def _(sp):
            def load_batch(turn, par, layer):
                b = 2 * turn + par
                if layer == 0:
                    if turn:
                        wait(sp, "xhat_ready", UNITS[par], 0)
                        wait(sp, "bias_added", UNITS[par], 0)
                    sp.dma_start(x_in[:, par], a["x"][b].rearrange("(t p) d -> p t d", p=P)).then_inc(turn_loaded, 16)
                if turn:
                    wait(sp, "mask_ready", UNITS[4 * layer + par], 0)
                m = a["mask_Bx1xSxS2_ik1"][b, 0] if layer == 0 else a["mask_BxSxS2_bk1"][b]
                sp.dma_start(mask_in[layer][:, par], m.rearrange("(t p) k -> p t k", p=P)).then_inc(turn_loaded, 16)

            sp.dma_start(ctx_nat[:], a["ctx_1024"].rearrange("b k d -> k b d")).then_inc(ld_ctx, 16)
            for n, name in enumerate(["L0_xattn_Wq", "L0_xattn_Wk", "L0_xattn_Wv", "L0_xattn_Wo",
                                      "L1_xattn_Wq", "L1_xattn_Wk", "L1_xattn_Wv"]):
                sp.dma_start(w_nat[:, n], a[name]).then_inc(ld_w, 16)
            load_batch(0, 0, 0)
            load_batch(0, 1, 0)
            sp.dma_start(wo[:, 1], a["L1_xattn_Wo"]).then_inc(ld_w, 16)
            load_batch(0, 0, 1)
            load_batch(0, 1, 1)
            sp.dma_start(up0_f.rearrange("p (e f) -> p e f", e=E0), a["L0_ffn_w1"].rearrange("e d f -> d e f")).then_inc(ld_up0, 16)
            sp.dma_start(dn0[:], a["L0_ffn_w2"].rearrange("e (c p) d -> p e c d", p=P)).then_inc(ld_dn, 16)
            sp.dma_start(up1_f.rearrange("p (e f) -> p e f", e=E1), a["L1_ffn_w1"].rearrange("e d f -> d e f")).then_inc(ld_up1, 16)
            sp.dma_start(dn1[:], a["L1_ffn_w2"].rearrange("e (c p) d -> p e c d", p=P)).then_inc(ld_dn, 16)
            sp.wait_ge(turn_loaded, 16 * 6)
            sp.sem_inc(turn_done, 1)
            for turn in range(TURNS):
                start_turn(sp, "sp")
                if turn + 1 < TURNS:
                    for layer in range(2):
                        for par in range(2):
                            load_batch(turn + 1, par, layer)
                for par in range(2):
                    wait(sp, "out_ready", UNITS[6 + par], 0)
                    sp.dma_start(out[2 * turn + par].rearrange("(t p) d -> p t d", p=P), y[:, 2 * turn + par])\
                      .then_inc(stored, 16)
                if turn + 1 < TURNS:
                    sp.wait_ge(turn_loaded, 16 * 6 * (turn + 2))
                    sp.sem_inc(turn_done, 1)
            sp.wait_ge(stored, 16 * B)

        @block.gpsimd
        def _(pool):
            g = nc.gpsimd
            g.memset(ones[:], 1.0).then_inc(const_made, 1)
            g.memset(ident[:], 0.0).then_inc(const_made, 1)
            g.memset(pick_f, 0.0).then_inc(const_made, 1)
            g.memset(own_v[:], 1.0).then_inc(const_made, 1)
            g.memset(own_k2[:], 1.0).then_inc(const_made, 1)
            g.memset(neg_half[:], -0.5).then_inc(const_made, 1)
            g.iota(iota8[:], [[1, E0]], base=0, channel_multiplier=0,
                   allow_small_or_imprecise_dtypes=True).then_inc(const_made, 1)
            pool.wait_ge(const_made, 7)
            g.affine_select(out=ident[:], in_=ident[:], compare_op=ALU.not_equal, fill=1.0, base=0,
                            pattern=[[-1, P]], channel_multiplier=1).then_inc(const_made, 1)
            for half in range(2):
                keys_of = pick_f[:, half, 0:HK].rearrange("p (h k) -> p h k", h=HALF)
                g.affine_select(out=keys_of, in_=keys_of, compare_op=ALU.not_equal, fill=1.0, base=0,
                                pattern=[[0, HALF], [-1, KEYS]], channel_multiplier=1).then_inc(const_made, 1)
                pool.wait_ge(const_made, 9 + 2 * half)
                g.affine_select(out=keys_of, in_=keys_of, compare_op=ALU.not_equal, fill=1.0,
                                base=-(CROW + HALF * half), pattern=[[-1, HALF], [0, KEYS]],
                                channel_multiplier=1).then_inc(const_made, 1)
            v_view = own_v[:].rearrange("p c (h j) -> p c h j", h=HALF)
            pool.wait_ge(const_made, 12)
            g.affine_select(out=v_view, in_=v_view, compare_op=ALU.is_ge, fill=0.0, base=0,
                            pattern=[[P, NCH], [-KEYS, HALF], [0, HD]], channel_multiplier=1).then_inc(const_made, 1)
            pool.wait_ge(const_made, 13)
            g.affine_select(out=v_view, in_=v_view, compare_op=ALU.is_ge, fill=0.0, base=KEYS - 1,
                            pattern=[[-P, NCH], [KEYS, HALF], [0, HD]], channel_multiplier=-1).then_inc(const_made, 1)
            g.affine_select(out=own_k2[:], in_=own_k2[:], compare_op=ALU.is_ge, fill=0.0, base=0,
                            pattern=[[-HALF * HD, 2], [-HD, HALF]], channel_multiplier=1).then_inc(const_made, 1)
            pool.wait_ge(const_made, 15)
            g.affine_select(out=own_k2[:], in_=own_k2[:], compare_op=ALU.is_ge, fill=0.0, base=HD - 1,
                            pattern=[[HALF * HD, 2], [HD, HALF]], channel_multiplier=-1).then_inc(const_made, 1)
            g.memset(eps_t[:], EPS).then_inc(const_made, 1)
            g.memset(k_st[:].bitcast(F32), 0.0).then_inc(const_made, 1)
            g.memset(shift[:].bitcast(F32), 0.0).then_inc(const_made, 1)
            g.memset(lead[:], 0.0).then_inc(const_made, 1)
            pool.wait_ge(const_made, 20)

            with pool.Fori(0, TURNS) as turn:
                pool.wait_ge(turn_done, 4)
                pool.sem_clear(range(sem_number(sems["mask_ready"]), sem_number(sems["out_ready"]) + 1))
                pool.sem_clear(turn_done)
                for name in ("act", "dve", "pe", "sp"):
                    pool.drain().then_inc(go[name], 1)
                before = None
                for kind, u, arg in ORDER:
                    last = POOL_LAST.get(kind)
                    if last is None:
                        continue
                    if before:
                        wait(pool, *before)
                    before = (last, u, arg)
                    if kind in ("ln", "ln2"):
                        two = kind == "ln2"
                        st, ve, rs = (stat2, var_e2, rstd2) if two else (stat, var_e, rstd)
                        pre = "ln2" if two else "ln"
                        wait(pool, pre + "_stats", u, 0)
                        g.tensor_scalar(ve[:], st[:, :, 1], EPS, None, ALU.add).then_inc(sems[pre + "_var"], 1)
                        wait(pool, pre + "_var", u, 0)
                        g.tensor_tensor(rs[:], ve[:], neg_half[:], ALU.pow).then_inc(sems[pre + "_rstd"], 1)
                    elif kind == "attn_bias":
                        if u.layer == 1:
                            wait(pool, "xhat_ready", u, 0)
                        g.tensor_tensor(x_bias[:, u.par], x_of(u)[:, u.par], spread_over(spread[:, u.layer], NT),
                                        ALU.add).then_inc(sems["bias_added"], 1)
                    elif kind == "keys":
                        src = k_lo[:, u.layer, arg, bass.ds(turn * 2 + u.par, 1), :].bitcast(F32)
                        g.tensor_tensor(
                            k_st[:, u.par, arg, 1, 0:HK].rearrange("p (h k) -> p h k", h=HALF),
                            src.broadcast_to([P, HALF, KEYS]),
                            own_k[:].unsqueeze(2).broadcast_to([P, HALF, KEYS]), ALU.mult).then_inc(sems["keys_lo"], 1)
                    elif kind == "query":
                        wait(pool, "query_hi", u, arg)
                        lo = slice(64, P)
                        g.tensor_tensor(q_st[lo, u.par, arg], q_full[lo, arg], q_st[lo, u.par, arg].bitcast(F32),
                                        ALU.subtract).then_inc(sems["query_ready"], 1)
                    elif kind == "up1":
                        t = arg % NT
                        wait(pool, "hid_stats", u, arg)
                        g.tensor_scalar(hvar[:, t], hstat[:, t, :, 1], EPS, None, ALU.add).then_inc(sems["hid_var"], 1)
                        wait(pool, "hid_var", u, arg)
                        g.tensor_tensor(hrstd[:, t], hvar[:, t], neg_half[:, 0:2], ALU.pow).then_inc(sems["hid_rstd"], 1)
                    elif kind == "finish":
                        wait(pool, "out_stats", u, 0)
                        g.tensor_scalar(var_e[:], stat[:, :, 1], EPS, None, ALU.add).then_inc(sems["out_var"], 1)
                        wait(pool, "out_var", u, 0)
                        g.tensor_tensor(rstd[:], var_e[:], neg_half[:], ALU.pow).then_inc(sems["out_rstd"], 1)
                        wait(pool, "out_rstd", u, 0)
                        g.tensor_tensor(x_bias[:, u.par], x[:, u.par], spread_over(spread[:, 3], NT),
                                        ALU.add).then_inc(sems["out_bias"], 1)

        @block.scalar
        def _(act):
            s = nc.scalar
            for n, (row, k) in enumerate([("L1_ffn_ln_g", NB_LNG), ("L1_ffn_ln_b", NB_LNB)]):
                act.dma_start(rows_sb[k:k + 8, :], a[row].rearrange("e (c p) -> (e c) p", p=P)).then_inc(ld_rows, 16)
            for n, name in enumerate(["L1_ffn_rn_g", "L1_ffn_rn_b", "L1_xattn_bq", "L1_xattn_bk", "L1_xattn_bv"]):
                act.dma_start(rows_sb[NB_RNG + n:NB_RNG + n + 1, :], a[name].unsqueeze(0)).then_inc(ld_rows, 16)
            for n, name in enumerate(["L1_xattn_bhq", "L1_xattn_bhk"]):
                for twice in range(2):
                    act.dma_start(rows_sb[NB_HB + 2 * n:NB_HB + 2 * n + 2, 64 * twice:64 * twice + 64],
                                  a[name].rearrange("(g h) d -> g (h d)", g=2)).then_inc(ld_rows, 16)
            act.dma_start(rows_sb[NB_RW:NB_RW + E1, :], a["L1_ffn_router_w"]).then_inc(ld_rows, 16)
            for n, name in enumerate(["L0_xattn_bo", "L1_xattn_bo", "L1_ffn_on_g", "L1_ffn_on_b"]):
                act.dma_start(flat_sb[:, n], a[name].unsqueeze(0)).then_inc(ld_flat, 16)
            act.dma_start(bhv_sb[:], a["L1_xattn_bhv"].rearrange("h d -> (h d)").unsqueeze(0)).then_inc(ld_flat, 16)
            for n, name in enumerate(["L1_xattn_Whq", "L1_xattn_Whk", "L1_xattn_Whv"]):
                act.dma_start(w_head[:, n].rearrange("p (h d) -> p h d", h=H),
                              a[name].rearrange("h e d -> e h d")).then_inc(ld_head, 16)
            act.dma_start(gate_nat[:], a["L0_ffn_gate_w"]).then_inc(ld_gate, 16)
            act.wait_ge(ld_up0, 16)
            s.activation(up0_hi[:], up0_f, ACT.Copy).then_inc(up_hi_made, 1)
            act.wait_ge(ld_up1, 16)
            s.activation(up1_hi[:], up1_f, ACT.Copy).then_inc(up_hi_made, 1)
            act.wait_ge(up_hi_made, 2)
            act.wait_ge(ld_dn, 32)
            act.drain().then_inc(turn_done, 1)

            with act.Fori(0, TURNS) as turn:
                start_turn(act, "act")
                for kind, u, arg in ORDER:
                    if kind == "values_in":
                        if u.at:
                            prev = [v for v in UNITS[:u.at] if v.kind == "attn"]
                            if prev:
                                short("short_full", "values", act, prev[-1], 1)
                        s.activation(v_now[:], v_all[:, u.layer, bass.ds(turn * 2 + u.par, 1), :]
                                     .rearrange("p o d -> p (o d)"), ACT.Copy).then_inc(sems["values_ready"], 1)
                    elif kind == "mask_T":
                        short("short_full", kind, act, u, arg)
                        s.activation(shift[0:KEYS, u.par], ps[0:KEYS, SH, 0:S // 2].bitcast(BF16),
                                     ACT.Copy).then_inc(sems["short_free"], 1)
                    elif kind == "xhat_T":
                        short("short_full", kind, act, u, arg)
                        s.activation(xT_hi[:, u.par], ps[:, SH, :], ACT.Copy).then_inc(sems["xT_hi_ready"], 1)
                    elif kind == "query":
                        short("short_free", kind, act, u, arg)
                        s.activation(q_st[:, u.par, arg], q_full[:, arg], ACT.Copy).then_inc(sems["query_hi"], 1)
                    elif kind == "peak_T":
                        short("short_full", kind, act, u, arg)
                        s.activation(shift[CROW:CK, u.par], ps[0:H, SH, :], ACT.Copy).then_inc(sems["short_free"], 1)
                    elif kind == "scores":
                        wait(act, "scores_full", u, arg)
                        if arg >= 3:
                            wait(act, "weigh_done", u, arg - 3)
                        s.activation(prob[:, arg % 3], ps[:, 4 + arg % 2, :], ACT.Exp,
                                     scale=SCALE[u.layer]).then_inc(sems["exp_done"], 1)
                    elif kind == "route":
                        wait(act, "lead_ready", u, 0)
                        s.activation(lead_e[:], lead[:], ACT.Exp).then_inc(sems["lead_exp"], 1)
                    elif kind == "up0":
                        e, half = divmod(arg, 2)
                        wait(act, "up0_full", u, arg)
                        if e >= 2:
                            wait(act, "down0_full", u, e - 2)
                        s.activation(hid_T[:, e % 2, half], ps[:, arg % 4, :], ACT.Silu).then_inc(sems["silu_done"], 1)
                    elif kind == "up1":
                        g2, t = divmod(arg, NT)
                        wait(act, "hid_shift", u, arg)
                        for e in range(2):
                            last = s.activation(hnorm[:, g2, t, e * FF1:(e + 1) * FF1],
                                                ps[:, t, e * FF1:(e + 1) * FF1], ACT.Identity,
                                                bias=hshift[:, t, e:e + 1], scale=hrstd[:, t, e:e + 1])
                        last.then_inc(sems["hid_norm"], 1)
                    elif kind == "turn1":
                        e, half = divmod(arg, 2)
                        wait(act, "turn1_full", u, arg)
                        if e >= 2:
                            wait(act, "down1_full", u, e - 2)
                        s.activation(hid_T[:, e % 2, half], ps[:, 4 + arg % 2, :], ACT.Relu,
                                     bias=cols[:, NB_LNB + arg:NB_LNB + arg + 1],
                                     scale=cols[:, NB_LNG + arg:NB_LNG + arg + 1]).then_inc(sems["relu_done"], 1)
                act.drain().then_inc(turn_done, 1)

        def fold_router(dve, v, turn, u):
            def then(ins, name):
                ins.then_inc(sems[name], 1)
                wait(dve, name, u, 0)

            def over(z):
                return z.unsqueeze(2).broadcast_to([P, NT, E1])

            lg = logit[:, :, 0:E1]
            short("short_free", "gate", dve, u, 0)
            wait(dve, "ln2_rstd", u, 0)
            v.memset(logit[:, :, E1:8], LOWEST)
            v.scalar_tensor_tensor(gsum[:], stat2[:, :, 0], -1.0, rstd2[:], ALU.mult, ALU.mult)
            then(v.tensor_tensor(lg, lg, over(rstd2[:]), ALU.mult), "fold_scaled")
            then(v.tensor_tensor(fold[:], over(gsum[:]), spread_over(gate1_sum[:, 0], NT), ALU.mult), "fold_mean")
            then(v.tensor_tensor(lg, lg, fold[:], ALU.add), "fold_added")
            v.tensor_tensor(lg, lg, spread_over(gate1_sum[:, 1], NT), ALU.add).then_inc(sems["fold_done"], 1)

        def route(dve, v, turn, u):
            def then(ins, name):
                ins.then_inc(sems[name], 1)
                wait(dve, name, u, 0)

            if u.kind == "moe0":
                short("short_free", "gate", dve, u, 0)
            else:
                wait(dve, "fold_done", u, 0)
            for t in range(NT):
                ins = v.max(top[:, t], logit[:, t])
            then(ins, "top_ready")
            for t in range(NT):
                v.max_index(top_at[:, t], top[:, t], logit[:, t])
            v.tensor_tensor(lead[:], top[:], top[:, :, 0:1].broadcast_to([P, NT, 8]),
                            ALU.subtract).then_inc(sems["lead_ready"], 1)
            wait(dve, "lead_exp", u, 0)
            if u.kind == "moe1":
                v.tensor_reduce(gsum[:], lead_e[:, :, 0:E1], AX_X, ALU.add)
            v.tensor_copy(top_f[:], top_at[:, :, 0:2])
            then(v.tensor_tensor(gden[:], lead_e[:, :, 0], lead_e[:, :, 1], ALU.add), "gate_den")
            if u.kind == "moe1":
                then(v.scalar_tensor_tensor(gden[:], gsum[:], EPS_GATE, gden[:], ALU.mult, ALU.add), "gate_den_eps")
            then(v.reciprocal(ginv[:], gden[:]), "gate_inv")
            v.tensor_tensor(gw[:], lead_e[:, :, 0:2], ginv[:].unsqueeze(2).broadcast_to([P, NT, 2]), ALU.mult)
            then(v.tensor_tensor(pair[:].rearrange("p t i e -> p (t i) e"), spread_over(iota8[:], 2 * NT),
                                 top_f[:].rearrange("p t i -> p (t i)").unsqueeze(2).broadcast_to([P, 2 * NT, 8]),
                                 ALU.is_equal), "pair_is")
            then(v.tensor_tensor(pair[:], pair[:], gw[:].unsqueeze(3).broadcast_to([P, NT, 2, 8]), ALU.mult),
                 "pair_ready")
            v.tensor_tensor(comb[:, u.par], pair[:, :, 0], pair[:, :, 1], ALU.add).then_inc(sems["comb_ready"], 1)

        @block.vector
        def _(dve):
            v = nc.vector
            n_dve = [0]

            def link(ins):
                n_dve[0] += 1
                ins.then_inc(setup_dve, 1)
                dve.wait_ge(setup_dve, n_dve[0])

            def ready(n):
                dve.wait_ge(setup_full, n)

            def freed(ins):
                ins.then_inc(setup_free, 1)

            dve.wait_ge(const_made, 20)
            v.tensor_copy(ident_b[:], ident[:])
            v.tensor_copy(ones_r[:], ones[0:KEYS, :])
            v.tensor_copy(pick[:], pick_f)
            v.tensor_tensor(own_k[:], own_k2[:, 0], own_k2[:, 1], ALU.add)
            for par in range(2):
                for half in range(2):
                    v.tensor_copy(v_st[:, par, half, :, HALF * HD:P], own_v[:])
            v.memset(qk_bias[:], 0.0).then_inc(const_cast, 1)
            dve.wait_ge(const_cast, 1)
            dve.wait_ge(ld_gate, 16)
            link(v.tensor_copy(gate0_hi[:], gate_nat[:]))
            link(v.tensor_tensor(gate0_lo[:], gate_nat[:], gate0_hi[:].bitcast(F32), ALU.subtract))

            def both_halves(bank, i):
                src = ps[:, bank, i * P:(i + 1) * P].rearrange("p (h c) -> p h c", h=2)
                return src.unsqueeze(2).broadcast_to([P, 2, 2, 64])

            def split_qk(layer, bank):
                for i in range(2):
                    dst_hi = wqk_hi[:, layer, i].rearrange("p h (t c) -> p h t c", t=2)
                    dst_lo = wqk_lo[:, layer, i].rearrange("p h (t c) -> p h t c", t=2)
                    link(v.tensor_copy(dst_hi, both_halves(bank, i)))
                    link(v.tensor_tensor(dst_lo, both_halves(bank, i), dst_hi.bitcast(F32), ALU.subtract))

            ready(1)
            freed(v.tensor_copy(cols[:], ps[:, 0, 0:29]))
            dve.wait_ge(setup_free, 1)
            v.tensor_scalar(gate1[:], cols[:, NB_RW:NB_RW + E1], cols[:, NB_RNG:NB_RNG + 1], None, ALU.mult)
            link(v.tensor_scalar(router_in[:, 1], cols[:, NB_RW:NB_RW + E1], cols[:, NB_RNB:NB_RNB + 1], None, ALU.mult))
            link(v.tensor_copy(router_in[:, 0], gate1[:]))
            link(v.tensor_copy(gate1_hi[:], gate1[:]))
            link(v.tensor_tensor(gate1_lo[:], gate1[:], gate1_hi[:].bitcast(F32), ALU.subtract))
            ready(2)
            split_qk(0, 1)
            v.tensor_copy(wv[:, 0], ps[:, 1, 2 * P:3 * P])
            freed(v.tensor_copy(wo[:, 0], ps[:, 1, 3 * P:4 * P]))
            ready(3)
            v.tensor_copy(ctx_T[:], ps[:, 2, 0:B * KEYS])
            link(v.tensor_copy(ctx_hi[:], ps[:, 2, 0:B * KEYS]))
            freed(v.tensor_tensor(ctx_lo[:], ps[:, 2, 0:B * KEYS], ctx_hi[:].bitcast(F32), ALU.subtract))
            ready(4)
            freed(v.tensor_copy(w_T[:], ps[:, 3, 0:3 * P].rearrange("p (i c) -> p i c", i=3)))
            ready(5)
            freed(v.tensor_copy(spread[:], ps[:, 4, :].rearrange("p (i c) -> p i c", i=4)))
            ready(6)
            split_qk(1, 5)
            freed(v.tensor_copy(wv[:, 1], ps[:, 5, 2 * P:3 * P]))
            ready(7)
            v.tensor_tensor(qk_bias[:, 1], ps[:, 6, 0:4].rearrange("p (i h) -> p i h", i=2),
                            cols[:, NB_HB:NB_HB + 4].rearrange("p (i h) -> p i h", i=2), ALU.add)
            v.tensor_tensor(v_bias[:], ps[0:1, 6, P:2 * P], bhv_sb[:], ALU.add)
            freed(v.tensor_copy(gate1_sum[:], ps[:, 6, 2 * P:2 * P + 2 * E1].rearrange("p (i e) -> p i e", i=2)))
            dve.wait_ge(setup_free, 7)
            n = 8
            for layer in range(2):
                for half in range(2):
                    ready(n)
                    link(v.tensor_scalar(k_full[:], ps[:, (n - 1) % 8, 0:B * KEYS], qk_bias[:, layer, 1, half:half + 1],
                                         None, ALU.add))
                    hi = k_hi[:, layer, half].rearrange("p b k -> p (b k)")
                    link(v.tensor_copy(hi, k_full[:]))
                    ins = v.tensor_tensor(k_lo[:, layer, half].rearrange("p b k -> p (b k)"), k_full[:],
                                          hi.bitcast(F32), ALU.subtract)
                    freed(ins)
                    dve.wait_ge(setup_free, n)
                    n += 1
                ready(n)
                freed(v.tensor_copy(v_all[:, layer], ps[0:KEYS, (n - 1) % 8, :].rearrange("p (b d) -> p b d", b=B)))
                n += 1
            dve.wait_ge(up_hi_made, 1)
            v.tensor_tensor(up0_lo[:], up0_f, up0_hi[:].bitcast(F32), ALU.subtract)
            dve.wait_ge(up_hi_made, 2)
            v.tensor_tensor(up1_lo[:], up1_f, up1_hi[:].bitcast(F32), ALU.subtract)
            v.memset(logit[:], 0.0)
            dve.drain().then_inc(turn_done, 1)

            with dve.Fori(0, TURNS) as turn:
                start_turn(dve, "dve")
                for kind, u, arg in ORDER:
                    par = u.par
                    if kind == "mask":
                        op = ALU.is_equal if u.layer == 0 else ALU.not_equal
                        v.tensor_scalar(mask_q[:, par], mask_in[u.layer][:, par], 0.0, -BIG, op,
                                        ALU.mult).then_inc(sems["mask_ready"], 1)
                    elif kind == "ln":
                        src = x_of(u)
                        if src is x:
                            before = UNITS[u.at - 2]
                            if before.kind == "attn":
                                short("short_free", "attn_out", dve, before, 0)
                            else:
                                wait(dve, "down0_done", before, E0 - 1)
                        for t in range(NT):
                            ins = v.bn_stats(bn[:, t], src[:, par, t])
                        ins.then_inc(sems["ln_bn"], 1)
                        wait(dve, "ln_bn", u, 0)
                        for t in range(NT):
                            ins = v.bn_aggr(stat[:, t], bn[:, t])
                        ins.then_inc(sems["ln_stats"], 1)
                        wait(dve, "ln_rstd", u, 0)
                        if u.at:
                            short("short_full", "xhat_T", dve, UNITS[u.at - 1], 0)
                        for t in range(NT):
                            ins = v.tensor_scalar(xhat[:, t], src[:, par, t], stat[:, t, 0:1], rstd[:, t:t + 1],
                                                  ALU.subtract, ALU.mult)
                        ins.then_inc(sems["xhat_ready"], 1)
                    elif kind == "ln2":
                        wait(dve, "xhat_ready", u, 0)
                        for t in range(NT):
                            ins = v.bn_stats(bn2[:, t], xhat[:, t])
                        ins.then_inc(sems["ln2_bn"], 1)
                        wait(dve, "ln2_bn", u, 0)
                        for t in range(NT):
                            ins = v.bn_aggr(stat2[:, t], bn2[:, t])
                        ins.then_inc(sems["ln2_stats"], 1)
                    elif kind == "keys":
                        src = k_hi[:, u.layer, arg, bass.ds(turn * 2 + par, 1), :].bitcast(F32)
                        v.tensor_tensor(
                            k_st[:, par, arg, 0, 0:HK].rearrange("p (h k) -> p h k", h=HALF),
                            src.broadcast_to([P, HALF, KEYS]),
                            own_k[:].unsqueeze(2).broadcast_to([P, HALF, KEYS]), ALU.mult).then_inc(sems["keys_hi"], 1)
                    elif kind == "xhat_T":
                        short("short_full", kind, dve, u, arg)
                        wait(dve, "xT_hi_ready", u, arg)
                        v.tensor_tensor(xT_lo[:, par], ps[:, SH, :], xT_hi[:, par].bitcast(F32),
                                        ALU.subtract).then_inc(sems["short_free"], 1)
                    elif kind == "row_valid":
                        short("short_full", kind, dve, u, arg)
                        v.tensor_scalar(valid[:], ps[:, SH, :], -BIG * (KEYS - 0.5), None,
                                        ALU.is_gt).then_inc(sems["short_free"], 1)
                    elif kind == "query":
                        short("short_full", kind, dve, u, arg)
                        if arg == 0:
                            short("short_free", "row_valid", dve, u, 0)
                        v.scalar_tensor_tensor(q_full[:, arg], ps[:, SH, :], qk_bias[:, u.layer, 0, arg:arg + 1],
                                               valid[:], ALU.add, ALU.mult).then_inc(sems["short_free"], 1)
                    elif kind == "values":
                        short("short_full", kind, dve, u, arg)
                        v.tensor_tensor(v_st[:, par, arg, :, 0:HALF * HD],
                                        ps[:, SH, 0:NCH * HALF * HD].rearrange("p (c j) -> p c j", c=NCH),
                                        own_v[:], ALU.mult).then_inc(sems["short_free"], 1)
                    elif kind == "peak":
                        t, half = divmod(arg, 2)
                        wait(dve, "peak_full", u, arg)
                        bank = 2 * (arg % 2)
                        v.tensor_reduce(neg_max[:, t, half * HALF:(half + 1) * HALF].rearrange("p (b h) -> p b h", b=2),
                                        ps[:, bank:bank + 2, 0:QW].rearrange("p b (h k) -> p b h k", h=QH),
                                        AX_X, ALU.max, negate=True).then_inc(sems["peak_done"], 1)
                    elif kind == "norm":
                        wait(dve, "weigh_done", u, NCH * (arg + 1) - 1)
                        v.reciprocal(inv[:, arg], ps[HALF * HD:P, PV[arg], :]).then_inc(sems["inv_ready"], 1)
                        wait(dve, "inv_ready", u, arg)
                        v.tensor_tensor(heads_T[64 * arg:64 * arg + 64], ps[0:HALF * HD, PV[arg], :], inv[:, arg],
                                        ALU.mult).then_inc(sems["norm_done"], 1)
                    elif kind == "attn_out":
                        short("short_full", kind, dve, u, arg)
                        wait(dve, "bias_added", u, 0)
                        v.tensor_tensor(x[:, par], ps[:, SH, :].rearrange("p (t d) -> p t d", t=NT), x_bias[:, par],
                                        ALU.add).then_inc(sems["short_free"], 1)
                    elif kind == "gate":
                        short("short_full", kind, dve, u, arg)
                        ne = E0 if u.kind == "moe0" else E1
                        v.tensor_copy(logit[:, :, 0:ne], ps[:, SH, 0:NT * ne].rearrange("p (t e) -> p t e", t=NT))\
                         .then_inc(sems["short_free"], 1)
                    elif kind == "fold":
                        fold_router(dve, v, turn, u)
                    elif kind == "route":
                        route(dve, v, turn, u)
                    elif kind == "down0":
                        wait(dve, "down0_full", u, arg)
                        if arg == 0:
                            wait(dve, "comb_ready", u, 0)
                        else:
                            wait(dve, "down0_done", u, arg - 1)
                        for t in range(NT):
                            ins = v.scalar_tensor_tensor(x[:, par, t], ps[:, 4 + arg % 2, t * P:(t + 1) * P],
                                                         comb[:, par, t, arg:arg + 1], x[:, par, t], ALU.mult, ALU.add)
                        ins.then_inc(sems["down0_done"], 1)
                    elif kind == "up1":
                        t = arg % NT
                        wait(dve, "up1_full", u, arg)
                        if arg >= NT:
                            wait(dve, "hid_norm", u, arg - NT)
                        for e in range(2):
                            ins = v.bn_stats(hbn[:, t, e], ps[:, t, e * FF1:(e + 1) * FF1])
                        ins.then_inc(sems["hid_bn"], 1)
                        wait(dve, "hid_bn", u, arg)
                        for e in range(2):
                            ins = v.bn_aggr(hstat[:, t, e], hbn[:, t, e])
                        ins.then_inc(sems["hid_stats"], 1)
                        wait(dve, "hid_rstd", u, arg)
                        v.scalar_tensor_tensor(hshift[:, t], hstat[:, t, :, 0], -1.0, hrstd[:, t], ALU.mult,
                                               ALU.mult).then_inc(sems["hid_shift"], 1)
                    elif kind == "down1":
                        wait(dve, "down1_full", u, arg)
                        if arg == 0:
                            wait(dve, "comb_ready", u, 0)
                        else:
                            wait(dve, "down1_done", u, arg - 1)
                        for t in range(NT):
                            src, w = ps[:, 6, t * P:(t + 1) * P], comb[:, par, t, arg:arg + 1]
                            if arg == 0:
                                ins = v.tensor_scalar(acc[:, t], src, w, None, ALU.mult)
                            else:
                                ins = v.scalar_tensor_tensor(acc[:, t], src, w, acc[:, t], ALU.mult, ALU.add)
                        ins.then_inc(sems["down1_done"], 1)
                    elif kind == "finish":
                        wait(dve, "down1_done", u, E1 - 1)
                        for t in range(NT):
                            ins = v.bn_stats(bn[:, t], acc[:, t])
                        ins.then_inc(sems["out_bn"], 1)
                        wait(dve, "out_bn", u, 0)
                        for t in range(NT):
                            ins = v.bn_aggr(stat[:, t], bn[:, t])
                        ins.then_inc(sems["out_stats"], 1)
                        wait(dve, "out_rstd", u, 0)
                        for t in range(NT):
                            ins = v.tensor_scalar(acc[:, t], acc[:, t], stat[:, t, 0:1], rstd[:, t:t + 1],
                                                  ALU.subtract, ALU.mult)
                        ins.then_inc(sems["out_hat"], 1)
                        wait(dve, "out_hat", u, 0)
                        v.tensor_tensor(acc[:], acc[:], spread_over(spread[:, 2], NT), ALU.mult).then_inc(sems["out_gain"], 1)
                        wait(dve, "out_gain", u, 0)
                        wait(dve, "out_bias", u, 0)


                        v.tensor_tensor(y[:, bass.ds(turn * 2 + par, 1)].rearrange("p o t d -> p (o t) d"), acc[:],
                                        x_bias[:, par], ALU.add).then_inc(sems["out_ready"], 1)
                dve.drain().then_inc(turn_done, 1)

        @block.tensor
        def _(pe):
            m = nc.tensor.matmul

            def turn_square(dst, src):
                k = src.shape[0]
                i = ident_b if src.dtype == BF16 else ident
                return nc.tensor.transpose(dst, src, i[0:k, 0:k])

            def split3(dst, w_hi, w_lo, x_hi, x_lo, stop=True):
                m(dst, w_lo, x_hi, start=True, stop=False)
                m(dst, w_hi, x_lo, start=False, stop=False)
                return m(dst, w_hi, x_hi, start=False, stop=stop)

            def full(ins):
                ins.then_inc(setup_full, 1)

            def free(n):
                pe.wait_ge(setup_free, n)

            pe.wait_ge(const_made, 20)
            pe.wait_ge(ld_rows, 16 * 12)
            full(turn_square(ps[:, 0, 0:29], rows_sb[:]))
            pe.wait_ge(ld_w, 16 * 8)
            for i in range(4):
                ins = turn_square(ps[:, 1, i * P:(i + 1) * P], w_nat[:, i])
            full(ins)
            pe.wait_ge(ld_ctx, 16)
            for b in range(B):
                ins = turn_square(ps[:, 2, b * KEYS:(b + 1) * KEYS], ctx_nat[:, b])
            full(ins)
            for i in range(3):
                ins = turn_square(ps[:, 3, i * P:(i + 1) * P], w_nat[:, 4 + i])
            full(ins)
            pe.wait_ge(ld_flat, 16 * 5)
            full(m(ps[:, 4, :], ones[0:1, :], flat_sb[:].rearrange("p i d -> p (i d)"), start=True, stop=True))
            pe.wait_ge(ld_head, 16 * 3)
            free(4)
            for i in range(3):
                ins = m(ps[:, 5, i * P:(i + 1) * P], w_T[:, i], w_head[:, i], start=True, stop=True)
            full(ins)
            for i in range(2):
                for half in range(2):
                    for twice in range(2):
                        m(ps[64 * twice:64 * twice + 64, 6, 2 * i + half:2 * i + half + 1],
                          w_head[:, i, 64 * half:64 * half + 64], cols[:, NB_B + i:NB_B + i + 1], start=True, stop=True)
            m(ps[0:1, 6, P:2 * P], cols[:, NB_B + 2:NB_B + 3], w_head[:, 2], start=True, stop=True)
            full(m(ps[:, 6, 2 * P:2 * P + 2 * E1], ones[:], router_in[:].rearrange("p i e -> p (i e)"),
                   start=True, stop=True))
            n = 8
            for layer in range(2):
                for half in range(2):
                    free(max(n - 8, 7 if layer else 4))
                    ins = split3(ps[:, (n - 1) % 8, 0:B * KEYS], wqk_hi[:, layer, 1, half], wqk_lo[:, layer, 1, half],
                                 ctx_hi[:], ctx_lo[:])
                    full(ins)
                    n += 1
                free(max(n - 8, 7 if layer else 4))
                for b in range(B):
                    ins = m(ps[0:KEYS, (n - 1) % 8, b * P:(b + 1) * P], ctx_T[:, b * KEYS:(b + 1) * KEYS], wv[:, layer],
                            start=True, stop=(layer == 0))
                    if layer:
                        ins = m(ps[0:KEYS, (n - 1) % 8, b * P:(b + 1) * P], ones[0:1, 0:KEYS], v_bias[:],
                                start=False, stop=True)
                full(ins)
                n += 1
            pe.wait_ge(const_cast, 1)
            free(n - 1)
            pe.wait_ge(ld_dn, 32)
            pe.drain().then_inc(turn_done, 1)

            with pe.Fori(0, TURNS) as turn:
                start_turn(pe, "pe")
                for kind, u, arg in ORDER:
                    par = u.par
                    if kind in SHORT:
                        short("short_free", kind, pe, u, arg, back=1)
                    if kind == "mask_T":
                        wait(pe, "mask_ready", u, 0)
                        for t in range(NT):
                            ins = turn_square(ps[0:KEYS, SH, t * P // 2:(t + 1) * P // 2].bitcast(BF16), mask_q[:, par, t])
                    elif kind == "xhat_T":
                        wait(pe, "xhat_ready", u, 0)
                        for t in range(NT):
                            ins = turn_square(ps[:, SH, t * P:(t + 1) * P], xhat[:, t])
                    elif kind == "row_valid":
                        ins = m(ps[:, SH, :], ones_r[:], shift[0:KEYS, par], start=True, stop=True)
                    elif kind == "query":
                        ins = split3(ps[:, SH, :], wqk_hi[:, u.layer, 0, arg], wqk_lo[:, u.layer, 0, arg],
                                     xT_hi[:, par], xT_lo[:, par])
                    elif kind == "values":
                        wait(pe, "values_ready", u, 0)
                        for c in range(NCH):
                            ins = m(ps[:, SH, c * 64:(c + 1) * 64], pick[0:KEYS, 0, c * P:(c + 1) * P].bitcast(F32),
                                    v_now[:, arg * 64:(arg + 1) * 64], start=True, stop=True)
                    elif kind == "gate":
                        ne, hi, lo = (E0, gate0_hi, gate0_lo) if u.kind == "moe0" else (E1, gate1_hi, gate1_lo)
                        for t in range(NT):
                            tok = slice(t * P, (t + 1) * P)
                            ins = split3(ps[:, SH, t * ne:(t + 1) * ne], xT_hi[:, par, tok], xT_lo[:, par, tok],
                                         hi[:], lo[:])
                    elif kind == "peak":
                        t, half = divmod(arg, 2)
                        if arg == 0:
                            wait(pe, "keys_hi", u, 1)
                            wait(pe, "query_ready", u, 1)
                        if arg >= 2:
                            wait(pe, "peak_done", u, arg - 2)
                        for i in range(2):
                            dst = ps[:, 2 * (arg % 2) + i, 0:QW]
                            m(dst, q_st[:, par, half, t * P:(t + 1) * P], k_st[:, par, half, 0, i * QW:(i + 1) * QW],
                              start=True, stop=False)
                            ins = m(dst, ident_b[:], spread_over(mask_q[:, par, t], QH), start=False, stop=True)
                        ins.then_inc(sems["peak_full"], 1)
                    elif kind == "peak_T":
                        wait(pe, "peak_done", u, 2 * NT - 1)
                        for t in range(NT):
                            ins = turn_square(ps[0:H, SH, t * P:(t + 1) * P], neg_max[:, t])
                    elif kind == "scores":
                        half, c = divmod(arg, NCH)
                        chunk = slice(c * P, (c + 1) * P)
                        if arg == 0:
                            wait(pe, "keys_lo", u, 1)
                        if arg >= 2:
                            wait(pe, "exp_done", u, arg - 2)
                        dst = ps[:, 4 + arg % 2, :]
                        m(dst, k_st[:, par, half, 1, chunk], q_st[:, par, half], start=True, stop=False)
                        m(dst, k_st[:, par, half, 0, chunk], q_st[:, par, half], start=False, stop=False)
                        if arg == 0:
                            short("short_free", "peak_T", pe, u, 0)
                        m(dst, pick[:, half, chunk], shift[:, par], start=False, stop=True)\
                            .then_inc(sems["scores_full"], 1)
                    elif kind == "weigh":
                        half, c = divmod(arg, NCH)
                        wait(pe, "exp_done", u, arg)
                        if arg == 0:
                            short("short_free", "values", pe, u, 1)
                        m(ps[:, PV[half], :], v_st[:, par, half, c], prob[:, arg % 3], start=(c == 0),
                          stop=(c == NCH - 1)).then_inc(sems["weigh_done"], 1)
                    elif kind == "attn_out":
                        wait(pe, "norm_done", u, 1)
                        for t in range(NT):
                            ins = m(ps[:, SH, t * P:(t + 1) * P], heads_T[:, t * P:(t + 1) * P], wo[:, u.layer],
                                    start=True, stop=True)
                    elif kind == "up0":
                        if arg >= 4:
                            wait(pe, "silu_done", u, arg - 4)
                        if arg == 0:
                            short("short_free", "xhat_T", pe, u, 0)
                        w = slice(arg * P, (arg + 1) * P)
                        split3(ps[:, arg % 4, :], up0_hi[:, w], up0_lo[:, w], xT_hi[:, par], xT_lo[:, par])\
                            .then_inc(sems["up0_full"], 1)
                    elif kind == "down0":
                        wait(pe, "silu_done", u, 2 * arg + 1)
                        if arg >= 2:
                            wait(pe, "down0_done", u, arg - 2)
                        elif UNITS[u.at - 1].kind == "moe0":
                            wait(pe, "down0_done", UNITS[u.at - 1], E0 - 2 + arg)
                        for t in range(NT):
                            for half in range(2):
                                ins = m(ps[:, 4 + arg % 2, t * P:(t + 1) * P], hid_T[:, arg % 2, half, t * P:(t + 1) * P],
                                        dn0[:, arg, half], start=(half == 0), stop=(half == 1))
                        ins.then_inc(sems["down0_full"], 1)
                    elif kind == "up1":
                        g2, t = divmod(arg, NT)
                        if arg == 0:
                            short("short_free", "xhat_T", pe, u, 0)
                        if arg >= NT:
                            wait(pe, "hid_norm", u, arg - NT)
                        tok = slice(t * P, (t + 1) * P)
                        w = slice(g2 * 512, (g2 + 1) * 512)
                        split3(ps[:, t, :], xT_hi[:, par, tok], xT_lo[:, par, tok], up1_hi[:, w], up1_lo[:, w])\
                            .then_inc(sems["up1_full"], 1)
                    elif kind == "turn1":
                        e, half = divmod(arg, 2)
                        if arg % 4 == 0:
                            wait(pe, "hid_norm", u, (e // 2) * NT + NT - 1)
                        if arg >= 2:
                            wait(pe, "relu_done", u, arg - 2)
                        at = (e % 2) * FF1 + half * P
                        for t in range(NT):
                            ins = turn_square(ps[:, 4 + arg % 2, t * P:(t + 1) * P], hnorm[:, e // 2, t, at:at + P])
                        ins.then_inc(sems["turn1_full"], 1)
                    elif kind == "down1":
                        wait(pe, "relu_done", u, 2 * arg + 1)
                        if arg >= 1:
                            wait(pe, "down1_done", u, arg - 1)
                        elif UNITS[u.at - 1].kind == "moe1":
                            wait(pe, "down1_done", UNITS[u.at - 1], E1 - 1)
                        for t in range(NT):
                            for half in range(2):
                                ins = m(ps[:, 6, t * P:(t + 1) * P], hid_T[:, arg % 2, half, t * P:(t + 1) * P],
                                        dn1[:, arg, half], start=(half == 0), stop=(half == 1))
                        ins.then_inc(sems["down1_full"], 1)
                    if kind in SHORT:
                        ins.then_inc(sems["short_full"], 1)
                pe.drain().then_inc(turn_done, 1)


def kernel(**inputs):
    import numpy as np
    import concourse.bacc as bacc
    from concourse.bass_utils import run_bass_kernel_spmd

    nc = bacc.Bacc("TRN2", target_bir_lowering=False, num_devices=1)
    arrays, args = {}, {}
    for name, value in inputs.items():
        arr = np.ascontiguousarray(value)
        arrays[f"in_{name}"] = arr
        args[name] = nc.dram_tensor(f"in_{name}", arr.shape, mybir.dt.from_np(arr.dtype), kind="ExternalInput").ap()
    out = nc.dram_tensor("out_0", (B, S, D), F32, kind="ExternalOutput").ap()
    build(nc, args, out)
    r = run_bass_kernel_spmd(nc, [arrays], core_ids=[0])
    return r.results[0]["out_0"]
```

```python
from contextlib import ExitStack

import concourse.bass as bass
from concourse import mybir

F32 = mybir.dt.float32
F32R = mybir.dt.float32r
BF16 = mybir.dt.bfloat16
I32 = mybir.dt.int32
U8 = mybir.dt.uint8
U32 = mybir.dt.uint32
ALU = mybir.AluOpType
ACT = mybir.ActivationFunctionType
AX_X = mybir.AxisListType.X

P = 128
B, S, D = 4, 512, 128
NT = S // P
KEYS = 77
H, HD = 16, 8
HALF = H // 2
HK = HALF * KEYS
NCH = -(-HK // P)
HKP = NCH * P
QH = HALF // 2
QW = QH * KEYS
E0, FF0 = 8, 256
E1, FF1 = 4, 256
NPK = NT * H // QH
CROW = 96
CK = CROW + H
BIG = 2.0 ** 100
LOWEST = -3.0e38
EPS = 1e-5
EPS_GATE = 1e-8
SCALE = (float(D) ** -0.5, float(HD) ** -0.5)
TURNS = B // 2


class Unit:
    def __init__(self, at, kind, layer, par):
        self.at, self.kind, self.layer, self.par = at, kind, layer, par


UNITS = [Unit(2 * n + par, kind, layer, par)
         for n, (kind, layer) in enumerate([("attn", 0), ("moe0", 0), ("attn", 1), ("moe1", 1)])
         for par in range(2)]
NEXT = Unit(len(UNITS), "attn", 0, 0)
UNITS.append(NEXT)


NAMES = dict(zip("a0 a1 m0 m1 b0 b1 f0 f1 n0".split(), UNITS))


def steps_of(text):
    words = [word.split(".") for word in text.split()]
    return [(kind, NAMES[unit], int(arg)) for kind, unit, arg in words]


ORDER = steps_of(
    """
scores.a0.0 mask.a1.0 ln.a1.0 mask_T.a1.0 scores.a0.1 values_in.a1.0 scores.a0.2 row_valid.a1.0 weigh.a0.0
weigh.a0.1 weigh.a0.2 ln_hat.a1.0 xhat_T.a1.0 keys.a1.0 scores.a0.3 scores.a0.4 query.a1.0 weigh.a0.3 query.a1.1
keys.a1.1 scores.a0.5 weigh.a0.4 values.a1.0 weigh.a0.5 peak.a1.0 values.a1.1 peak.a1.1 scores.a0.6 peak.a1.2
peak.a1.3 peak.a1.4 scores.a0.7 peak.a1.5 attn_bias.a1.0 scores.a0.8 peak.a1.6 peak.a1.7 peak.a1.8 weigh.a0.6
peak.a1.9 den.a0.0 peak.a1.10 peak.a1.11 scores.a0.9 peak.a1.12 weigh.a0.7 peak.a1.13 peak.a1.14 den.a0.1
peak.a1.15 weigh.a0.8 weigh.a0.9 norm.a0.0 peak_T.a1.0
    """
    """
scores.a1.0 norm.a0.1 scores.a1.1 weigh.a1.0 scores.a1.2 norm.a0.2 scores.a1.3 weigh.a1.1 scores.a1.4 norm.a0.3
weigh.a1.2 den.a1.0 attn_out.a0.0 weigh.a1.3 weigh.a1.4 ln.m0.0 scores.a1.5 scores.a1.6 weigh.a1.5 weigh.a1.6
ln_hat.m0.0 scores.a1.7 xhat_T.m0.0 scores.a1.8 weigh.a1.7 scores.a1.9 gate.m0.0 weigh.a1.8 weigh.a1.9
route.m0.0 norm.a1.0 den.a1.1
    """
    """
up0.m0.0 norm.a1.1 norm.a1.2 up0.m0.1 up0.m0.2 norm.a1.3 up0.m0.3 up0.m0.4 down0.m0.0 down0.m0.1 up0.m0.5
up0.m0.6 attn_out.a1.0 up0.m0.7 ln.m1.0 down0.m0.2 down0.m0.3 up0.m0.8 up0.m0.9 ln_hat.m1.0 up0.m0.10 down0.m0.4
up0.m0.11 xhat_T.m1.0 up0.m0.12 up0.m0.13 mask.b0.0 down0.m0.5 gate.m1.0 up0.m0.14 up0.m0.15 route.m1.0
down0.m0.6 down0.m0.7 mask_T.b0.0 ln.b0.0
    """
    """
up0.m1.0 up0.m1.1 keys.b0.0 attn_bias.b0.0 values_in.b0.0 up0.m1.2 ln_hat.b0.0 keys.b0.1 down0.m1.0 xhat_T.b0.0
up0.m1.3 up0.m1.4 down0.m1.1 row_valid.b0.0 up0.m1.5 up0.m1.6 query.b0.0 up0.m1.7 query.b0.1 down0.m1.2
values.b0.0 up0.m1.8 peak.b0.0 values.b0.1 peak.b0.1 up0.m1.9 down0.m1.3 up0.m1.10 peak.b0.2 peak.b0.3 peak.b0.4
peak.b0.5 up0.m1.11 peak.b0.6 peak.b0.7 up0.m1.12 peak.b0.8 peak.b0.9 down0.m1.4 peak.b0.10 peak.b0.11
down0.m1.5 peak.b0.12 up0.m1.13 peak.b0.13 up0.m1.14 peak.b0.14 peak.b0.15 up0.m1.15 peak_T.b0.0 down0.m1.6
mask.b1.0 down0.m1.7
    """
    """
scores.b0.0 scores.b0.1 mask_T.b1.0 ln.b1.0 scores.b0.2 row_valid.b1.0 keys.b1.0 ln_hat.b1.0 values_in.b1.0
weigh.b0.0 weigh.b0.1 scores.b0.3 weigh.b0.2 keys.b1.1 xhat_T.b1.0 scores.b0.4 scores.b0.5 query.b1.0 query.b1.1
weigh.b0.3 den.b0.0 values.b1.0 weigh.b0.4 scores.b0.6 peak.b1.0 peak.b1.1 peak.b1.2 weigh.b0.5 attn_bias.b1.0
values.b1.1 peak.b1.3 scores.b0.7 peak.b1.4 peak.b1.5 weigh.b0.6 peak.b1.6 peak.b1.7 scores.b0.8 peak.b1.8
peak.b1.9 scores.b0.9 weigh.b0.7 peak.b1.10 peak.b1.11 weigh.b0.8 peak.b1.12 peak.b1.13 peak.b1.14 weigh.b0.9
peak.b1.15 den.b0.1 peak_T.b1.0
    """
    """
scores.b1.0 norm.b0.0 scores.b1.1 norm.b0.1 weigh.b1.0 scores.b1.2 scores.b1.3 norm.b0.2 norm.b0.3 weigh.b1.1
attn_out.b0.0 weigh.b1.2 scores.b1.4 ln.f0.0 ln_hat.f0.0 weigh.b1.3 out_res.f0.0 ln2.f0.0 weigh.b1.4 scores.b1.5
den.b1.0 xhat_T.f0.0 weigh.b1.5 scores.b1.6 gate.f0.0 fold.f0.0 up1.f0.0 up1.f0.1 scores.b1.7 scores.b1.8
route.f0.0 hid_hat.f0.0 hid_hat.f0.1 up1.f0.2 weigh.b1.6 scores.b1.9 hid_hat.f0.2 weigh.b1.7 up1.f0.3 weigh.b1.8
weigh.b1.9 den.b1.1 hid_hat.f0.3
    """
    """
turn1.f0.0 turn1.f0.1 norm.b1.0 norm.b1.1 norm.b1.2 norm.b1.3 up1.f0.4 turn1.f0.2 up1.f0.5 up1.f0.6 turn1.f0.3
attn_out.b1.0 hid_hat.f0.4 down1.f0.0 ln.f1.0 hid_hat.f0.5 down1.f0.1 ln_hat.f1.0 up1.f0.7 hid_hat.f0.6
hid_hat.f0.7 out_res.f1.0 ln2.f1.0 xhat_T.f1.0 turn1.f0.4 turn1.f0.5 up1.f1.0 up1.f1.1 turn1.f0.6 hid_hat.f1.0
up1.f1.2 gate.f1.0 hid_hat.f1.1 fold.f1.0 hid_hat.f1.2 route.f1.0 turn1.f0.7 down1.f0.2 up1.f1.3 up1.f1.4
hid_hat.f1.3 down1.f0.3
    """
    """
turn1.f1.0 hid_hat.f1.4 mask.n0.0 turn1.f1.1 turn1.f1.2 out_stats.f0.0 out_shift.f0.0 ln.n0.0 up1.f1.5
down1.f1.0 mask_T.n0.0 values_in.n0.0 turn1.f1.3 hid_hat.f1.5 up1.f1.6 ln_hat.n0.0 up1.f1.7 hid_hat.f1.6
hid_hat.f1.7 down1.f1.1 xhat_T.n0.0 keys.n0.0 turn1.f1.4 turn1.f1.5 row_valid.n0.0 turn1.f1.6 query.n0.0
keys.n0.1 turn1.f1.7 query.n0.1 down1.f1.2 out_hat.f0.0 values.n0.0 down1.f1.3 out_stats.f1.0 values.n0.1
peak.n0.0 peak.n0.1 peak.n0.2 peak.n0.3 out_shift.f1.0 peak.n0.4 peak.n0.5 peak.n0.6 peak.n0.7 peak.n0.8
peak.n0.9 peak.n0.10 peak.n0.11 peak.n0.12 peak.n0.13 peak.n0.14 peak.n0.15 peak_T.n0.0 attn_bias.n0.0
out_hat.f1.0
    """
    )

W0_T, CTX_T, K0_A, K0_B, V0, COLS, W1_T, ROWS, JOINED, JOINED_BIAS, K1_A, K1_B, V1 = range(1, 14)
CASTS, UPS = 0, 14

FIRST = steps_of(
    """
mask.n0.0 ln.n0.0 setup.n0.2 setup.n0.1 ln_hat.n0.0 mask_T.n0.0 setup.n0.3 setup.n0.4 xhat_T.n0.0 setup.n0.5
setup.n0.0 row_valid.n0.0 keys.n0.0 values_in.n0.0 setup.n0.6 query.n0.0 keys.n0.1 setup.n0.7 query.n0.1
values.n0.0 setup.n0.8 setup.n0.9 peak.n0.0 values.n0.1 setup.n0.10 setup.n0.14 peak.n0.1 peak.n0.2
attn_bias.n0.0 peak.n0.3 peak.n0.4 peak.n0.5 peak.n0.6 peak.n0.7 setup.n0.11 peak.n0.8 setup.n0.12 setup.n0.13
peak.n0.9 peak.n0.10 peak.n0.11 peak.n0.12 peak.n0.13 peak.n0.14 peak.n0.15 peak_T.n0.0
    """)
SHORT = ("mask_T", "xhat_T", "row_valid", "query", "values", "gate", "peak_T", "attn_out")


POOL_LAST = {"ln": "ln_rstd", "ln2": "ln2_rstd", "attn_bias": "bias_added", "keys": "keys_lo",
             "query": "query_ready", "up1": "hid_rstd", "out_stats": "out_rstd", "out_res": "out_bias"}


def build(nc: bass.Bass, a, out):
    ctx = ExitStack()
    with ctx:
        def sb(name, shape, dt=F32):
            return ctx.enter_context(nc.sbuf_tensor(name, shape, dt))

        def sem(name):
            return ctx.enter_context(nc.semaphore(name))

        rows_sb = sb("rows_sb", [29, P])
        NB_LNG, NB_LNB, NB_RNG, NB_RNB, NB_B, NB_HB, NB_RW = 0, 8, 16, 17, 18, 21, 25
        cols = sb("cols", [P, 29])
        flat_sb = sb("flat_sb", [1, 4, P])
        bhv_sb = sb("bhv_sb", [1, P])
        spread = sb("spread", [P, 4, P])
        w_T = sb("w_T", [P, 3, P])
        w_head = sb("w_head", [P, 3, P])
        ctx_nat = sb("ctx_nat", [KEYS, B, P])
        ctx_hi = sb("ctx_hi", [P, B * KEYS], F32R)
        ctx_lo = sb("ctx_lo", [P, B * KEYS], F32R)
        ctx_T = sb("ctx_T", [P, B * KEYS])
        k_full = sb("k_full", [P, B * KEYS])
        router_in = sb("router_in", [P, 2, E1])
        gate_nat = sb("gate_nat", [P, E0])

        ones = sb("ones", [P, P])
        ones_r = sb("ones_r", [KEYS, P], F32R)
        ident = sb("ident", [P, P])
        ident_b = sb("ident_b", [P, P], BF16)
        pick = sb("pick", [CK, 2, HKP], F32R)
        own_v = sb("own_v", [P, NCH, HALF * HD])
        own_k2 = sb("own_k2", [P, 2, HALF])
        own_k = sb("own_k", [P, HALF])
        iota8 = sb("iota8", [P, E0])
        neg_half = sb("neg_half", [P, NT])
        keys_t = sb("keys_t", [P, 1])
        wqk_hi = sb("wqk_hi", [P, 2, 2, 2, P], F32R)
        wqk_lo = sb("wqk_lo", [P, 2, 2, 2, P], F32R)
        qk_bias = sb("qk_bias", [P, 2, 2, 2])
        wv = sb("wv", [P, 2, P])
        v_bias = sb("v_bias", [1, P])
        wo = sb("wo", [P, 2, P])
        k_hi = sb("k_hi", [P, 2, 2, B, KEYS], F32R)
        k_lo = sb("k_lo", [P, 2, 2, B, KEYS], F32R)
        v_all = sb("v_all", [KEYS, 2, B, P])
        gate0_hi = sb("gate0_hi", [P, E0], F32R)
        gate0_lo = sb("gate0_lo", [P, E0], F32R)
        gate1 = sb("gate1", [P, E1])
        gate1_hi = sb("gate1_hi", [P, E1], F32R)
        gate1_lo = sb("gate1_lo", [P, E1], F32R)
        gate1_sum = sb("gate1_sum", [P, 2, E1])
        up0_hi = sb("up0_hi", [P, E0 * FF0], F32R)
        up0_lo = sb("up0_lo", [P, E0 * FF0], F32R)
        dn0 = sb("dn0", [P, E0, 2, P])
        up1_hi = sb("up1_hi", [P, E1 * FF1], F32R)
        up1_lo = sb("up1_lo", [P, E1 * FF1], F32R)
        dn1 = sb("dn1", [P, E1, 2, P])

        x_in = sb("x_in", [P, 2, NT, P])
        mask_in = [sb("mask0_in", [P, 2, NT, KEYS], I32), sb("mask1_in", [P, 2, NT, KEYS], U8)]
        x = sb("x", [P, 2, NT, P])
        x_bias = sb("x_bias", [P, 2, NT, P])
        bn = sb("bn", [P, 2, NT, 6])
        stat = sb("stat", [P, 2, NT, 2])
        var_e = sb("var_e", [P, 2, NT])
        rstd = sb("rstd", [P, 2, NT])
        mshift = sb("mshift", [P, 2, NT])
        bn2 = sb("bn2", [P, NT, 6])
        stat2 = sb("stat2", [P, NT, 2])
        var_e2 = sb("var_e2", [P, NT])
        rstd2 = sb("rstd2", [P, NT])
        xhat = sb("xhat", [P, 2, NT, P])
        xT_hi = sb("xT_hi", [P, 2, S], F32R)
        xT_lo = sb("xT_lo", [P, 2, S], F32R)
        mask_q = sb("mask_q", [P, 2, NT, KEYS], BF16)
        shift = sb("shift", [CK, 2, S], F32R)
        valid = sb("valid", [P, S])
        q_full = sb("q_full", [P, 2, S])
        q_st = sb("q_st", [P, 2, 2, S], F32R)
        k_st = sb("k_st", [P, 2, 2, 2, HKP], F32R)
        v_hi = sb("v_hi", [KEYS, P], F32R)
        v_lo = sb("v_lo", [KEYS, P], F32R)
        v_st = sb("v_st", [P, 2, 2, NCH, P])
        neg_max = sb("neg_max", [P, NT, H])
        prob = sb("prob", [P, 3, S])
        den = sb("den", [P, S])
        inv = sb("inv", [P, S])
        heads_T = sb("heads_T", [P, S])
        logit = sb("logit", [P, NT, 8])
        top = sb("top", [P, NT, 8])
        top_at = sb("top_at", [P, NT, 8], U32)
        top_f = sb("top_f", [P, NT, 2])
        lead = sb("lead", [P, NT, 8])
        lead_e = sb("lead_e", [P, NT, 8])
        gsum = sb("gsum", [P, NT])
        gden = sb("gden", [P, NT])
        ginv = sb("ginv", [P, NT])
        gw = sb("gw", [P, NT, 2])
        pair = sb("pair", [P, NT, 2, 8])
        comb = sb("comb", [P, 2, NT, 8])
        hid_T = sb("hid_T", [P, 2, 2, S])
        hbn = sb("hbn", [P, NT, 2, 6])
        hstat = sb("hstat", [P, NT, 2, 2])
        hvar = sb("hvar", [P, NT, 2])
        hrstd = sb("hrstd", [P, NT, 2])
        hshift = sb("hshift", [P, NT, 2])
        hnorm = sb("hnorm", [P, 2, NT, 2 * FF1])
        acc = sb("acc", [P, 2, NT, P])
        out_bn = sb("out_bn", [P, NT, 6])
        out_stat = sb("out_stat", [P, NT, 2])
        out_var = sb("out_var", [P, NT])
        out_rstd = sb("out_rstd", [P, NT])
        out_shift = sb("out_shift", [P, NT])
        fold = sb("fold", [P, NT, E1])

        w_nat = prob[:].rearrange("p a c -> p (a c)")[:, 0:7 * P].rearrange("p (i c) -> p i c", i=7)
        pick_f = hid_T[0:CK].rearrange("p a b c -> p (a b c)")[:, 0:2 * HKP].rearrange("p (i c) -> p i c", i=2)
        up0_f = hnorm[:, 0].rearrange("p a c -> p (a c)")
        up1_f = hnorm[:, 1].rearrange("p a c -> p (a c)")[:, 0:E1 * FF1]

        ps = ctx.enter_context(nc.psum_tensor("ps", [P, 8, 512], F32))
        PK = {1: (2, 3, 1), 4: (2, 3), 5: (2, 3), 8: (2, 3, 0)}
        UP0 = (2, 0)
        UP1 = (0, 2, 3)
        DN1 = (6, 1)
        SETUP_BANK = (None, 1, 2, 4, 5, 6, 0, 3, 1, 4, 5, 6, 1, 4)
        SH = 7
        PV = ((6, 0), (1, 6))
        VAL = (slice(0, 64), slice(64, P))
        DEN = (slice(64, P), slice(0, 64))

        ld_rows, ld_flat, ld_w, ld_w1, ld_head, ld_ctx = (
            sem(n) for n in ("ld_rows", "ld_flat", "ld_w", "ld_w1", "ld_head", "ld_ctx"))
        ld_gate, ld_up0, ld_dn, ld_up1 = (sem(n) for n in ("ld_gate", "ld_up0", "ld_dn", "ld_up1"))
        IDENT, CONST = 6, 16
        ident_made, const_made, const_cast = sem("ident_made"), sem("const_made"), sem("const_cast")
        setup_full, setup_free, setup_dve = sem("setup_full"), sem("setup_free"), sem("setup_dve")
        up_hi_made, up_lo_made = sem("up_hi_made"), sem("up_lo_made")
        turn_done = sem("turn_done")

        counts = {}

        phase = {}

        sems = {}
        for name, kinds in {
            "mask_ready": ("mask",), "ln_bn": ("ln",), "ln_stats": ("ln",), "ln_var": ("ln",), "ln_rstd": ("ln",),
            "mshift_ready": ("ln_hat",), "xhat_ready": ("ln_hat",), "ln2_bn": ("ln2",), "ln2_stats": ("ln2",), "ln2_var": ("ln2",),
            "ln2_rstd": ("ln2",), "bias_added": ("attn_bias",), "values_hi": ("values_in",), "values_ready": ("values_in",),
            "keys_hi": ("keys",), "keys_lo": ("keys",), "short_full": SHORT, "short_free": SHORT,
            "xT_hi_ready": ("xhat_T",), "query_hi": ("query",), "query_ready": ("query",),
            "peak_full": ("peak",), "peak_done": ("peak",), "scores_full": ("scores",), "exp_done": ("scores",),
            "weigh_done": ("weigh",), "den_ready": ("den",), "inv_ready": ("norm",), "norm_done": ("norm",),
            "fold_scaled": ("fold",), "fold_mean": ("fold",), "fold_added": ("fold",), "fold_done": ("fold",),
            "gate_den_eps": ("fold",), "top_ready": ("route",), "lead_ready": ("route",), "lead_exp": ("route",),
            "gate_den": ("route",), "gate_inv": ("route",), "pair_is": ("route",), "pair_ready": ("route",),
            "comb_ready": ("route",),
            "up0_full": ("up0",), "silu_done": ("up0",), "down0_full": ("down0",), "down0_done": ("down0",),
            "up1_full": ("up1",), "hid_bn": ("up1",), "hid_stats": ("up1",), "hid_var": ("up1",), "hid_rstd": ("up1",),
            "hid_shift": ("hid_hat",), "hid_norm": ("hid_hat",), "turn1_full": ("turn1",), "relu_done": ("turn1",),
            "down1_full": ("down1",), "down1_done": ("down1",),
            "next_in": (), "acc_free": (), "out_bn": ("out_stats",), "out_stats": ("out_stats",), "out_var": ("out_stats",),
            "out_rstd": ("out_stats",), "out_bias": ("out_res",), "out_mshift": ("out_shift",), "out_hat": ("out_shift",), "out_gain": ("out_hat",),
            "out_ready": ("out_hat",),
        }.items():
            sems[name] = sem(name)
            counts[name] = kinds
        go = {name: sem(f"go_{name}") for name in ("act", "dve", "pe", "sp")}
        turn_loaded, next_loaded = sem("turn_loaded"), sem("next_loaded")
        stored = sem("stored")

        def begin(steps):
            phase["steps"] = steps
            phase["table"] = {}
            for name, kinds in counts.items():
                table, n = phase["table"].setdefault(name, {}), 0
                for kind, u, arg in steps:
                    if kind in kinds:
                        n += 1
                        table[kind, u.at, arg] = n

        def wait(eng, name, u, arg, kind=None, back=0):
            table = phase["table"][name]
            for k in (kind,) if kind else counts[name]:
                n = table.get((k, u.at, arg), 0) - back
                if n >= 1:
                    eng.wait_ge(sems[name], n)

        def short(name, kind, eng, u, arg, back=0):
            wait(eng, name, u, arg, kind, back)

        def batch(u, turn):
            return (turn + (u is NEXT)) * 2 + u.par

        def sem_number(s):
            return s.num

        def start_turn(eng, name):
            eng.wait_ge(go[name], 1)
            eng.sem_clear(go[name])

        def keys_of_batch(src, u, half, turn):
            rows = src[:].rearrange("p l h b k -> p (l h b) k")
            return rows[:, bass.ds(batch(u, turn) + (2 * u.layer + half) * B, 1), :].bitcast(F32)

        def values_of_batch(u, turn):
            rows = v_all[:].rearrange("p l b d -> p (l b) d")
            return rows[:, bass.ds(batch(u, turn) + u.layer * B, 1), :].rearrange("p o d -> p (o d)")

        def up1_bank(u, arg):
            return UP1[arg % 3]

        def attn_before(u):
            prev = [v for v in UNITS[:u.at] if v.kind == "attn"]
            return prev[-1] if prev else None

        def x_of(u):
            return x_in if u.kind == "attn" and u.layer == 0 else x

        def spread_over(row, n):
            return row.unsqueeze(1).broadcast_to([row.shape[0], n, row.shape[1]])

        block = ctx.enter_context(nc.Block())

        @block.sync
        def _(sp):
            begin(ORDER)

            def load_batch(turn, par, layer, loaded):
                b = 2 * turn + par
                if layer == 0:
                    if turn:
                        wait(sp, "xhat_ready", UNITS[par], 0)
                        wait(sp, "bias_added", UNITS[par], 0)
                    sp.dma_start(x_in[:, par], a["x"][b].rearrange("(t p) d -> p t d", p=P)).then_inc(loaded, 16)
                if turn:
                    wait(sp, "mask_ready", UNITS[4 * layer + par], 0)
                m = a["mask_Bx1xSxS2_ik1"][b, 0] if layer == 0 else a["mask_BxSxS2_bk1"][b]
                sp.dma_start(mask_in[layer][:, par], m.rearrange("(t p) k -> p t k", p=P)).then_inc(loaded, 16)

            begin(ORDER)
            sp.dma_start(w_nat[:, 0], a["L0_xattn_Wq"]).then_inc(ld_w, 16)
            sp.dma_start(x_in[:, 0], a["x"][0].rearrange("(t p) d -> p t d", p=P)).then_inc(next_loaded, 16)
            sp.dma_start(w_nat[:, 3], a["L0_xattn_Wo"]).then_inc(ld_w, 16)
            sp.wait_ge(next_loaded, 32)
            sp.sem_inc(sems["next_in"], 1)
            for n, name in enumerate(["L1_xattn_Wq", "L1_xattn_Wk", "L1_xattn_Wv"]):
                sp.dma_start(w_nat[:, 4 + n], a[name]).then_inc(ld_w1, 16)
            for n, name in enumerate(["L1_xattn_Whq", "L1_xattn_Whk", "L1_xattn_Whv"]):
                sp.dma_start(w_head[:, n].rearrange("p (h d) -> p h d", h=H),
                             a[name].rearrange("h e d -> e h d")).then_inc(ld_head, 16)
            for n, (row, k) in enumerate([("L1_ffn_ln_g", NB_LNG), ("L1_ffn_ln_b", NB_LNB)]):
                sp.dma_start(rows_sb[k:k + 8, :], a[row].rearrange("e (c p) -> (e c) p", p=P)).then_inc(ld_rows, 16)
            for n, name in enumerate(["L1_ffn_rn_g", "L1_ffn_rn_b", "L1_xattn_bq", "L1_xattn_bk", "L1_xattn_bv"]):
                sp.dma_start(rows_sb[NB_RNG + n:NB_RNG + n + 1, :], a[name].unsqueeze(0)).then_inc(ld_rows, 16)
            for n, name in enumerate(["L1_xattn_bhq", "L1_xattn_bhk"]):
                for twice in range(2):
                    sp.dma_start(rows_sb[NB_HB + 2 * n:NB_HB + 2 * n + 2, 64 * twice:64 * twice + 64],
                                 a[name].rearrange("(g h) d -> g (h d)", g=2)).then_inc(ld_rows, 16)
            sp.dma_start(rows_sb[NB_RW:NB_RW + E1, :], a["L1_ffn_router_w"]).then_inc(ld_rows, 16)
            for n, name in enumerate(["L0_xattn_bo", "L1_xattn_bo", "L1_ffn_on_g", "L1_ffn_on_b"]):
                sp.dma_start(flat_sb[:, n], a[name].unsqueeze(0)).then_inc(ld_flat, 16)
            sp.dma_start(bhv_sb[:], a["L1_xattn_bhv"].rearrange("h d -> (h d)").unsqueeze(0)).then_inc(ld_flat, 16)
            sp.dma_start(wo[:, 1], a["L1_xattn_Wo"]).then_inc(ld_w1, 16)
            sp.dma_start(gate_nat[:], a["L0_ffn_gate_w"]).then_inc(ld_gate, 16)
            sp.dma_start(up0_f.rearrange("p (e f) -> p e f", e=E0), a["L0_ffn_w1"].rearrange("e d f -> d e f")).then_inc(ld_up0, 16)
            load_batch(0, 1, 0, turn_loaded)
            load_batch(0, 0, 1, turn_loaded)
            load_batch(0, 1, 1, turn_loaded)
            sp.dma_start(up1_f.rearrange("p (e f) -> p e f", e=E1), a["L1_ffn_w1"].rearrange("e d f -> d e f")).then_inc(ld_up1, 16)
            sp.dma_start(dn0[:], a["L0_ffn_w2"].rearrange("e (c p) d -> p e c d", p=P)).then_inc(ld_dn, 16)
            sp.dma_start(dn1[:], a["L1_ffn_w2"].rearrange("e (c p) d -> p e c d", p=P)).then_inc(ld_dn, 16)
            sp.wait_ge(ld_dn, 32)
            sp.wait_ge(ld_w1, 64)
            sp.wait_ge(turn_loaded, 64)
            sp.sem_inc(turn_done, 1)
            for turn in range(TURNS):
                start_turn(sp, "sp")
                if turn + 1 < TURNS:
                    load_batch(turn + 1, 0, 0, next_loaded)
                if turn:
                    sp.wait_ge(stored, 32 * turn)
                sp.sem_inc(sems["acc_free"], 1)
                if turn + 1 < TURNS:
                    sp.wait_ge(next_loaded, 32 * (turn + 2))
                sp.sem_inc(sems["next_in"], 1)
                if turn + 1 < TURNS:
                    for par, layer in ((1, 0), (0, 1), (1, 1)):
                        load_batch(turn + 1, par, layer, turn_loaded)
                for par in range(2):
                    wait(sp, "out_ready", UNITS[6 + par], 0)
                    sp.dma_start(out[2 * turn + par].rearrange("(t p) d -> p t d", p=P), acc[:, par])\
                      .then_inc(stored, 16)
                if turn + 1 < TURNS:
                    sp.wait_ge(turn_loaded, 64 * (turn + 2))
                    sp.sem_inc(turn_done, 1)
            sp.wait_ge(stored, 16 * B)

        @block.gpsimd
        def _(pool):
            g = nc.gpsimd
            g.memset(ident[:], 0.0).then_inc(ident_made, 1)
            g.memset(ones[:], 1.0).then_inc(ident_made, 1)
            pool.wait_ge(ident_made, 2)
            g.affine_select(out=ident[:], in_=ident[:], compare_op=ALU.not_equal, fill=1.0, base=0,
                            pattern=[[-1, P]], channel_multiplier=1).then_inc(ident_made, 1)
            g.memset(neg_half[:], -0.5).then_inc(ident_made, 1)
            g.memset(keys_t[:], float(KEYS)).then_inc(ident_made, 1)
            g.memset(shift[:, 0].bitcast(F32), 0.0).then_inc(ident_made, 1)
            pool.wait_ge(ident_made, IDENT)

            def constants():
                g.memset(own_k2[:], 1.0).then_inc(const_made, 1)
                g.memset(own_v[:], 1.0).then_inc(const_made, 1)
                g.memset(pick_f, 0.0).then_inc(const_made, 1)
                g.memset(shift[:, 1].bitcast(F32), 0.0).then_inc(const_made, 1)
                for par in range(2):
                    g.memset(k_st[:, par].rearrange("p h l k -> p (h l) k")[:, :, HK:HKP].bitcast(F32),
                             0.0).then_inc(const_made, 1)
                g.iota(iota8[:], [[1, E0]], base=0, channel_multiplier=0,
                       allow_small_or_imprecise_dtypes=True).then_inc(const_made, 1)
                g.memset(lead[:], 0.0).then_inc(const_made, 1)
                n = 8
                pool.wait_ge(const_made, n)
                for half in range(2):
                    keys_of = pick_f[:, half, 0:HK].rearrange("p (h k) -> p h k", h=HALF)
                    g.affine_select(out=keys_of, in_=keys_of, compare_op=ALU.not_equal, fill=1.0, base=0,
                                    pattern=[[0, HALF], [-1, KEYS]], channel_multiplier=1).then_inc(const_made, 1)
                    pool.wait_ge(const_made, n + 1 + 2 * half)
                    g.affine_select(out=keys_of, in_=keys_of, compare_op=ALU.not_equal, fill=1.0,
                                    base=-(CROW + HALF * half), pattern=[[-1, HALF], [0, KEYS]],
                                    channel_multiplier=1).then_inc(const_made, 1)
                v_view = own_v[:].rearrange("p c (h j) -> p c h j", h=HALF)
                g.affine_select(out=v_view, in_=v_view, compare_op=ALU.is_ge, fill=0.0, base=0,
                                pattern=[[P, NCH], [-KEYS, HALF], [0, HD]], channel_multiplier=1).then_inc(const_made, 1)
                g.affine_select(out=own_k2[:], in_=own_k2[:], compare_op=ALU.is_ge, fill=0.0, base=0,
                                pattern=[[-HALF * HD, 2], [-HD, HALF]], channel_multiplier=1).then_inc(const_made, 1)
                pool.wait_ge(const_made, n + 6)
                g.affine_select(out=v_view, in_=v_view, compare_op=ALU.is_ge, fill=0.0, base=KEYS - 1,
                                pattern=[[-P, NCH], [KEYS, HALF], [0, HD]], channel_multiplier=-1).then_inc(const_made, 1)
                g.affine_select(out=own_k2[:], in_=own_k2[:], compare_op=ALU.is_ge, fill=0.0, base=HD - 1,
                                pattern=[[HALF * HD, 2], [HD, HALF]], channel_multiplier=-1).then_inc(const_made, 1)
                pool.wait_ge(const_made, CONST)

            def meet():
                pool.wait_ge(turn_done, 4)
                pool.sem_clear(range(sem_number(sems["mask_ready"]), sem_number(sems["out_ready"]) + 1))
                pool.sem_clear(turn_done)
                for name in ("act", "dve", "pe", "sp"):
                    pool.drain().then_inc(go[name], 1)

            def steps(turn):
                before = None
                for kind, u, arg in phase["steps"]:
                    if kind == "setup" and arg == CASTS:
                        constants()
                    if kind == "setup" and arg == UPS:
                        wait(pool, *before)
                        before = None
                        pool.wait_ge(up_hi_made, 1)
                        g.tensor_tensor(up0_lo[:], up0_f, up0_hi[:].bitcast(F32), ALU.subtract).then_inc(up_lo_made, 1)
                        pool.wait_ge(up_hi_made, 2)
                        pool.wait_ge(up_lo_made, 1)
                        g.tensor_tensor(up1_lo[:], up1_f, up1_hi[:].bitcast(F32), ALU.subtract).then_inc(up_lo_made, 1)
                        pool.wait_ge(up_lo_made, 2)
                    if kind == "keys" and phase["steps"] is FIRST and arg == 0:
                        pool.wait_ge(setup_free, V0)
                        pool.wait_ge(const_cast, 2)
                    if kind == "attn_bias" and phase["steps"] is FIRST:
                        pool.wait_ge(setup_free, ROWS)
                    last = POOL_LAST.get(kind)
                    if last is None:
                        continue
                    if before:
                        wait(pool, *before)
                    before = (last, u, arg)
                    if kind in ("ln", "ln2"):
                        two = kind == "ln2"
                        ve, rs = (var_e2[:], rstd2[:]) if two else (var_e[:, u.par], rstd[:, u.par])
                        pre = "ln2" if two else "ln"
                        wait(pool, pre + "_var", u, 0)
                        g.tensor_tensor(rs, ve, neg_half[:], ALU.pow).then_inc(sems[pre + "_rstd"], 1)
                    elif kind == "attn_bias":
                        if u.layer == 1:
                            wait(pool, "xhat_ready", u, 0)
                        elif u is NEXT:
                            wait(pool, "out_ready", UNITS[6], 0)
                        g.tensor_tensor(x_bias[:, u.par], x_of(u)[:, u.par], spread_over(spread[:, u.layer], NT),
                                        ALU.add).then_inc(sems["bias_added"], 1)
                    elif kind == "keys":
                        src = keys_of_batch(k_lo, u, arg, turn)
                        g.tensor_tensor(
                            k_st[:, u.par, arg, 1, 0:HK].rearrange("p (h k) -> p h k", h=HALF),
                            src.broadcast_to([P, HALF, KEYS]),
                            own_k[:].unsqueeze(2).broadcast_to([P, HALF, KEYS]), ALU.mult).then_inc(sems["keys_lo"], 1)
                    elif kind == "query":
                        wait(pool, "query_hi", u, arg)
                        lo = slice(64, P)
                        g.tensor_tensor(q_st[lo, u.par, arg], q_full[lo, arg], q_st[lo, u.par, arg].bitcast(F32),
                                        ALU.subtract).then_inc(sems["query_ready"], 1)
                    elif kind == "up1":
                        t = arg % NT
                        wait(pool, "hid_var", u, arg)
                        g.tensor_tensor(hrstd[:, t], hvar[:, t], neg_half[:, 0:2], ALU.pow).then_inc(sems["hid_rstd"], 1)
                    elif kind == "out_stats":
                        wait(pool, "out_var", u, 0)
                        g.tensor_tensor(out_rstd[:], out_var[:], neg_half[:], ALU.pow).then_inc(sems["out_rstd"], 1)
                    elif kind == "out_res":
                        wait(pool, "ln_var", u, 0)
                        g.tensor_tensor(x_bias[:, u.par], x[:, u.par], spread_over(spread[:, 3], NT),
                                        ALU.add).then_inc(sems["out_bias"], 1)

                if before:
                    wait(pool, *before)

            begin(FIRST)
            steps(-1)
            begin(ORDER)
            with pool.Fori(0, TURNS) as turn:
                meet()
                steps(turn)

        @block.scalar
        def _(act):
            s = nc.scalar
            act.dma_start(w_nat[:, 1], a["L0_xattn_Wk"]).then_inc(ld_w, 16)
            act.dma_start(mask_in[0][:, 0], a["mask_Bx1xSxS2_ik1"][0, 0].rearrange("(t p) k -> p t k", p=P))\
               .then_inc(next_loaded, 16)
            act.dma_start(w_nat[:, 2], a["L0_xattn_Wv"]).then_inc(ld_w, 16)
            act.dma_start(ctx_nat[:], a["ctx_1024"].rearrange("b k d -> k b d")).then_inc(ld_ctx, 16)
            act.wait_ge(ident_made, IDENT)

            def steps(turn):
                for kind, u, arg in phase["steps"]:
                    if kind == "setup":
                        if arg == UPS:
                            act.wait_ge(const_made, CONST)
                            for par in range(2):
                                for half in range(2):
                                    s.activation(v_st[:, par, half, :, DEN[half]], own_v[:], ACT.Copy)
                            act.wait_ge(ld_up0, 16)
                            s.activation(up0_hi[:], up0_f, ACT.Copy).then_inc(up_hi_made, 1)
                            act.wait_ge(ld_up1, 16)
                            s.activation(up1_hi[:], up1_f, ACT.Copy).then_inc(up_hi_made, 1)
                            act.wait_ge(up_hi_made, 2)
                    elif kind == "values_in":
                        if phase["steps"] is FIRST:
                            act.wait_ge(setup_free, V0)
                        if u.at:
                            prev = [v for v in UNITS[:u.at] if v.kind == "attn"]
                            if prev:
                                short("short_full", "values", act, prev[-1], 1)
                        s.activation(v_hi[:], values_of_batch(u, turn), ACT.Copy).then_inc(sems["values_hi"], 1)
                    elif kind == "ln_hat":
                        wait(act, "mshift_ready", u, 0)
                        if u.at >= 2:
                            short("short_full", "xhat_T", act, UNITS[u.at - 2], 0)
                        src = x_of(u)
                        for t in range(NT):
                            ins = s.activation(xhat[:, u.par, t], src[:, u.par, t], ACT.Identity,
                                               bias=mshift[:, u.par, t:t + 1], scale=rstd[:, u.par, t:t + 1])
                        ins.then_inc(sems["xhat_ready"], 1)
                    elif kind == "mask_T":
                        short("short_full", kind, act, u, arg)
                        s.activation(shift[0:KEYS, u.par], ps[0:KEYS, SH, 0:S // 2].bitcast(BF16),
                                     ACT.Copy).then_inc(sems["short_free"], 1)
                    elif kind == "xhat_T":
                        short("short_full", kind, act, u, arg)
                        s.activation(xT_hi[:, u.par], ps[:, SH, :], ACT.Copy).then_inc(sems["xT_hi_ready"], 1)
                    elif kind == "row_valid":
                        short("short_full", kind, act, u, arg)
                        s.activation(valid[:], ps[:, SH, :], ACT.Sign, bias=keys_t[:],
                                     scale=1.0 / BIG).then_inc(sems["short_free"], 1)
                    elif kind == "query":
                        short("short_free", kind, act, u, arg)
                        s.activation(q_st[:, u.par, arg], q_full[:, arg], ACT.Copy).then_inc(sems["query_hi"], 1)
                    elif kind == "peak_T":
                        short("short_full", kind, act, u, arg)
                        s.activation(shift[CROW:CK, u.par], ps[0:H, SH, :], ACT.Copy).then_inc(sems["short_free"], 1)
                    elif kind == "scores":
                        wait(act, "scores_full", u, arg)
                        if arg >= 3:
                            wait(act, "weigh_done", u, arg - 3)
                        s.activation(prob[:, arg % 3], ps[:, 4 + arg % 2, :], ACT.Exp,
                                     scale=SCALE[u.layer]).then_inc(sems["exp_done"], 1)
                    elif kind == "den":
                        wait(act, "weigh_done", u, NCH * (arg + 1) - 1)
                        if arg == 0:
                            prev = attn_before(u)
                            if prev:
                                wait(act, "inv_ready", prev, NT - 1)
                        s.activation(den[64 * arg:64 * arg + 64], ps[DEN[arg], PV[u.par][arg], :],
                                     ACT.Copy).then_inc(sems["den_ready"], 1)
                    elif kind == "route":
                        wait(act, "lead_ready", u, 0)
                        s.activation(lead_e[:], lead[:], ACT.Exp).then_inc(sems["lead_exp"], 1)
                    elif kind == "up0":
                        e, half = divmod(arg, 2)
                        wait(act, "up0_full", u, arg)
                        if e >= 2:
                            wait(act, "down0_full", u, e - 2)
                        s.activation(hid_T[:, e % 2, half], ps[:, UP0[u.par] + arg % 2, :], ACT.Silu).then_inc(sems["silu_done"], 1)
                    elif kind == "hid_hat":
                        g2, t = divmod(arg, NT)
                        wait(act, "hid_shift", u, arg)
                        for e in range(2):
                            last = s.activation(hnorm[:, g2, t, e * FF1:(e + 1) * FF1],
                                                ps[:, up1_bank(u, arg), e * FF1:(e + 1) * FF1], ACT.Identity,
                                                bias=hshift[:, t, e:e + 1], scale=hrstd[:, t, e:e + 1])
                        last.then_inc(sems["hid_norm"], 1)
                    elif kind == "out_shift":
                        wait(act, "out_mshift", u, 0)
                        for t in range(NT):
                            ins = s.activation(acc[:, u.par, t], acc[:, u.par, t], ACT.Identity,
                                               bias=out_shift[:, t:t + 1], scale=out_rstd[:, t:t + 1])
                        ins.then_inc(sems["out_hat"], 1)
                    elif kind == "turn1":
                        e, half = divmod(arg, 2)
                        wait(act, "turn1_full", u, arg)
                        if e >= 2:
                            wait(act, "down1_full", u, e - 2)
                        s.activation(hid_T[:, e % 2, half], ps[:, 4 + arg % 2, :], ACT.Relu,
                                     bias=cols[:, NB_LNB + arg:NB_LNB + arg + 1],
                                     scale=cols[:, NB_LNG + arg:NB_LNG + arg + 1]).then_inc(sems["relu_done"], 1)

            begin(FIRST)
            steps(-1)
            act.drain().then_inc(turn_done, 1)
            begin(ORDER)
            with act.Fori(0, TURNS) as turn:
                start_turn(act, "act")
                steps(turn)
                act.drain().then_inc(turn_done, 1)

        def fold_router(dve, v, turn, u):
            def then(ins, name):
                ins.then_inc(sems[name], 1)
                wait(dve, name, u, 0)

            def over(z):
                return z.unsqueeze(2).broadcast_to([P, NT, E1])

            lg = logit[:, :, 0:E1]
            short("short_free", "gate", dve, u, 0)
            wait(dve, "ln2_rstd", u, 0)
            v.memset(logit[:, :, E1:8], LOWEST)
            v.scalar_tensor_tensor(gsum[:], stat2[:, :, 0], -1.0, rstd2[:], ALU.mult, ALU.mult)
            then(v.tensor_tensor(lg, lg, over(rstd2[:]), ALU.mult), "fold_scaled")
            then(v.tensor_tensor(fold[:], over(gsum[:]), spread_over(gate1_sum[:, 0], NT), ALU.mult), "fold_mean")
            then(v.tensor_tensor(lg, lg, fold[:], ALU.add), "fold_added")
            v.tensor_tensor(lg, lg, spread_over(gate1_sum[:, 1], NT), ALU.add).then_inc(sems["fold_done"], 1)

        def route(dve, v, turn, u):
            def then(ins, name):
                ins.then_inc(sems[name], 1)
                wait(dve, name, u, 0)

            if u.kind == "moe0":
                short("short_free", "gate", dve, u, 0)
            else:
                wait(dve, "fold_done", u, 0)
            for t in range(NT):
                ins = v.max(top[:, t], logit[:, t])
            then(ins, "top_ready")
            for t in range(NT):
                v.max_index(top_at[:, t], top[:, t], logit[:, t])
            v.tensor_tensor(lead[:], top[:], top[:, :, 0:1].broadcast_to([P, NT, 8]),
                            ALU.subtract).then_inc(sems["lead_ready"], 1)
            wait(dve, "lead_exp", u, 0)
            if u.kind == "moe1":
                v.tensor_reduce(gsum[:], lead_e[:, :, 0:E1], AX_X, ALU.add)
            v.tensor_copy(top_f[:], top_at[:, :, 0:2])
            then(v.tensor_tensor(gden[:], lead_e[:, :, 0], lead_e[:, :, 1], ALU.add), "gate_den")
            if u.kind == "moe1":
                then(v.scalar_tensor_tensor(gden[:], gsum[:], EPS_GATE, gden[:], ALU.mult, ALU.add), "gate_den_eps")
            then(v.reciprocal(ginv[:], gden[:]), "gate_inv")
            v.tensor_tensor(gw[:], lead_e[:, :, 0:2], ginv[:].unsqueeze(2).broadcast_to([P, NT, 2]), ALU.mult)
            then(v.tensor_tensor(pair[:].rearrange("p t i e -> p (t i) e"), spread_over(iota8[:], 2 * NT),
                                 top_f[:].rearrange("p t i -> p (t i)").unsqueeze(2).broadcast_to([P, 2 * NT, 8]),
                                 ALU.is_equal), "pair_is")
            then(v.tensor_tensor(pair[:], pair[:], gw[:].unsqueeze(3).broadcast_to([P, NT, 2, 8]), ALU.mult),
                 "pair_ready")
            v.tensor_tensor(comb[:, u.par], pair[:, :, 0], pair[:, :, 1], ALU.add).then_inc(sems["comb_ready"], 1)

        @block.vector
        def _(dve):
            v = nc.vector
            n_dve = [0]

            def link(ins):
                n_dve[0] += 1
                ins.then_inc(setup_dve, 1)
                dve.wait_ge(setup_dve, n_dve[0])

            def ready(n):
                dve.wait_ge(setup_full, n)

            def freed(ins):
                ins.then_inc(setup_free, 1)

            dve.wait_ge(ident_made, IDENT)
            v.tensor_copy(ident_b[:], ident[:])
            v.memset(qk_bias[:], 0.0)
            v.tensor_copy(ones_r[:], ones[0:KEYS, :]).then_inc(const_cast, 1)
            dve.wait_ge(const_cast, 1)

            def both_halves(bank, i):
                src = ps[:, bank, i * P:(i + 1) * P].rearrange("p (h c) -> p h c", h=2)
                return src.unsqueeze(2).broadcast_to([P, 2, 2, 64])

            def split_qk(layer, bank):
                for i in range(2):
                    dst_hi = wqk_hi[:, layer, i].rearrange("p h (t c) -> p h t c", t=2)
                    dst_lo = wqk_lo[:, layer, i].rearrange("p h (t c) -> p h t c", t=2)
                    link(v.tensor_copy(dst_hi, both_halves(bank, i)))
                    link(v.tensor_tensor(dst_lo, both_halves(bank, i), dst_hi.bitcast(F32), ALU.subtract))

            def setup(part):
                if part == CASTS:
                    dve.wait_ge(const_made, CONST)
                    v.tensor_tensor(own_k[:], own_k2[:, 0], own_k2[:, 1], ALU.add)
                    v.tensor_copy(pick[:], pick_f).then_inc(const_cast, 1)
                    dve.wait_ge(const_cast, 2)
                elif part == UPS:
                    dve.wait_ge(ld_gate, 16)
                    link(v.tensor_copy(gate0_hi[:], gate_nat[:]))
                    link(v.tensor_tensor(gate0_lo[:], gate_nat[:], gate0_hi[:].bitcast(F32), ALU.subtract))
                    v.memset(logit[:], 0.0)
                else:
                    ready(part)
                    bank = SETUP_BANK[part]
                if part == W0_T:
                    split_qk(0, bank)
                    v.tensor_copy(wv[:, 0], ps[:, bank, 2 * P:3 * P])
                    freed(v.tensor_copy(wo[:, 0], ps[:, bank, 3 * P:4 * P]))
                elif part == CTX_T:
                    v.tensor_copy(ctx_T[:], ps[:, bank, 0:B * KEYS])
                    link(v.tensor_copy(ctx_hi[:], ps[:, bank, 0:B * KEYS]))
                    freed(v.tensor_tensor(ctx_lo[:], ps[:, bank, 0:B * KEYS], ctx_hi[:].bitcast(F32), ALU.subtract))
                elif part in (K0_A, K0_B, K1_A, K1_B):
                    layer, half = int(part >= K1_A), (part - K0_A) % 2 if part < K1_A else part - K1_A
                    link(v.tensor_scalar(k_full[:], ps[:, bank, 0:B * KEYS], qk_bias[:, layer, 1, half:half + 1],
                                         None, ALU.add))
                    hi = k_hi[:, layer, half].rearrange("p b k -> p (b k)")
                    link(v.tensor_copy(hi, k_full[:]))
                    freed(v.tensor_tensor(k_lo[:, layer, half].rearrange("p b k -> p (b k)"), k_full[:],
                                          hi.bitcast(F32), ALU.subtract))
                    dve.wait_ge(setup_free, part)
                elif part in (V0, V1):
                    freed(v.tensor_copy(v_all[:, int(part == V1)], ps[0:KEYS, bank, :].rearrange("p (b d) -> p b d", b=B)))
                elif part == COLS:
                    freed(v.tensor_copy(cols[:], ps[:, bank, 0:29]))
                    dve.wait_ge(setup_free, part)
                    v.tensor_scalar(gate1[:], cols[:, NB_RW:NB_RW + E1], cols[:, NB_RNG:NB_RNG + 1], None, ALU.mult)
                    link(v.tensor_scalar(router_in[:, 1], cols[:, NB_RW:NB_RW + E1], cols[:, NB_RNB:NB_RNB + 1],
                                         None, ALU.mult))
                    link(v.tensor_copy(router_in[:, 0], gate1[:]))
                    link(v.tensor_copy(gate1_hi[:], gate1[:]))
                    link(v.tensor_tensor(gate1_lo[:], gate1[:], gate1_hi[:].bitcast(F32), ALU.subtract))
                elif part == W1_T:
                    freed(v.tensor_copy(w_T[:], ps[:, bank, 0:3 * P].rearrange("p (i c) -> p i c", i=3)))
                elif part == ROWS:
                    freed(v.tensor_copy(spread[:], ps[:, bank, :].rearrange("p (i c) -> p i c", i=4)))
                elif part == JOINED:
                    split_qk(1, bank)
                    freed(v.tensor_copy(wv[:, 1], ps[:, bank, 2 * P:3 * P]))
                elif part == JOINED_BIAS:
                    v.tensor_tensor(qk_bias[:, 1], ps[:, bank, 0:4].rearrange("p (i h) -> p i h", i=2),
                                    cols[:, NB_HB:NB_HB + 4].rearrange("p (i h) -> p i h", i=2), ALU.add)
                    v.tensor_tensor(v_bias[:], ps[0:1, bank, P:2 * P], bhv_sb[:], ALU.add)
                    freed(v.tensor_copy(gate1_sum[:], ps[:, bank, 2 * P:2 * P + 2 * E1]
                                        .rearrange("p (i e) -> p i e", i=2)))
                    dve.wait_ge(setup_free, part)

            def steps(turn):
                for kind, u, arg in phase["steps"]:
                    par = u.par
                    if kind == "setup":
                        setup(arg)
                    elif kind == "mask":
                        op = ALU.is_equal if u.layer == 0 else ALU.not_equal
                        if u is NEXT:
                            dve.wait_ge(sems["next_in"], 1)
                        v.tensor_scalar(mask_q[:, par], mask_in[u.layer][:, par], 0.0, -BIG, op,
                                        ALU.mult).then_inc(sems["mask_ready"], 1)
                    elif kind == "ln":
                        src = x_of(u)
                        if src is x:
                            before = UNITS[u.at - 2]
                            if before.kind == "attn":
                                short("short_free", "attn_out", dve, before, 0)
                            else:
                                wait(dve, "down0_done", before, E0 - 1)
                        for t in range(NT):
                            ins = v.bn_stats(bn[:, par, t], src[:, par, t])
                        ins.then_inc(sems["ln_bn"], 1)
                        wait(dve, "ln_bn", u, 0)
                        for t in range(NT):
                            ins = v.bn_aggr(stat[:, par, t], bn[:, par, t])
                        ins.then_inc(sems["ln_stats"], 1)
                        wait(dve, "ln_stats", u, 0)
                        v.tensor_scalar(var_e[:, par], stat[:, par, :, 1], EPS, None, ALU.add).then_inc(sems["ln_var"], 1)
                    elif kind == "ln_hat":
                        wait(dve, "ln_rstd", u, 0)
                        v.scalar_tensor_tensor(mshift[:, par], stat[:, par, :, 0], -1.0, rstd[:, par], ALU.mult,
                                               ALU.mult).then_inc(sems["mshift_ready"], 1)
                    elif kind == "ln2":
                        wait(dve, "xhat_ready", u, 0)
                        for t in range(NT):
                            ins = v.bn_stats(bn2[:, t], xhat[:, par, t])
                        ins.then_inc(sems["ln2_bn"], 1)
                        wait(dve, "ln2_bn", u, 0)
                        for t in range(NT):
                            ins = v.bn_aggr(stat2[:, t], bn2[:, t])
                        ins.then_inc(sems["ln2_stats"], 1)
                        wait(dve, "ln2_stats", u, 0)
                        v.tensor_scalar(var_e2[:], stat2[:, :, 1], EPS, None, ALU.add).then_inc(sems["ln2_var"], 1)
                    elif kind == "values_in":
                        wait(dve, "values_hi", u, 0)
                        v.tensor_tensor(v_lo[:], values_of_batch(u, turn), v_hi[:].bitcast(F32),
                                        ALU.subtract).then_inc(sems["values_ready"], 1)
                    elif kind == "keys":
                        src = keys_of_batch(k_hi, u, arg, turn)
                        v.tensor_tensor(
                            k_st[:, par, arg, 0, 0:HK].rearrange("p (h k) -> p h k", h=HALF),
                            src.broadcast_to([P, HALF, KEYS]),
                            own_k[:].unsqueeze(2).broadcast_to([P, HALF, KEYS]), ALU.mult).then_inc(sems["keys_hi"], 1)
                    elif kind == "xhat_T":
                        short("short_full", kind, dve, u, arg)
                        wait(dve, "xT_hi_ready", u, arg)
                        v.tensor_tensor(xT_lo[:, par], ps[:, SH, :], xT_hi[:, par].bitcast(F32),
                                        ALU.subtract).then_inc(sems["short_free"], 1)
                    elif kind == "query":
                        short("short_full", kind, dve, u, arg)
                        if arg == 0:
                            short("short_free", "row_valid", dve, u, 0)
                        v.scalar_tensor_tensor(q_full[:, arg], ps[:, SH, :], qk_bias[:, u.layer, 0, arg:arg + 1],
                                               valid[:], ALU.add, ALU.mult).then_inc(sems["short_free"], 1)
                    elif kind == "values":
                        short("short_full", kind, dve, u, arg)
                        v.tensor_tensor(v_st[:, par, arg, :, VAL[arg]],
                                        ps[:, SH, 0:NCH * HALF * HD].rearrange("p (c j) -> p c j", c=NCH),
                                        own_v[:], ALU.mult).then_inc(sems["short_free"], 1)
                    elif kind == "peak":
                        t, quarter = divmod(arg, H // QH)
                        wait(dve, "peak_full", u, arg)
                        v.tensor_reduce(neg_max[:, t, quarter * QH:(quarter + 1) * QH],
                                        ps[:, PK[u.at][arg % len(PK[u.at])], 0:QW].rearrange("p (h k) -> p h k", h=QH),
                                        AX_X, ALU.max, negate=True).then_inc(sems["peak_done"], 1)
                    elif kind == "norm":
                        tok = slice(arg * P, (arg + 1) * P)
                        wait(dve, "den_ready", u, 1)
                        v.reciprocal(inv[:, tok], den[:, tok]).then_inc(sems["inv_ready"], 1)
                        wait(dve, "inv_ready", u, arg)
                        for half in range(2):
                            ins = v.tensor_tensor(heads_T[VAL[half], tok], ps[VAL[half], PV[par][half], tok],
                                                  inv[VAL[half], tok], ALU.mult)
                        ins.then_inc(sems["norm_done"], 1)
                    elif kind == "attn_out":
                        short("short_full", kind, dve, u, arg)
                        wait(dve, "bias_added", u, 0)
                        v.tensor_tensor(x[:, par], ps[:, SH, :].rearrange("p (t d) -> p t d", t=NT), x_bias[:, par],
                                        ALU.add).then_inc(sems["short_free"], 1)
                    elif kind == "gate":
                        short("short_full", kind, dve, u, arg)
                        ne = E0 if u.kind == "moe0" else E1
                        v.tensor_copy(logit[:, :, 0:ne], ps[:, SH, 0:NT * ne].rearrange("p (t e) -> p t e", t=NT))\
                         .then_inc(sems["short_free"], 1)
                    elif kind == "fold":
                        fold_router(dve, v, turn, u)
                    elif kind == "route":
                        route(dve, v, turn, u)
                    elif kind == "down0":
                        wait(dve, "down0_full", u, arg)
                        if arg == 0:
                            wait(dve, "comb_ready", u, 0)
                        else:
                            wait(dve, "down0_done", u, arg - 1)
                        for t in range(NT):
                            ins = v.scalar_tensor_tensor(x[:, par, t], ps[:, 4 + arg % 2, t * P:(t + 1) * P],
                                                         comb[:, par, t, arg:arg + 1], x[:, par, t], ALU.mult, ALU.add)
                        ins.then_inc(sems["down0_done"], 1)
                    elif kind == "up1":
                        t = arg % NT
                        wait(dve, "up1_full", u, arg)
                        if arg >= NT:
                            wait(dve, "hid_norm", u, arg - NT)
                        for e in range(2):
                            ins = v.bn_stats(hbn[:, t, e], ps[:, up1_bank(u, arg), e * FF1:(e + 1) * FF1])
                        ins.then_inc(sems["hid_bn"], 1)
                        wait(dve, "hid_bn", u, arg)
                        for e in range(2):
                            ins = v.bn_aggr(hstat[:, t, e], hbn[:, t, e])
                        ins.then_inc(sems["hid_stats"], 1)
                        wait(dve, "hid_stats", u, arg)
                        v.tensor_scalar(hvar[:, t], hstat[:, t, :, 1], EPS, None, ALU.add).then_inc(sems["hid_var"], 1)
                    elif kind == "hid_hat":
                        t = arg % NT
                        wait(dve, "hid_rstd", u, arg)
                        v.scalar_tensor_tensor(hshift[:, t], hstat[:, t, :, 0], -1.0, hrstd[:, t], ALU.mult,
                                               ALU.mult).then_inc(sems["hid_shift"], 1)
                    elif kind == "down1":
                        wait(dve, "down1_full", u, arg)
                        if arg == 0:
                            wait(dve, "comb_ready", u, 0)
                            dve.wait_ge(sems["acc_free"], 1)
                        else:
                            wait(dve, "down1_done", u, arg - 1)
                        for t in range(NT):
                            src, w = ps[:, DN1[arg % 2], t * P:(t + 1) * P], comb[:, par, t, arg:arg + 1]
                            if arg == 0:
                                ins = v.tensor_scalar(acc[:, par, t], src, w, None, ALU.mult)
                            else:
                                ins = v.scalar_tensor_tensor(acc[:, par, t], src, w, acc[:, par, t], ALU.mult, ALU.add)
                        ins.then_inc(sems["down1_done"], 1)
                    elif kind == "out_stats":
                        wait(dve, "down1_done", u, E1 - 1)
                        for t in range(NT):
                            ins = v.bn_stats(out_bn[:, t], acc[:, par, t])
                        ins.then_inc(sems["out_bn"], 1)
                        wait(dve, "out_bn", u, 0)
                        for t in range(NT):
                            ins = v.bn_aggr(out_stat[:, t], out_bn[:, t])
                        ins.then_inc(sems["out_stats"], 1)
                        wait(dve, "out_stats", u, 0)
                        v.tensor_scalar(out_var[:], out_stat[:, :, 1], EPS, None, ALU.add).then_inc(sems["out_var"], 1)
                    elif kind == "out_shift":
                        wait(dve, "out_rstd", u, 0)
                        v.scalar_tensor_tensor(out_shift[:], out_stat[:, :, 0], -1.0, out_rstd[:], ALU.mult,
                                               ALU.mult).then_inc(sems["out_mshift"], 1)
                    elif kind == "out_hat":
                        wait(dve, "out_hat", u, 0)
                        v.tensor_tensor(acc[:, par], acc[:, par], spread_over(spread[:, 2], NT), ALU.mult).then_inc(sems["out_gain"], 1)
                        wait(dve, "out_gain", u, 0)
                        wait(dve, "out_bias", u, 0)
                        v.tensor_tensor(acc[:, par], acc[:, par], x_bias[:, par], ALU.add).then_inc(sems["out_ready"], 1)

            begin(FIRST)
            steps(-1)
            dve.drain().then_inc(turn_done, 1)
            begin(ORDER)
            with dve.Fori(0, TURNS) as turn:
                start_turn(dve, "dve")
                steps(turn)
                dve.drain().then_inc(turn_done, 1)

        @block.tensor
        def _(pe):
            m = nc.tensor.matmul

            def turn_square(dst, src):
                k = src.shape[0]
                i = ident_b if src.dtype == BF16 else ident
                return nc.tensor.transpose(dst, src, i[0:k, 0:k])

            def split3(dst, w_hi, w_lo, x_hi, x_lo, stop=True):
                m(dst, w_lo, x_hi, start=True, stop=False)
                m(dst, w_hi, x_lo, start=False, stop=False)
                return m(dst, w_hi, x_hi, start=False, stop=stop)

            def free(n):
                pe.wait_ge(setup_free, n)

            pe.wait_ge(const_cast, 1)

            def setup(part):
                if part in (CASTS, UPS):
                    return
                bank = SETUP_BANK[part]
                layer = int(part >= K1_A)
                before = [q for q in range(1, part) if SETUP_BANK[q] == bank]
                needs = {JOINED: W1_T, JOINED_BIAS: COLS, K0_A: CTX_T, K1_A: JOINED_BIAS, V1: JOINED_BIAS}.get(part, 0)
                if max(before + [needs]):
                    free(max(before + [needs]))
                if part == W0_T:
                    pe.wait_ge(ld_w, 16 * 4)
                    for i in range(4):
                        ins = turn_square(ps[:, bank, i * P:(i + 1) * P], w_nat[:, i])
                elif part == CTX_T:
                    pe.wait_ge(ld_ctx, 16)
                    for b in range(B):
                        ins = turn_square(ps[:, bank, b * KEYS:(b + 1) * KEYS], ctx_nat[:, b])
                elif part in (K0_A, K0_B, K1_A, K1_B):
                    half = part in (K0_B, K1_B)
                    ins = split3(ps[:, bank, 0:B * KEYS], wqk_hi[:, layer, 1, int(half)], wqk_lo[:, layer, 1, int(half)],
                                 ctx_hi[:], ctx_lo[:])
                elif part in (V0, V1):
                    for b in range(B):
                        ins = m(ps[0:KEYS, bank, b * P:(b + 1) * P], ctx_T[:, b * KEYS:(b + 1) * KEYS], wv[:, layer],
                                start=True, stop=(layer == 0))
                        if layer:
                            ins = m(ps[0:KEYS, bank, b * P:(b + 1) * P], ones[0:1, 0:KEYS], v_bias[:],
                                    start=False, stop=True)
                elif part == COLS:
                    pe.wait_ge(ld_rows, 16 * 12)
                    ins = turn_square(ps[:, bank, 0:29], rows_sb[:])
                elif part == W1_T:
                    pe.wait_ge(ld_w1, 16 * 4)
                    for i in range(3):
                        ins = turn_square(ps[:, bank, i * P:(i + 1) * P], w_nat[:, 4 + i])
                elif part == ROWS:
                    pe.wait_ge(ld_flat, 16 * 5)
                    ins = m(ps[:, bank, :], ones[0:1, :], flat_sb[:].rearrange("p i d -> p (i d)"), start=True, stop=True)
                elif part == JOINED:
                    pe.wait_ge(ld_head, 16 * 3)
                    for i in range(3):
                        ins = m(ps[:, bank, i * P:(i + 1) * P], w_T[:, i], w_head[:, i], start=True, stop=True)
                elif part == JOINED_BIAS:
                    for i in range(2):
                        for half in range(2):
                            for twice in range(2):
                                m(ps[64 * twice:64 * twice + 64, bank, 2 * i + half:2 * i + half + 1],
                                  w_head[:, i, 64 * half:64 * half + 64], cols[:, NB_B + i:NB_B + i + 1],
                                  start=True, stop=True)
                    m(ps[0:1, bank, P:2 * P], cols[:, NB_B + 2:NB_B + 3], w_head[:, 2], start=True, stop=True)
                    ins = m(ps[:, bank, 2 * P:2 * P + 2 * E1], ones[:], router_in[:].rearrange("p i e -> p (i e)"),
                            start=True, stop=True)
                ins.then_inc(setup_full, 1)

            def steps(turn):
                for kind, u, arg in phase["steps"]:
                    par = u.par
                    if kind in SHORT:
                        short("short_free", kind, pe, u, arg, back=1)
                    if kind == "setup":
                        setup(arg)
                    elif kind == "mask_T":
                        wait(pe, "mask_ready", u, 0)
                        for t in range(NT):
                            ins = turn_square(ps[0:KEYS, SH, t * P // 2:(t + 1) * P // 2].bitcast(BF16), mask_q[:, par, t])
                    elif kind == "xhat_T":
                        wait(pe, "xhat_ready", u, 0)
                        for t in range(NT):
                            ins = turn_square(ps[:, SH, t * P:(t + 1) * P], xhat[:, par, t])
                    elif kind == "row_valid":
                        ins = m(ps[:, SH, :], ones_r[:], shift[0:KEYS, par], start=True, stop=True)
                    elif kind == "query":
                        ins = split3(ps[:, SH, :], wqk_hi[:, u.layer, 0, arg], wqk_lo[:, u.layer, 0, arg],
                                     xT_hi[:, par], xT_lo[:, par])
                    elif kind == "values":
                        wait(pe, "values_ready", u, 0)
                        if phase["steps"] is FIRST:
                            pe.wait_ge(const_cast, 2)
                        for c in range(NCH):
                            for v_part in (v_lo, v_hi):
                                ins = m(ps[:, SH, c * 64:(c + 1) * 64], pick[0:KEYS, 0, c * P:(c + 1) * P],
                                        v_part[:, arg * 64:(arg + 1) * 64], start=(v_part is v_lo), stop=(v_part is v_hi))
                    elif kind == "gate":
                        ne, hi, lo = (E0, gate0_hi, gate0_lo) if u.kind == "moe0" else (E1, gate1_hi, gate1_lo)
                        for t in range(NT):
                            tok = slice(t * P, (t + 1) * P)
                            ins = split3(ps[:, SH, t * ne:(t + 1) * ne], xT_hi[:, par, tok], xT_lo[:, par, tok],
                                         hi[:], lo[:])
                    elif kind == "peak":
                        t, quarter = divmod(arg, H // QH)
                        half, i = divmod(quarter, 2)
                        if arg == 0:
                            wait(pe, "keys_hi", u, 1)
                            wait(pe, "query_ready", u, 1)
                        if arg >= len(PK[u.at]):
                            wait(pe, "peak_done", u, arg - len(PK[u.at]))
                        dst = ps[:, PK[u.at][arg % len(PK[u.at])], 0:QW]
                        m(dst, q_st[:, par, half, t * P:(t + 1) * P], k_st[:, par, half, 0, i * QW:(i + 1) * QW],
                          start=True, stop=False)
                        m(dst, ident_b[:], spread_over(mask_q[:, par, t], QH), start=False, stop=True)\
                            .then_inc(sems["peak_full"], 1)
                    elif kind == "peak_T":
                        wait(pe, "peak_done", u, NPK - 1)
                        for t in range(NT):
                            ins = turn_square(ps[0:H, SH, t * P:(t + 1) * P], neg_max[:, t])
                    elif kind == "scores":
                        half, c = divmod(arg, NCH)
                        chunk = slice(c * P, (c + 1) * P)
                        if arg == 0:
                            wait(pe, "keys_lo", u, 1)
                        if arg >= 2:
                            wait(pe, "exp_done", u, arg - 2)
                        elif u.at and UNITS[u.at - 1].kind == "moe0":
                            wait(pe, "down0_done", UNITS[u.at - 1], E0 - 2 + arg)
                        dst = ps[:, 4 + arg % 2, :]
                        m(dst, k_st[:, par, half, 1, chunk], q_st[:, par, half], start=True, stop=False)
                        m(dst, k_st[:, par, half, 0, chunk], q_st[:, par, half], start=False, stop=False)
                        if arg == 0:
                            short("short_free", "peak_T", pe, u, 0)
                        m(dst, pick[:, half, chunk], shift[:, par], start=False, stop=True)\
                            .then_inc(sems["scores_full"], 1)
                    elif kind == "weigh":
                        half, c = divmod(arg, NCH)
                        wait(pe, "exp_done", u, arg)
                        if arg == 0:
                            short("short_free", "values", pe, u, 1)
                        if arg == NCH and attn_before(u):
                            wait(pe, "norm_done", attn_before(u), NT - 1)
                        m(ps[:, PV[par][half], :], v_st[:, par, half, c], prob[:, arg % 3], start=(c == 0),
                          stop=(c == NCH - 1)).then_inc(sems["weigh_done"], 1)
                    elif kind == "attn_out":
                        wait(pe, "norm_done", u, NT - 1)
                        for t in range(NT):
                            ins = m(ps[:, SH, t * P:(t + 1) * P], heads_T[:, t * P:(t + 1) * P], wo[:, u.layer],
                                    start=True, stop=True)
                    elif kind == "up0":
                        if arg >= 2:
                            wait(pe, "silu_done", u, arg - 2)
                        elif arg == 0 and par == 1:
                            wait(pe, "norm_done", attn_before(u), NT - 1)
                        if arg == 0:
                            short("short_free", "xhat_T", pe, u, 0)
                        w = slice(arg * P, (arg + 1) * P)
                        split3(ps[:, UP0[par] + arg % 2, :], up0_hi[:, w], up0_lo[:, w], xT_hi[:, par], xT_lo[:, par])\
                            .then_inc(sems["up0_full"], 1)
                    elif kind == "down0":
                        wait(pe, "silu_done", u, 2 * arg + 1)
                        if arg >= 2:
                            wait(pe, "down0_done", u, arg - 2)
                        elif UNITS[u.at - 1].kind == "moe0":
                            wait(pe, "down0_done", UNITS[u.at - 1], E0 - 2 + arg)
                        for t in range(NT):
                            for half in range(2):
                                ins = m(ps[:, 4 + arg % 2, t * P:(t + 1) * P], hid_T[:, arg % 2, half, t * P:(t + 1) * P],
                                        dn0[:, arg, half], start=(half == 0), stop=(half == 1))
                        ins.then_inc(sems["down0_full"], 1)
                    elif kind == "up1":
                        g2, t = divmod(arg, NT)
                        if arg == 0:
                            short("short_free", "xhat_T", pe, u, 0)
                        if arg >= 3:
                            wait(pe, "hid_norm", u, arg - 3)
                        elif par == 1:
                            wait(pe, "hid_norm", UNITS[u.at - 1], 2 * NT - 1)
                        tok = slice(t * P, (t + 1) * P)
                        w = slice(g2 * 512, (g2 + 1) * 512)
                        split3(ps[:, up1_bank(u, arg), :], xT_hi[:, par, tok], xT_lo[:, par, tok], up1_hi[:, w], up1_lo[:, w])\
                            .then_inc(sems["up1_full"], 1)
                    elif kind == "turn1":
                        e, half = divmod(arg, 2)
                        if arg % 4 == 0:
                            wait(pe, "hid_norm", u, (e // 2) * NT + NT - 1)
                        if arg >= 2:
                            wait(pe, "relu_done", u, arg - 2)
                        at = (e % 2) * FF1 + half * P
                        for t in range(NT):
                            ins = turn_square(ps[:, 4 + arg % 2, t * P:(t + 1) * P], hnorm[:, e // 2, t, at:at + P])
                        ins.then_inc(sems["turn1_full"], 1)
                    elif kind == "down1":
                        wait(pe, "relu_done", u, 2 * arg + 1)
                        if arg >= 2:
                            wait(pe, "down1_done", u, arg - 2)
                        elif UNITS[u.at - 1].kind == "moe1":
                            wait(pe, "down1_done", UNITS[u.at - 1], E1 - 2 + arg)
                        else:
                            wait(pe, "norm_done", attn_before(u), NT - 1)
                        for t in range(NT):
                            for half in range(2):
                                ins = m(ps[:, DN1[arg % 2], t * P:(t + 1) * P], hid_T[:, arg % 2, half, t * P:(t + 1) * P],
                                        dn1[:, arg, half], start=(half == 0), stop=(half == 1))
                        ins.then_inc(sems["down1_full"], 1)
                    if kind in SHORT:
                        ins.then_inc(sems["short_full"], 1)

            begin(FIRST)
            steps(-1)
            pe.drain().then_inc(turn_done, 1)
            begin(ORDER)
            with pe.Fori(0, TURNS) as turn:
                start_turn(pe, "pe")
                steps(turn)
                pe.drain().then_inc(turn_done, 1)


def kernel(**inputs):
    import numpy as np
    import concourse.bacc as bacc
    from concourse.bass_utils import run_bass_kernel_spmd

    nc = bacc.Bacc("TRN2", target_bir_lowering=False, num_devices=1)
    arrays, args = {}, {}
    for name, value in inputs.items():
        arr = np.ascontiguousarray(value)
        arrays[f"in_{name}"] = arr
        args[name] = nc.dram_tensor(f"in_{name}", arr.shape, mybir.dt.from_np(arr.dtype), kind="ExternalInput").ap()
    out = nc.dram_tensor("out_0", (B, S, D), F32, kind="ExternalOutput").ap()
    build(nc, args, out)
    r = run_bass_kernel_spmd(nc, [arrays], core_ids=[0])
    return r.results[0]["out_0"]
```

```python
from contextlib import ExitStack

import concourse.bass as bass
from concourse import mybir

F32 = mybir.dt.float32
F32R = mybir.dt.float32r
BF16 = mybir.dt.bfloat16
I32 = mybir.dt.int32
U8 = mybir.dt.uint8
U32 = mybir.dt.uint32
ALU = mybir.AluOpType
ACT = mybir.ActivationFunctionType
AX_X = mybir.AxisListType.X

P = 128
B, S, D = 4, 512, 128
NT = S // P
KEYS = 77
H, HD = 16, 8
HALF = H // 2
HK = HALF * KEYS
NCH = -(-HK // P)
VCH = (range(4), range(4, NCH))
HKP = NCH * P
QH = HALF // 2
QW = QH * KEYS
E0, FF0 = 8, 256
E1, FF1 = 4, 256
NPK = NT * H // QH
CROW = 96
CK = CROW + H
BIG = 2.0 ** 100
LOWEST = -3.0e38
EPS = 1e-5
EPS_GATE = 1e-8
SCALE = (float(D) ** -0.5, float(HD) ** -0.5)
TURNS = B // 2


class Unit:
    def __init__(self, at, kind, layer, par):
        self.at, self.kind, self.layer, self.par = at, kind, layer, par


UNITS = [Unit(2 * n + par, kind, layer, par)
         for n, (kind, layer) in enumerate([("attn", 0), ("moe0", 0), ("attn", 1), ("moe1", 1)])
         for par in range(2)]
NEXT = Unit(len(UNITS), "attn", 0, 0)
UNITS.append(NEXT)
NAMES = dict(zip("a0 a1 m0 m1 b0 b1 f0 f1 n0".split(), UNITS))


W0_T, CTX_T, K0_A, K0_B, V0, COLS, W1_T, ROWS, JOINED, JOINED_BIAS, K1_A, K1_B, V1 = range(1, 14)
CASTS, UPS = 0, 14
MOVED = (V0, W1_T, ROWS, V1)
PARTS = dict(CASTS=CASTS, W0_T=W0_T, CTX_T=CTX_T, K0_A=K0_A, K0_B=K0_B, V0=V0, COLS=COLS, W1_T=W1_T, ROWS=ROWS,
             JOINED=JOINED, JOINED_BIAS=JOINED_BIAS, K1_A=K1_A, K1_B=K1_B, V1=V1, UPS=UPS)


def steps_of(text):
    words = [word.split(".") for word in text.split()]
    return [(kind, NAMES[unit], PARTS[arg] if arg in PARTS else int(arg)) for kind, unit, arg in words]


ORDER = steps_of(
    """
mask.a1.0 keys.a1.0 mask_T.a1.0 keys.a1.1 scores.a0.0 ln.a1.0 values_in.a1.0 scores.a0.1 row_valid.a1.0
ln_hat.a1.0 weigh.a0.0 scores.a0.2 scores.a0.3 weigh.a0.1 xhat_T.a1.0 scores.a0.4 weigh.a0.2 query.a1.0
weigh.a0.3 scores.a0.5 query.a1.1 weigh.a0.4 scores.a0.6 values.a1.0 mask.b0.0 weigh.a0.5 peak.a1.0 den.a0.0
peak.a1.1 values.a1.1 peak.a1.2 scores.a0.7 peak.a1.3 peak.a1.4 scores.a0.8 peak.a1.5 peak.a1.6 peak.a1.7
scores.a0.9 keys.b0.0 peak.a1.8 peak.a1.9 peak.a1.10 weigh.a0.6 weigh.a0.7 peak.a1.11 den.a0.1 peak.a1.12
peak.a1.13 weigh.a0.8 peak.a1.14 peak.a1.15 weigh.a0.9 attn_bias.a1.0 peak_T.a1.0
    """
    """
scores.a1.0 norm.a0.0 scores.a1.1 weigh.a1.0 scores.a1.2 scores.a1.3 norm.a0.1 weigh.a1.1 norm.a0.2 norm.a0.3
weigh.a1.2 scores.a1.4 attn_out.a0.0 scores.a1.5 ln.m0.0 keys.b0.1 weigh.a1.3 scores.a1.6 den.a1.0 weigh.a1.4
ln_hat.m0.0 scores.a1.7 weigh.a1.5 weigh.a1.6 xhat_T.m0.0 scores.a1.8 weigh.a1.7 gate.m0.0 scores.a1.9
route.m0.0 norm.a1.0
    """
    """
up0.m0.0 up0.m0.1 weigh.a1.8 den.a1.1 norm.a1.1 weigh.a1.9 up0.m0.2 up0.m0.3 down0.m0.0 norm.a1.2 up0.m0.4
norm.a1.3 up0.m0.5 down0.m0.1 up0.m0.6 down0.m0.2 up0.m0.7 up0.m0.8 attn_out.a1.0 up0.m0.9 up0.m0.10 ln.m1.0
ln_hat.m1.0 down0.m0.3 up0.m0.11 down0.m0.4 xhat_T.m1.0 mask.b1.0 down0.m0.5 up0.m0.12 up0.m0.13 gate.m1.0
values_in.b0.0 up0.m0.14 up0.m0.15 route.m1.0
    """
    """
up0.m1.0 down0.m0.6 down0.m0.7 up0.m1.1 mask_T.b0.0 ln.b0.0 up0.m1.2 up0.m1.3 row_valid.b0.0 ln_hat.b0.0
keys.b1.0 up0.m1.4 down0.m1.0 up0.m1.5 xhat_T.b0.0 up0.m1.6 up0.m1.7 query.b0.0 down0.m1.1 query.b0.1 down0.m1.2
down0.m1.3 up0.m1.8 peak.b0.0 peak.b0.1 up0.m1.9 peak.b0.2 peak.b0.3 values.b0.0 peak.b0.4 peak.b0.5 up0.m1.10
mask_T.b1.0 peak.b0.6 up0.m1.11 peak.b0.7 peak.b0.8 down0.m1.4 attn_bias.b0.0 peak.b0.9 peak.b0.10
row_valid.b1.0 up0.m1.12 up0.m1.13 peak.b0.11 peak.b0.12 up0.m1.14 peak.b0.13 peak.b0.14 up0.m1.15 down0.m1.5
peak.b0.15 down0.m1.6 peak_T.b0.0 down0.m1.7
    """
    """
scores.b0.0 values.b0.1 scores.b0.1 ln.b1.0 scores.b0.2 ln_hat.b1.0 keys.b1.1 weigh.b0.0 weigh.b0.1 scores.b0.3
scores.b0.4 xhat_T.b1.0 weigh.b0.2 weigh.b0.3 values_in.b1.0 query.b1.0 scores.b0.5 query.b1.1 weigh.b0.4
scores.b0.6 values.b1.0 weigh.b0.5 peak.b1.0 peak.b1.1 values.b1.1 scores.b0.7 peak.b1.2 peak.b1.3 weigh.b0.6
den.b0.0 peak.b1.4 peak.b1.5 scores.b0.8 peak.b1.6 peak.b1.7 weigh.b0.7 attn_bias.b1.0 peak.b1.8 peak.b1.9
scores.b0.9 peak.b1.10 peak.b1.11 weigh.b0.8 peak.b1.12 peak.b1.13 den.b0.1 weigh.b0.9 peak.b1.14 peak.b1.15
norm.b0.0 peak_T.b1.0 norm.b0.1
    """
    """
scores.b1.0 scores.b1.1 weigh.b1.0 weigh.b1.1 norm.b0.2 scores.b1.2 scores.b1.3 norm.b0.3 attn_out.b0.0 ln.f0.0
scores.b1.4 scores.b1.5 weigh.b1.2 weigh.b1.3 ln_hat.f0.0 mask.n0.0 scores.b1.6 weigh.b1.4 xhat_T.f0.0
scores.b1.7 out_res.f0.0 ln2.f0.0 den.b1.0 up1.f0.0 up1.f0.1 up1.f0.2 gate.f0.0 weigh.b1.5 scores.b1.8
weigh.b1.6 hid_hat.f0.0 fold.f0.0 weigh.b1.7 hid_hat.f0.1 route.f0.0 scores.b1.9 up1.f0.3 den.b1.1 hid_hat.f0.2
weigh.b1.8 norm.b1.0 hid_hat.f0.3 weigh.b1.9 norm.b1.1 norm.b1.2 norm.b1.3 up1.f0.4
    """
    """
turn1.f0.0 turn1.f0.1 up1.f0.5 attn_out.b1.0 hid_hat.f0.4 up1.f0.6 hid_hat.f0.5 turn1.f0.2 ln.f1.0 turn1.f0.3
hid_hat.f0.6 down1.f0.0 ln_hat.f1.0 up1.f0.7 hid_hat.f0.7 down1.f0.1 xhat_T.f1.0 turn1.f0.4 ln2.f1.0 up1.f1.0
up1.f1.1 hid_hat.f1.0 turn1.f0.5 gate.f1.0 turn1.f0.6 up1.f1.2 out_res.f1.0 hid_hat.f1.1 fold.f1.0 hid_hat.f1.2
up1.f1.3 route.f1.0 mask_T.n0.0 turn1.f0.7 down1.f0.2 values_in.n0.0 hid_hat.f1.3 up1.f1.4 down1.f0.3 up1.f1.5
row_valid.n0.0
    """
    """
turn1.f1.0 turn1.f1.1 hid_hat.f1.4 turn1.f1.2 ln.n0.0 hid_hat.f1.5 up1.f1.6 turn1.f1.3 ln_hat.n0.0 up1.f1.7
hid_hat.f1.6 out_stats.f0.0 hid_hat.f1.7 down1.f1.0 down1.f1.1 xhat_T.n0.0 turn1.f1.4 turn1.f1.5 out_shift.f0.0
keys.n0.0 turn1.f1.6 query.n0.0 keys.n0.1 turn1.f1.7 out_hat.f0.0 down1.f1.2 query.n0.1 down1.f1.3 values.n0.0
out_stats.f1.0 peak.n0.0 peak.n0.1 peak.n0.2 peak.n0.3 out_shift.f1.0 peak.n0.4 peak.n0.5 peak.n0.6 peak.n0.7
peak.n0.8 peak.n0.9 peak.n0.10 attn_bias.n0.0 peak.n0.11 out_hat.f1.0 peak.n0.12 peak.n0.13 values.n0.1
peak.n0.14 peak.n0.15 peak_T.n0.0
    """
    )

FIRST = steps_of(
    """
mask.n0.0 ln.n0.0 mask_T.n0.0 ln_hat.n0.0 setup.n0.W0_T row_valid.n0.0 setup.n0.CTX_T setup.n0.K0_A xhat_T.n0.0
setup.n0.K0_B setup.n0.V0 setup.n0.CASTS query.n0.0 setup.n0.COLS setup.n0.W1_T keys.n0.0 query.n0.1
setup.n0.ROWS keys.n0.1 setup.n0.JOINED setup.n0.JOINED_BIAS peak.n0.0 peak.n0.1 setup.n0.UPS peak.n0.2
setup.n0.K1_A peak.n0.3 peak.n0.4 values_in.n0.0 peak.n0.5 peak.n0.6 peak.n0.7 peak.n0.8 peak.n0.9 values.n0.0
peak.n0.10 peak.n0.11 peak.n0.12 peak.n0.13 values.n0.1 peak.n0.14 peak.n0.15 setup.n0.K1_B attn_bias.n0.0
peak_T.n0.0 setup.n0.V1
    """)

SHORT = ("mask_T", "xhat_T", "row_valid", "query", "values", "gate", "peak_T", "attn_out")


POOL_LAST = {"ln": "ln_rstd", "ln2": "ln2_rstd", "attn_bias": "bias_added", "keys": "keys_lo",
             "query": "query_ready", "up1": "hid_rstd", "out_stats": "out_rstd", "out_res": "out_bias"}


def build(nc: bass.Bass, a, out):
    ctx = ExitStack()
    with ctx:
        def sb(name, shape, dt=F32):
            return ctx.enter_context(nc.sbuf_tensor(name, shape, dt))

        def sem(name):
            return ctx.enter_context(nc.semaphore(name))

        rows_sb = sb("rows_sb", [29, P])
        NB_LNG, NB_LNB, NB_RNG, NB_RNB, NB_B, NB_HB, NB_RW = 0, 8, 16, 17, 18, 21, 25
        cols = sb("cols", [P, 29])
        flat_sb = sb("flat_sb", [1, 4, P])
        bhv_sb = sb("bhv_sb", [1, P])
        spread = sb("spread", [P, 4, P])
        w_T = sb("w_T", [P, 3, P])
        w_head = sb("w_head", [P, 3, P])
        ctx_nat = sb("ctx_nat", [KEYS, B, P])
        ctx_hi = sb("ctx_hi", [P, B * KEYS], F32R)
        ctx_lo = sb("ctx_lo", [P, B * KEYS], F32R)
        ctx_T = sb("ctx_T", [P, B * KEYS])
        k_full = sb("k_full", [P, B * KEYS])
        router_in = sb("router_in", [P, 2, E1])
        gate_nat = sb("gate_nat", [P, E0])

        ones = sb("ones", [P, P])
        ones_r = sb("ones_r", [KEYS, P], F32R)
        ident = sb("ident", [P, P])
        ident_b = sb("ident_b", [P, P], BF16)
        pick = sb("pick", [CK, 2, HKP], F32R)
        own_v = sb("own_v", [P, NCH, HALF * HD])
        own_k2 = sb("own_k2", [P, 2, HALF])
        own_k = sb("own_k", [P, HALF])
        iota8 = sb("iota8", [P, E0])
        neg_half = sb("neg_half", [P, NT])
        table_in = sb("table_in", [P, NT])
        wqk_hi = sb("wqk_hi", [P, 2, 2, 2, P], F32R)
        wqk_lo = sb("wqk_lo", [P, 2, 2, 2, P], F32R)
        qk_bias = sb("qk_bias", [P, 2, 2, 2])
        wv = sb("wv", [P, 2, P])
        v_bias = sb("v_bias", [1, P])
        wo = sb("wo", [P, 2, P])
        k_hi = sb("k_hi", [P, 2, 2, B, KEYS], F32R)
        k_lo = sb("k_lo", [P, 2, 2, B, KEYS], F32R)
        v_all = sb("v_all", [KEYS, 2, B, P])
        gate0_r = sb("gate0_r", [P, 2, E0], F32R)
        gate1 = sb("gate1", [P, E1])
        gate1_r = sb("gate1_r", [P, 2, E1], F32R)
        gate1_sum = sb("gate1_sum", [P, 2, E1])
        up0_hi = sb("up0_hi", [P, E0 * FF0], F32R)
        up0_lo = sb("up0_lo", [P, E0 * FF0], F32R)
        dn0 = sb("dn0", [P, E0, 2, P])
        up1_hi = sb("up1_hi", [P, E1 * FF1], F32R)
        up1_lo = sb("up1_lo", [P, E1 * FF1], F32R)
        dn1 = sb("dn1", [P, E1, 2, P])

        x_in = sb("x_in", [P, 2, NT, P])
        mask_in = [sb("mask0_in", [P, 2, NT, KEYS], I32), sb("mask1_in", [P, 2, NT, KEYS], U8)]
        x = sb("x", [P, 2, NT, P])
        x_bias = sb("x_bias", [P, 2, NT, P])
        bn = sb("bn", [P, 2, NT, 6])
        stat = sb("stat", [P, 2, NT, 2])
        var_e = sb("var_e", [P, 2, NT])
        rstd = sb("rstd", [P, 2, NT])
        mshift = sb("mshift", [P, 2, NT])
        bn2 = sb("bn2", [P, NT, 6])
        stat2 = sb("stat2", [P, NT, 2])
        var_e2 = sb("var_e2", [P, NT])
        rstd2 = sb("rstd2", [P, NT])
        xhat = sb("xhat", [P, 2, NT, P])
        xT_hi = sb("xT_hi", [P, 2, S], F32R)
        xT_lo = sb("xT_lo", [P, 2, S], F32R)
        mask_q = sb("mask_q", [P, 2, NT, KEYS], BF16)
        shift = sb("shift", [CK, 2, S], F32R)
        valid = sb("valid", [P, S])
        q_full = sb("q_full", [P, 2, S])
        q_st = sb("q_st", [P, 2, 2, S], F32R)
        k_st = sb("k_st", [P, 2, 2, 2, HKP], F32R)
        v_hi = sb("v_hi", [KEYS, P], F32R)
        v_lo = sb("v_lo", [KEYS, P], F32R)
        v_st = sb("v_st", [P, 2, 2, NCH, P])
        neg_max = sb("neg_max", [P, NT, H])
        prob = sb("prob", [P, 3, S])
        den = sb("den", [P, S])
        inv = sb("inv", [P, S])
        heads_T = sb("heads_T", [P, S])
        logit = sb("logit", [P, NT, 8])
        top = sb("top", [P, NT, 8])
        top_at = sb("top_at", [P, NT, 8], U32)
        top_f = sb("top_f", [P, NT, 2])
        lead = sb("lead", [P, NT, 8])
        lead_e = sb("lead_e", [P, NT, 8])
        gsum = sb("gsum", [P, NT])
        gden = sb("gden", [P, NT])
        ginv = sb("ginv", [P, NT])
        gw = sb("gw", [P, NT, 2])
        pair = sb("pair", [P, NT, 2, 8])
        comb = sb("comb", [P, 2, NT, 8])
        hid_T = sb("hid_T", [P, 2, 2, S])
        hbn = sb("hbn", [P, NT, 2, 6])
        hstat = sb("hstat", [P, NT, 2, 2])
        hvar = sb("hvar", [P, NT, 2])
        hrstd = sb("hrstd", [P, NT, 2])
        hshift = sb("hshift", [P, NT, 2])
        hnorm = sb("hnorm", [P, 2, NT, 2 * FF1])
        acc = sb("acc", [P, 2, NT, P])
        out_bn = sb("out_bn", [P, NT, 6])
        out_stat = sb("out_stat", [P, NT, 2])
        out_var = sb("out_var", [P, NT])
        out_rstd = sb("out_rstd", [P, NT])
        out_shift = sb("out_shift", [P, NT])
        fold = sb("fold", [P, NT, E1])

        w_nat = prob[:].rearrange("p a c -> p (a c)")[:, 0:7 * P].rearrange("p (i c) -> p i c", i=7)
        pick_f = hid_T[0:CK].rearrange("p a b c -> p (a b c)")[:, 0:2 * HKP].rearrange("p (i c) -> p i c", i=2)
        up0_f = hnorm[:, 0].rearrange("p a c -> p (a c)")
        up1_f = hnorm[:, 1].rearrange("p a c -> p (a c)")[:, 0:E1 * FF1]

        ps = ctx.enter_context(nc.psum_tensor("ps", [P, 8, 512], F32))
        PK = {1: (2, 3, 1), 4: (2, 3), 5: (2, 3), 8: (2, 3, 0)}
        UP0 = (2, 0)
        UP1 = (0, 2, 3)
        DN1 = (6, 1)
        SETUP_BANK = (None, 1, 2, 4, 5, 6, 0, 3, 1, 4, 5, 6, 1, 4)
        SH = 7
        PV = ((6, 0), (1, 6))
        VAL = (slice(0, 64), slice(64, P))
        DEN = (slice(64, P), slice(0, 64))

        ld_rows, ld_flat, ld_w, ld_w1, ld_head, ld_ctx = (
            sem(n) for n in ("ld_rows", "ld_flat", "ld_w", "ld_w1", "ld_head", "ld_ctx"))
        ld_gate, ld_up0, ld_dn, ld_up1 = (sem(n) for n in ("ld_gate", "ld_up0", "ld_dn", "ld_up1"))
        IDENT, CONST = 5, 16
        ident_made, const_made, const_cast = sem("ident_made"), sem("const_made"), sem("const_cast")
        setup_full, setup_free, setup_dve = sem("setup_full"), sem("setup_free"), sem("setup_dve")
        setup_moved, pick_made = sem("setup_moved"), sem("pick_made")

        def wait_part(eng, part):
            if part in MOVED:
                eng.wait_ge(setup_moved, MOVED.index(part) + 1)
            else:
                eng.wait_ge(setup_free, part - sum(p < part for p in MOVED))

        up_hi_made, up_lo_made = sem("up_hi_made"), sem("up_lo_made")
        turn_done = sem("turn_done")

        counts = {}

        phase = {}

        sems = {}
        for name, kinds in {
            "mask_ready": ("mask",), "ln_bn": ("ln",), "ln_stats": ("ln",), "ln_var": ("ln",),
            "ln_rstd": ("ln",), "mshift_ready": ("ln_hat",), "xhat_ready": ("ln_hat",), "ln2_bn": ("ln2",),
            "ln2_stats": ("ln2",), "ln2_var": ("ln2",), "ln2_rstd": ("ln2",), "bias_added": ("attn_bias",),
            "values_hi": ("values_in",), "values_ready": ("values_in",), "keys_hi": ("keys",),
            "keys_lo": ("keys",), "short_full": SHORT, "short_free": SHORT, "xT_hi_ready": ("xhat_T",),
            "query_hi": ("query",), "query_ready": ("query",), "gate_hi": ("gate",), "peak_full": ("peak",),
            "peak_done": ("peak",), "scores_full": ("scores",), "exp_done": ("scores",),
            "weigh_done": ("weigh",), "den_ready": ("den",), "inv_ready": ("norm",), "norm_done": ("norm",),
            "fold_scaled": ("fold",), "fold_mean": ("fold",), "fold_added": ("fold",), "fold_done": ("fold",),
            "gate_den_eps": ("fold",), "top_ready": ("route",), "lead_ready": ("route",),
            "lead_exp": ("route",), "gate_den": ("route",), "gate_inv": ("route",), "pair_is": ("route",),
            "pair_ready": ("route",), "comb_ready": ("route",), "up0_full": ("up0",), "silu_done": ("up0",),
            "down0_full": ("down0",), "down0_done": ("down0",), "up1_full": ("up1",), "hid_bn": ("up1",),
            "hid_stats": ("up1",), "hid_var": ("up1",), "hid_rstd": ("up1",), "hid_shift": ("hid_hat",),
            "hid_norm": ("hid_hat",), "turn1_full": ("turn1",), "relu_done": ("turn1",),
            "down1_full": ("down1",), "down1_done": ("down1",), "next_in": (), "acc_free": (),
            "out_bn": ("out_stats",), "out_stats": ("out_stats",), "out_var": ("out_stats",),
            "out_rstd": ("out_stats",), "out_bias": ("out_res",), "out_mshift": ("out_shift",),
            "out_hat": ("out_shift",), "out_gain": ("out_hat",), "out_ready": ("out_hat",),
        }.items():
            sems[name] = sem(name)
            counts[name] = kinds
        go = {name: sem(f"go_{name}") for name in ("act", "dve", "pe", "sp")}
        turn_loaded, next_loaded = sem("turn_loaded"), sem("next_loaded")
        stored = sem("stored")

        def begin(steps):
            phase["steps"] = steps
            phase["table"] = {}
            for name, kinds in counts.items():
                table, n = phase["table"].setdefault(name, {}), 0
                for kind, u, arg in steps:
                    if kind in kinds:
                        n += 1
                        table[kind, u.at, arg] = n

        def wait(eng, name, u, arg, kind=None, back=0):
            table = phase["table"][name]
            for k in (kind,) if kind else counts[name]:
                n = table.get((k, u.at, arg), 0) - back
                if n >= 1:
                    eng.wait_ge(sems[name], n)

        def short(name, kind, eng, u, arg, back=0):
            wait(eng, name, u, arg, kind, back)

        def batch(u, turn):
            return (turn + (u is NEXT)) * 2 + u.par

        def start_turn(eng, name):
            eng.wait_ge(go[name], 1)
            eng.sem_clear(go[name])

        def keys_of_batch(src, u, half, turn):
            rows = src[:].rearrange("p l h b k -> p (l h b) k")
            return rows[:, bass.ds(batch(u, turn) + (2 * u.layer + half) * B, 1), :].bitcast(F32)

        def values_of_batch(u, turn):
            rows = v_all[:].rearrange("p l b d -> p (l b) d")
            return rows[:, bass.ds(batch(u, turn) + u.layer * B, 1), :].rearrange("p o d -> p (o d)")

        def up1_bank(u, arg):
            return UP1[arg % 3]

        def attn_before(u):
            prev = [v for v in UNITS[:u.at] if v.kind == "attn"]
            return prev[-1] if prev else None

        def x_of(u):
            return x_in if u.kind == "attn" and u.layer == 0 else x

        def spread_over(row, n):
            return row.unsqueeze(1).broadcast_to([row.shape[0], n, row.shape[1]])

        block = ctx.enter_context(nc.Block())

        @block.sync
        def _(sp):
            begin(ORDER)

            def load_batch(turn, par, layer, loaded):
                b = 2 * turn + par
                if layer == 0:
                    if turn:
                        wait(sp, "xhat_ready", UNITS[par], 0)
                        wait(sp, "bias_added", UNITS[par], 0)
                    sp.dma_start(x_in[:, par], a["x"][b].rearrange("(t p) d -> p t d", p=P)).then_inc(loaded, 16)
                if turn:
                    wait(sp, "mask_ready", UNITS[4 * layer + par], 0)
                m = a["mask_Bx1xSxS2_ik1"][b, 0] if layer == 0 else a["mask_BxSxS2_bk1"][b]
                sp.dma_start(mask_in[layer][:, par], m.rearrange("(t p) k -> p t k", p=P)).then_inc(loaded, 16)

            sp.dma_start(w_nat[:, 0], a["L0_xattn_Wq"]).then_inc(ld_w, 16)
            sp.dma_start(x_in[:, 0], a["x"][0].rearrange("(t p) d -> p t d", p=P)).then_inc(next_loaded, 16)
            sp.dma_start(w_nat[:, 3], a["L0_xattn_Wo"]).then_inc(ld_w, 16)
            sp.wait_ge(next_loaded, 32)
            sp.sem_inc(sems["next_in"], 1)
            for n, name in enumerate(["L1_xattn_Wq", "L1_xattn_Wk", "L1_xattn_Wv"]):
                sp.dma_start(w_nat[:, 4 + n], a[name]).then_inc(ld_w1, 16)
            for n, name in enumerate(["L1_xattn_Whq", "L1_xattn_Whk", "L1_xattn_Whv"]):
                sp.dma_start(w_head[:, n].rearrange("p (h d) -> p h d", h=H),
                             a[name].rearrange("h e d -> e h d")).then_inc(ld_head, 16)
            for n, (row, k) in enumerate([("L1_ffn_ln_g", NB_LNG), ("L1_ffn_ln_b", NB_LNB)]):
                sp.dma_start(rows_sb[k:k + 8, :], a[row].rearrange("e (c p) -> (e c) p", p=P)).then_inc(ld_rows, 16)
            for n, name in enumerate(["L1_ffn_rn_g", "L1_ffn_rn_b", "L1_xattn_bq", "L1_xattn_bk", "L1_xattn_bv"]):
                sp.dma_start(rows_sb[NB_RNG + n:NB_RNG + n + 1, :], a[name].unsqueeze(0)).then_inc(ld_rows, 16)
            for n, name in enumerate(["L1_xattn_bhq", "L1_xattn_bhk"]):
                for twice in range(2):
                    sp.dma_start(rows_sb[NB_HB + 2 * n:NB_HB + 2 * n + 2, 64 * twice:64 * twice + 64],
                                 a[name].rearrange("(g h) d -> g (h d)", g=2)).then_inc(ld_rows, 16)
            sp.dma_start(rows_sb[NB_RW:NB_RW + E1, :], a["L1_ffn_router_w"]).then_inc(ld_rows, 16)
            for n, name in enumerate(["L0_xattn_bo", "L1_xattn_bo", "L1_ffn_on_g", "L1_ffn_on_b"]):
                sp.dma_start(flat_sb[:, n], a[name].unsqueeze(0)).then_inc(ld_flat, 16)
            sp.dma_start(bhv_sb[:], a["L1_xattn_bhv"].rearrange("h d -> (h d)").unsqueeze(0)).then_inc(ld_flat, 16)
            sp.dma_start(wo[:, 1], a["L1_xattn_Wo"]).then_inc(ld_w1, 16)
            sp.dma_start(gate_nat[:], a["L0_ffn_gate_w"]).then_inc(ld_gate, 16)
            sp.dma_start(up0_f.rearrange("p (e f) -> p e f", e=E0),
                         a["L0_ffn_w1"].rearrange("e d f -> d e f")).then_inc(ld_up0, 16)
            load_batch(0, 1, 0, turn_loaded)
            load_batch(0, 0, 1, turn_loaded)
            load_batch(0, 1, 1, turn_loaded)
            sp.dma_start(up1_f.rearrange("p (e f) -> p e f", e=E1),
                         a["L1_ffn_w1"].rearrange("e d f -> d e f")).then_inc(ld_up1, 16)
            sp.dma_start(dn0[:], a["L0_ffn_w2"].rearrange("e (c p) d -> p e c d", p=P)).then_inc(ld_dn, 16)
            sp.dma_start(dn1[:], a["L1_ffn_w2"].rearrange("e (c p) d -> p e c d", p=P)).then_inc(ld_dn, 16)
            sp.wait_ge(ld_dn, 32)
            sp.wait_ge(ld_w1, 64)
            sp.wait_ge(turn_loaded, 64)
            sp.sem_inc(turn_done, 1)
            for turn in range(TURNS):
                start_turn(sp, "sp")
                if turn + 1 < TURNS:
                    load_batch(turn + 1, 0, 0, next_loaded)
                if turn:
                    sp.wait_ge(stored, 32 * turn)
                sp.sem_inc(sems["acc_free"], 1)
                if turn + 1 < TURNS:
                    sp.wait_ge(next_loaded, 32 * (turn + 2))
                sp.sem_inc(sems["next_in"], 1)
                if turn + 1 < TURNS:
                    for par, layer in ((1, 0), (0, 1), (1, 1)):
                        load_batch(turn + 1, par, layer, turn_loaded)
                for par in range(2):
                    wait(sp, "out_ready", UNITS[6 + par], 0)
                    sp.dma_start(out[2 * turn + par].rearrange("(t p) d -> p t d", p=P), acc[:, par])\
                      .then_inc(stored, 16)
                if turn + 1 < TURNS:
                    sp.wait_ge(turn_loaded, 64 * (turn + 2))
                    sp.sem_inc(turn_done, 1)
            sp.wait_ge(stored, 16 * B)

        @block.gpsimd
        def _(pool):
            g = nc.gpsimd
            g.memset(ident[:], 0.0).then_inc(ident_made, 1)
            g.memset(ones[:], 1.0).then_inc(ident_made, 1)
            pool.wait_ge(ident_made, 2)
            g.affine_select(out=ident[:], in_=ident[:], compare_op=ALU.not_equal, fill=1.0, base=0,
                            pattern=[[-1, P]], channel_multiplier=1).then_inc(ident_made, 1)
            g.memset(neg_half[:], -0.5).then_inc(ident_made, 1)
            g.memset(shift[:, 0].bitcast(F32), 0.0).then_inc(ident_made, 1)
            pool.wait_ge(ident_made, IDENT)

            def constants():
                g.memset(own_k2[:], 1.0).then_inc(const_made, 1)
                g.memset(own_v[:], 1.0).then_inc(const_made, 1)
                g.memset(pick_f, 0.0).then_inc(const_made, 1)
                g.memset(shift[:, 1].bitcast(F32), 0.0).then_inc(const_made, 1)
                for par in range(2):
                    g.memset(k_st[:, par].rearrange("p h l k -> p (h l) k")[:, :, HK:HKP].bitcast(F32),
                             0.0).then_inc(const_made, 1)
                g.iota(iota8[:], [[1, E0]], base=0, channel_multiplier=0,
                       allow_small_or_imprecise_dtypes=True).then_inc(const_made, 1)
                g.memset(lead[:], 0.0).then_inc(const_made, 1)
                n = 8
                pool.wait_ge(const_made, n)
                for half in range(2):
                    keys_of = pick_f[:, half, 0:HK].rearrange("p (h k) -> p h k", h=HALF)
                    g.affine_select(out=keys_of, in_=keys_of, compare_op=ALU.not_equal, fill=1.0, base=0,
                                    pattern=[[0, HALF], [-1, KEYS]], channel_multiplier=1).then_inc(const_made, 1)
                    pool.wait_ge(const_made, n + 1 + 2 * half)
                    g.affine_select(out=keys_of, in_=keys_of, compare_op=ALU.not_equal, fill=1.0,
                                    base=-(CROW + HALF * half), pattern=[[-1, HALF], [0, KEYS]],
                                    channel_multiplier=1).then_inc(const_made, 1)
                v_view = own_v[:].rearrange("p c (h j) -> p c h j", h=HALF)
                g.affine_select(out=v_view, in_=v_view, compare_op=ALU.is_ge, fill=0.0, base=0,
                                pattern=[[P, NCH], [-KEYS, HALF], [0, HD]], channel_multiplier=1).then_inc(const_made, 1)
                g.affine_select(out=own_k2[:], in_=own_k2[:], compare_op=ALU.is_ge, fill=0.0, base=0,
                                pattern=[[-HALF * HD, 2], [-HD, HALF]], channel_multiplier=1).then_inc(const_made, 1)
                pool.wait_ge(const_made, n + 6)
                g.affine_select(out=v_view, in_=v_view, compare_op=ALU.is_ge, fill=0.0, base=KEYS - 1,
                                pattern=[[-P, NCH], [KEYS, HALF], [0, HD]], channel_multiplier=-1).then_inc(const_made, 1)
                g.affine_select(out=own_k2[:], in_=own_k2[:], compare_op=ALU.is_ge, fill=0.0, base=HD - 1,
                                pattern=[[HALF * HD, 2], [HD, HALF]], channel_multiplier=-1).then_inc(const_made, 1)
                pool.wait_ge(const_made, CONST)

            def meet():
                pool.wait_ge(turn_done, 4)
                pool.sem_clear(range(sems["mask_ready"].num, sems["out_ready"].num + 1))
                pool.sem_clear(turn_done)
                for name in ("act", "dve", "pe", "sp"):
                    pool.drain().then_inc(go[name], 1)

            def steps(turn):
                before = None
                for kind, u, arg in phase["steps"]:
                    if kind == "setup" and arg == CASTS:
                        constants()
                    if kind == "setup" and arg == UPS:
                        wait(pool, *before)
                        before = None
                        pool.wait_ge(up_hi_made, 1)
                        g.tensor_tensor(up0_lo[:], up0_f, up0_hi[:].bitcast(F32), ALU.subtract).then_inc(up_lo_made, 1)
                        pool.wait_ge(up_hi_made, 2)
                        pool.wait_ge(up_lo_made, 1)
                        g.tensor_tensor(up1_lo[:], up1_f, up1_hi[:].bitcast(F32), ALU.subtract).then_inc(up_lo_made, 1)
                        pool.wait_ge(up_lo_made, 2)
                    if kind == "keys" and phase["steps"] is FIRST and arg == 0:
                        wait_part(pool, K0_B)
                        pool.wait_ge(const_cast, 2)
                    if kind == "attn_bias" and phase["steps"] is FIRST:
                        wait_part(pool, ROWS)
                    last = POOL_LAST.get(kind)
                    if last is None:
                        continue
                    if before:
                        wait(pool, *before)
                    before = (last, u, arg)
                    if kind in ("ln", "ln2"):
                        two = kind == "ln2"
                        ve, rs = (var_e2[:], rstd2[:]) if two else (var_e[:, u.par], rstd[:, u.par])
                        pre = "ln2" if two else "ln"
                        wait(pool, pre + "_var", u, 0)
                        g.tensor_tensor(rs, ve, neg_half[:], ALU.pow).then_inc(sems[pre + "_rstd"], 1)
                    elif kind == "attn_bias":
                        if u.layer == 1:
                            wait(pool, "xhat_ready", u, 0)
                        elif u is NEXT:
                            wait(pool, "out_ready", UNITS[6], 0)
                        g.tensor_tensor(x_bias[:, u.par], x_of(u)[:, u.par], spread_over(spread[:, u.layer], NT),
                                        ALU.add).then_inc(sems["bias_added"], 1)
                    elif kind == "keys":
                        src = keys_of_batch(k_lo, u, arg, turn)
                        g.tensor_tensor(
                            k_st[:, u.par, arg, 1, 0:HK].rearrange("p (h k) -> p h k", h=HALF),
                            src.broadcast_to([P, HALF, KEYS]),
                            own_k[:].unsqueeze(2).broadcast_to([P, HALF, KEYS]), ALU.mult).then_inc(sems["keys_lo"], 1)
                    elif kind == "query":
                        wait(pool, "query_hi", u, arg)
                        lo = slice(64, P)
                        g.tensor_tensor(q_st[lo, u.par, arg], q_full[lo, arg], q_st[lo, u.par, arg].bitcast(F32),
                                        ALU.subtract).then_inc(sems["query_ready"], 1)
                    elif kind == "up1":
                        t = arg % NT
                        wait(pool, "hid_var", u, arg)
                        g.tensor_tensor(hrstd[:, t], hvar[:, t], neg_half[:, 0:2], ALU.pow).then_inc(sems["hid_rstd"], 1)
                    elif kind == "out_stats":
                        wait(pool, "out_var", u, 0)
                        g.tensor_tensor(out_rstd[:], out_var[:], neg_half[:], ALU.pow).then_inc(sems["out_rstd"], 1)
                    elif kind == "out_res":
                        wait(pool, "ln_var", u, 0)
                        g.tensor_tensor(x_bias[:, u.par], x[:, u.par], spread_over(spread[:, 3], NT),
                                        ALU.add).then_inc(sems["out_bias"], 1)

                if before:
                    wait(pool, *before)

            begin(FIRST)
            steps(-1)
            begin(ORDER)
            with pool.Fori(0, TURNS) as turn:
                meet()
                steps(turn)

        @block.scalar
        def _(act):
            s = nc.scalar
            act.dma_start(w_nat[:, 1], a["L0_xattn_Wk"]).then_inc(ld_w, 16)
            act.dma_start(mask_in[0][:, 0], a["mask_Bx1xSxS2_ik1"][0, 0].rearrange("(t p) k -> p t k", p=P))\
               .then_inc(next_loaded, 16)
            act.dma_start(w_nat[:, 2], a["L0_xattn_Wv"]).then_inc(ld_w, 16)
            act.dma_start(ctx_nat[:], a["ctx_1024"].rearrange("b k d -> k b d")).then_inc(ld_ctx, 16)
            act.wait_ge(ident_made, IDENT)
            s.activation(table_in[:], neg_half[:], ACT.Exp)

            def steps(turn):
                for kind, u, arg in phase["steps"]:
                    if kind == "setup":
                        if arg in MOVED:
                            act.wait_ge(setup_full, arg)
                            bank = ps[:, SETUP_BANK[arg]]
                            if arg == W1_T:
                                dst, src = w_T[:], bank[:, 0:3 * P].rearrange("p (i c) -> p i c", i=3)
                            elif arg == ROWS:
                                dst, src = spread[:], bank.rearrange("p (i c) -> p i c", i=4)
                            else:
                                dst, src = v_all[:, int(arg == V1)], bank[0:KEYS].rearrange("p (b d) -> p b d", b=B)
                            s.activation(dst, src, ACT.Copy).then_inc(setup_moved, 1)
                        elif arg == CASTS:
                            act.wait_ge(const_made, CONST)
                            s.activation(pick[:], pick_f, ACT.Copy).then_inc(pick_made, 1)
                        elif arg == UPS:
                            act.wait_ge(const_made, CONST)
                            for par in range(2):
                                for half in range(2):
                                    s.activation(v_st[:, par, half, :, DEN[half]], own_v[:], ACT.Copy)
                            act.wait_ge(ld_up0, 16)
                            s.activation(up0_hi[:], up0_f, ACT.Copy).then_inc(up_hi_made, 1)
                            act.wait_ge(ld_up1, 16)
                            s.activation(up1_hi[:], up1_f, ACT.Copy).then_inc(up_hi_made, 1)
                            act.wait_ge(up_hi_made, 2)
                    elif kind == "values_in":
                        if phase["steps"] is FIRST:
                            wait_part(act, V0)
                        if u.at:
                            prev = [v for v in UNITS[:u.at] if v.kind == "attn"]
                            if prev:
                                short("short_full", "values", act, prev[-1], 1)
                        s.activation(v_hi[:], values_of_batch(u, turn), ACT.Copy).then_inc(sems["values_hi"], 1)
                    elif kind == "ln_hat":
                        wait(act, "mshift_ready", u, 0)
                        if u.at >= 2:
                            short("short_full", "xhat_T", act, UNITS[u.at - 2], 0)
                        src = x_of(u)
                        for t in range(NT):
                            ins = s.activation(xhat[:, u.par, t], src[:, u.par, t], ACT.Identity,
                                               bias=mshift[:, u.par, t:t + 1], scale=rstd[:, u.par, t:t + 1])
                        ins.then_inc(sems["xhat_ready"], 1)
                    elif kind == "mask_T":
                        short("short_full", kind, act, u, arg)
                        s.activation(shift[0:KEYS, u.par], ps[0:KEYS, SH, 0:S // 2].bitcast(BF16),
                                     ACT.Copy).then_inc(sems["short_free"], 1)
                    elif kind == "xhat_T":
                        short("short_full", kind, act, u, arg)
                        if u.at >= 2:
                            before = UNITS[u.at - 2]
                            if before.kind == "attn":
                                short("short_full", "query", act, before, 1)
                            elif before.kind == "moe0":
                                wait(act, "up0_full", before, 2 * E0 - 1)
                            else:
                                wait(act, "up1_full", before, 2 * NT - 1)
                        s.activation(xT_hi[:, u.par], ps[:, SH, :], ACT.Copy).then_inc(sems["xT_hi_ready"], 1)
                    elif kind == "query":
                        short("short_free", kind, act, u, arg)
                        s.activation(q_st[:, u.par, arg], q_full[:, arg], ACT.Copy).then_inc(sems["query_hi"], 1)
                    elif kind == "peak_T":
                        short("short_full", kind, act, u, arg)
                        s.activation(shift[CROW:CK, u.par], ps[0:H, SH, :], ACT.Copy).then_inc(sems["short_free"], 1)
                    elif kind == "scores":
                        wait(act, "scores_full", u, arg)
                        if arg >= 3:
                            wait(act, "weigh_done", u, arg - 3)
                        elif attn_before(u):
                            wait(act, "weigh_done", attn_before(u), 2 * NCH - 3 + arg)
                        s.activation(prob[:, arg % 3], ps[:, 4 + arg % 2, :], ACT.Exp,
                                     scale=SCALE[u.layer]).then_inc(sems["exp_done"], 1)
                    elif kind == "den":
                        wait(act, "weigh_done", u, NCH * (arg + 1) - 1)
                        if arg == 0:
                            prev = attn_before(u)
                            if prev:
                                wait(act, "inv_ready", prev, NT - 1)
                        s.activation(den[64 * arg:64 * arg + 64], ps[DEN[arg], PV[u.par][arg], :],
                                     ACT.Copy).then_inc(sems["den_ready"], 1)
                    elif kind == "route":
                        wait(act, "lead_ready", u, 0)
                        s.activation(lead_e[:], lead[:], ACT.Exp).then_inc(sems["lead_exp"], 1)
                    elif kind == "up0":
                        e, half = divmod(arg, 2)
                        wait(act, "up0_full", u, arg)
                        if e >= 2:
                            wait(act, "down0_full", u, e - 2)
                        elif half == 0 and UNITS[u.at - 1].kind == "moe0":
                            wait(act, "down0_full", UNITS[u.at - 1], E0 - 2 + e)
                        s.activation(hid_T[:, e % 2, half], ps[:, UP0[u.par] + arg % 2, :], ACT.Silu).then_inc(sems["silu_done"], 1)
                    elif kind == "hid_hat":
                        g2, t = divmod(arg, NT)
                        wait(act, "hid_shift", u, arg)
                        if t == 0 and UNITS[u.at - 1].kind == "moe1":
                            wait(act, "turn1_full", UNITS[u.at - 1], 4 * g2 + 3)
                        for e in range(2):
                            last = s.activation(hnorm[:, g2, t, e * FF1:(e + 1) * FF1],
                                                ps[:, up1_bank(u, arg), e * FF1:(e + 1) * FF1], ACT.Identity,
                                                bias=hshift[:, t, e:e + 1], scale=hrstd[:, t, e:e + 1])
                        last.then_inc(sems["hid_norm"], 1)
                    elif kind == "out_shift":
                        wait(act, "out_mshift", u, 0)
                        for t in range(NT):
                            ins = s.activation(acc[:, u.par, t], acc[:, u.par, t], ACT.Identity,
                                               bias=out_shift[:, t:t + 1], scale=out_rstd[:, t:t + 1])
                        ins.then_inc(sems["out_hat"], 1)
                    elif kind == "turn1":
                        e, half = divmod(arg, 2)
                        wait(act, "turn1_full", u, arg)
                        if e >= 2:
                            wait(act, "down1_full", u, e - 2)
                        elif half == 0 and UNITS[u.at - 1].kind == "moe1":
                            wait(act, "down1_full", UNITS[u.at - 1], E1 - 2 + e)
                        s.activation(hid_T[:, e % 2, half], ps[:, 4 + arg % 2, :], ACT.Relu,
                                     bias=cols[:, NB_LNB + arg:NB_LNB + arg + 1],
                                     scale=cols[:, NB_LNG + arg:NB_LNG + arg + 1]).then_inc(sems["relu_done"], 1)

            begin(FIRST)
            steps(-1)
            act.drain().then_inc(turn_done, 1)
            begin(ORDER)
            with act.Fori(0, TURNS) as turn:
                start_turn(act, "act")
                steps(turn)
                act.drain().then_inc(turn_done, 1)

        def fold_router(dve, v, turn, u):
            def then(ins, name):
                ins.then_inc(sems[name], 1)
                wait(dve, name, u, 0)

            def over(z):
                return z.unsqueeze(2).broadcast_to([P, NT, E1])

            lg = logit[:, :, 0:E1]
            short("short_free", "gate", dve, u, 0)
            wait(dve, "ln2_rstd", u, 0)
            v.memset(logit[:, :, E1:8], LOWEST)
            v.scalar_tensor_tensor(gsum[:], stat2[:, :, 0], -1.0, rstd2[:], ALU.mult, ALU.mult)
            then(v.tensor_tensor(lg, lg, over(rstd2[:]), ALU.mult), "fold_scaled")
            then(v.tensor_tensor(fold[:], over(gsum[:]), spread_over(gate1_sum[:, 0], NT), ALU.mult), "fold_mean")
            then(v.tensor_tensor(lg, lg, fold[:], ALU.add), "fold_added")
            v.tensor_tensor(lg, lg, spread_over(gate1_sum[:, 1], NT), ALU.add).then_inc(sems["fold_done"], 1)

        def route(dve, v, turn, u):
            def then(ins, name):
                ins.then_inc(sems[name], 1)
                wait(dve, name, u, 0)

            if u.kind == "moe0":
                short("short_free", "gate", dve, u, 0)
            else:
                wait(dve, "fold_done", u, 0)
            for t in range(NT):
                ins = v.max(top[:, t], logit[:, t])
            then(ins, "top_ready")
            for t in range(NT):
                v.max_index(top_at[:, t], top[:, t], logit[:, t])
            v.tensor_tensor(lead[:], top[:], top[:, :, 0:1].broadcast_to([P, NT, 8]),
                            ALU.subtract).then_inc(sems["lead_ready"], 1)
            wait(dve, "lead_exp", u, 0)
            if u.kind == "moe1":
                v.tensor_reduce(gsum[:], lead_e[:, :, 0:E1], AX_X, ALU.add)
            v.tensor_copy(top_f[:], top_at[:, :, 0:2])
            then(v.tensor_tensor(gden[:], lead_e[:, :, 0], lead_e[:, :, 1], ALU.add), "gate_den")
            if u.kind == "moe1":
                then(v.scalar_tensor_tensor(gden[:], gsum[:], EPS_GATE, gden[:], ALU.mult, ALU.add), "gate_den_eps")
            then(v.reciprocal(ginv[:], gden[:]), "gate_inv")
            v.tensor_tensor(gw[:], lead_e[:, :, 0:2], ginv[:].unsqueeze(2).broadcast_to([P, NT, 2]), ALU.mult)
            then(v.tensor_tensor(pair[:].rearrange("p t i e -> p (t i) e"), spread_over(iota8[:], 2 * NT),
                                 top_f[:].rearrange("p t i -> p (t i)").unsqueeze(2).broadcast_to([P, 2 * NT, 8]),
                                 ALU.is_equal), "pair_is")
            then(v.tensor_tensor(pair[:], pair[:], gw[:].unsqueeze(3).broadcast_to([P, NT, 2, 8]), ALU.mult),
                 "pair_ready")
            v.tensor_tensor(comb[:, u.par], pair[:, :, 0], pair[:, :, 1], ALU.add).then_inc(sems["comb_ready"], 1)

        @block.vector
        def _(dve):
            v = nc.vector
            n_dve = [0]

            def link(ins):
                n_dve[0] += 1
                ins.then_inc(setup_dve, 1)
                dve.wait_ge(setup_dve, n_dve[0])

            def ready(n):
                dve.wait_ge(setup_full, n)

            def freed(ins):
                ins.then_inc(setup_free, 1)

            dve.wait_ge(ident_made, IDENT)
            v.tensor_copy(ident_b[:], ident[:])
            v.memset(qk_bias[:], 0.0)
            v.tensor_copy(ones_r[:], ones[0:KEYS, :]).then_inc(const_cast, 1)
            dve.wait_ge(const_cast, 1)

            def both_halves(bank, i):
                src = ps[:, bank, i * P:(i + 1) * P].rearrange("p (h c) -> p h c", h=2)
                return src.unsqueeze(2).broadcast_to([P, 2, 2, 64])

            def split_qk(layer, bank):
                for i in range(2):
                    dst_hi = wqk_hi[:, layer, i].rearrange("p h (t c) -> p h t c", t=2)
                    dst_lo = wqk_lo[:, layer, i].rearrange("p h (t c) -> p h t c", t=2)
                    link(v.tensor_copy(dst_hi, both_halves(bank, i)))
                    link(v.tensor_tensor(dst_lo, both_halves(bank, i), dst_hi.bitcast(F32), ALU.subtract))

            def setup(part):
                if part == CASTS:
                    dve.wait_ge(const_made, CONST)
                    v.tensor_tensor(own_k[:], own_k2[:, 0], own_k2[:, 1], ALU.add).then_inc(const_cast, 1)
                    dve.wait_ge(const_cast, 2)
                elif part == UPS:
                    dve.wait_ge(ld_gate, 16)
                    link(v.tensor_copy(gate0_r[:, 0], gate_nat[:]))
                    link(v.tensor_tensor(gate0_r[:, 1], gate_nat[:], gate0_r[:, 0].bitcast(F32), ALU.subtract))
                    v.memset(logit[:], 0.0)
                elif part not in MOVED:
                    ready(part)
                    bank = SETUP_BANK[part]
                if part == W0_T:
                    split_qk(0, bank)
                    v.tensor_copy(wv[:, 0], ps[:, bank, 2 * P:3 * P])
                    freed(v.tensor_copy(wo[:, 0], ps[:, bank, 3 * P:4 * P]))
                elif part == CTX_T:
                    v.tensor_copy(ctx_T[:], ps[:, bank, 0:B * KEYS])
                    link(v.tensor_copy(ctx_hi[:], ps[:, bank, 0:B * KEYS]))
                    freed(v.tensor_tensor(ctx_lo[:], ps[:, bank, 0:B * KEYS], ctx_hi[:].bitcast(F32), ALU.subtract))
                elif part in (K0_A, K0_B, K1_A, K1_B):
                    layer, half = int(part >= K1_A), (part - K0_A) % 2 if part < K1_A else part - K1_A
                    keys = ps[:, bank, 0:B * KEYS]
                    if layer:
                        link(v.tensor_scalar(k_full[:], keys, qk_bias[:, layer, 1, half:half + 1], None, ALU.add))
                        keys = k_full[:]
                    hi = k_hi[:, layer, half].rearrange("p b k -> p (b k)")
                    link(v.tensor_copy(hi, keys))
                    freed(v.tensor_tensor(k_lo[:, layer, half].rearrange("p b k -> p (b k)"), keys,
                                          hi.bitcast(F32), ALU.subtract))
                    wait_part(dve, part)
                elif part == COLS:
                    link(v.tensor_copy(cols[:], ps[:, bank, 0:29]))
                    v.tensor_scalar(gate1[:], cols[:, NB_RW:NB_RW + E1], cols[:, NB_RNG:NB_RNG + 1], None, ALU.mult)
                    link(v.tensor_scalar(router_in[:, 1], cols[:, NB_RW:NB_RW + E1], cols[:, NB_RNB:NB_RNB + 1],
                                         None, ALU.mult))
                    link(v.tensor_copy(router_in[:, 0], gate1[:]))
                    link(v.tensor_copy(gate1_r[:, 0], gate1[:]))
                    freed(v.tensor_tensor(gate1_r[:, 1], gate1[:], gate1_r[:, 0].bitcast(F32), ALU.subtract))
                elif part == JOINED:
                    split_qk(1, bank)
                    freed(v.tensor_copy(wv[:, 1], ps[:, bank, 2 * P:3 * P]))
                elif part == JOINED_BIAS:
                    v.tensor_tensor(qk_bias[:, 1], ps[:, bank, 0:4].rearrange("p (i h) -> p i h", i=2),
                                    cols[:, NB_HB:NB_HB + 4].rearrange("p (i h) -> p i h", i=2), ALU.add)
                    v.tensor_tensor(v_bias[:], ps[0:1, bank, P:2 * P], bhv_sb[:], ALU.add)
                    freed(v.tensor_copy(gate1_sum[:], ps[:, bank, 2 * P:2 * P + 2 * E1]
                                        .rearrange("p (i e) -> p i e", i=2)))
                    wait_part(dve, part)

            def steps(turn):
                for kind, u, arg in phase["steps"]:
                    par = u.par
                    if kind == "setup":
                        setup(arg)
                    elif kind == "mask":
                        op = ALU.is_equal if u.layer == 0 else ALU.not_equal
                        if u is NEXT:
                            dve.wait_ge(sems["next_in"], 1)
                        v.tensor_scalar(mask_q[:, par], mask_in[u.layer][:, par], 0.0, -BIG, op,
                                        ALU.mult).then_inc(sems["mask_ready"], 1)
                    elif kind == "ln":
                        src = x_of(u)
                        if src is x:
                            before = UNITS[u.at - 2]
                            if before.kind == "attn":
                                short("short_free", "attn_out", dve, before, 0)
                            else:
                                wait(dve, "down0_done", before, E0 - 1)
                        for t in range(NT):
                            ins = v.bn_stats(bn[:, par, t], src[:, par, t])
                        ins.then_inc(sems["ln_bn"], 1)
                        wait(dve, "ln_bn", u, 0)
                        for t in range(NT):
                            ins = v.bn_aggr(stat[:, par, t], bn[:, par, t])
                        ins.then_inc(sems["ln_stats"], 1)
                        wait(dve, "ln_stats", u, 0)
                        v.tensor_scalar(var_e[:, par], stat[:, par, :, 1], EPS, None, ALU.add).then_inc(sems["ln_var"], 1)
                    elif kind == "ln_hat":
                        wait(dve, "ln_rstd", u, 0)
                        v.scalar_tensor_tensor(mshift[:, par], stat[:, par, :, 0], -1.0, rstd[:, par], ALU.mult,
                                               ALU.mult).then_inc(sems["mshift_ready"], 1)
                    elif kind == "ln2":
                        wait(dve, "xhat_ready", u, 0)
                        for t in range(NT):
                            ins = v.bn_stats(bn2[:, t], xhat[:, par, t])
                        ins.then_inc(sems["ln2_bn"], 1)
                        wait(dve, "ln2_bn", u, 0)
                        for t in range(NT):
                            ins = v.bn_aggr(stat2[:, t], bn2[:, t])
                        ins.then_inc(sems["ln2_stats"], 1)
                        wait(dve, "ln2_stats", u, 0)
                        v.tensor_scalar(var_e2[:], stat2[:, :, 1], EPS, None, ALU.add).then_inc(sems["ln2_var"], 1)
                    elif kind == "values_in":
                        wait(dve, "values_hi", u, 0)
                        v.tensor_tensor(v_lo[:], values_of_batch(u, turn), v_hi[:].bitcast(F32),
                                        ALU.subtract).then_inc(sems["values_ready"], 1)
                    elif kind == "keys":
                        src = keys_of_batch(k_hi, u, arg, turn)
                        v.tensor_tensor(
                            k_st[:, par, arg, 0, 0:HK].rearrange("p (h k) -> p h k", h=HALF),
                            src.broadcast_to([P, HALF, KEYS]),
                            own_k[:].unsqueeze(2).broadcast_to([P, HALF, KEYS]), ALU.mult).then_inc(sems["keys_hi"], 1)
                    elif kind == "xhat_T":
                        short("short_full", kind, dve, u, arg)
                        wait(dve, "xT_hi_ready", u, arg)
                        v.tensor_tensor(xT_lo[:, par], ps[:, SH, :], xT_hi[:, par].bitcast(F32),
                                        ALU.subtract).then_inc(sems["short_free"], 1)
                    elif kind == "row_valid":
                        short("short_full", kind, dve, u, arg)
                        v.tensor_scalar(valid[:], ps[:, SH, :], -BIG * (KEYS - 0.5), None,
                                        ALU.is_gt).then_inc(sems["short_free"], 1)
                    elif kind == "query":
                        short("short_full", kind, dve, u, arg)
                        if attn_before(u):
                            wait(dve, "query_ready", attn_before(u), arg)
                        if arg == 0:
                            short("short_free", "row_valid", dve, u, 0)
                        v.scalar_tensor_tensor(q_full[:, arg], ps[:, SH, :], qk_bias[:, u.layer, 0, arg:arg + 1],
                                               valid[:], ALU.add, ALU.mult).then_inc(sems["short_free"], 1)
                    elif kind == "values":
                        short("short_full", kind, dve, u, arg)
                        first, last = VCH[arg][0], VCH[arg][-1] + 1
                        rows = ps[:, SH, 0:(last - first) * P].rearrange("p (c h j) -> p c h j", c=last - first, h=2)
                        for half in range(2):
                            ins = v.tensor_tensor(v_st[:, par, half, first:last, VAL[half]], rows[:, :, half],
                                                  own_v[:, first:last], ALU.mult)
                        ins.then_inc(sems["short_free"], 1)
                    elif kind == "peak":
                        t, quarter = divmod(arg, H // QH)
                        wait(dve, "peak_full", u, arg)
                        if arg == 0 and attn_before(u):
                            short("short_full", "peak_T", dve, attn_before(u), 0)
                        v.tensor_reduce(neg_max[:, t, quarter * QH:(quarter + 1) * QH],
                                        ps[:, PK[u.at][arg % len(PK[u.at])], 0:QW].rearrange("p (h k) -> p h k", h=QH),
                                        AX_X, ALU.max, negate=True).then_inc(sems["peak_done"], 1)
                    elif kind == "norm":
                        tok = slice(arg * P, (arg + 1) * P)
                        wait(dve, "den_ready", u, 1)
                        if arg == 0 and attn_before(u):
                            short("short_full", "attn_out", dve, attn_before(u), 0)
                        v.reciprocal(inv[:, tok], den[:, tok]).then_inc(sems["inv_ready"], 1)
                        wait(dve, "inv_ready", u, arg)
                        for half in range(2):
                            ins = v.tensor_tensor(heads_T[VAL[half], tok], ps[VAL[half], PV[par][half], tok],
                                                  inv[VAL[half], tok], ALU.mult)
                        ins.then_inc(sems["norm_done"], 1)
                    elif kind == "attn_out":
                        short("short_full", kind, dve, u, arg)
                        wait(dve, "bias_added", u, 0)
                        v.tensor_tensor(x[:, par], ps[:, SH, :].rearrange("p (t d) -> p t d", t=NT), x_bias[:, par],
                                        ALU.add).then_inc(sems["short_free"], 1)
                    elif kind == "gate":
                        short("short_full", kind, dve, u, arg)
                        ne = E0 if u.kind == "moe0" else E1
                        both = ps[:, SH, 0:NT * 2 * ne].rearrange("p (t i e) -> p t i e", t=NT, i=2)
                        v.tensor_copy(logit[:, :, 0:ne], both[:, :, 0]).then_inc(sems["gate_hi"], 1)
                        wait(dve, "gate_hi", u, arg)
                        v.tensor_tensor(logit[:, :, 0:ne], logit[:, :, 0:ne], both[:, :, 1],
                                        ALU.add).then_inc(sems["short_free"], 1)
                    elif kind == "fold":
                        fold_router(dve, v, turn, u)
                    elif kind == "route":
                        route(dve, v, turn, u)
                    elif kind == "down0":
                        wait(dve, "down0_full", u, arg)
                        if arg == 0:
                            wait(dve, "comb_ready", u, 0)
                        else:
                            wait(dve, "down0_done", u, arg - 1)
                        for t in range(NT):
                            ins = v.scalar_tensor_tensor(x[:, par, t], ps[:, 4 + arg % 2, t * P:(t + 1) * P],
                                                         comb[:, par, t, arg:arg + 1], x[:, par, t], ALU.mult, ALU.add)
                        ins.then_inc(sems["down0_done"], 1)
                    elif kind == "up1":
                        t = arg % NT
                        wait(dve, "up1_full", u, arg)
                        if arg >= NT:
                            wait(dve, "hid_norm", u, arg - NT)
                        elif UNITS[u.at - 1].kind == "moe1":
                            wait(dve, "hid_norm", UNITS[u.at - 1], arg + NT)
                        for e in range(2):
                            ins = v.bn_stats(hbn[:, t, e], ps[:, up1_bank(u, arg), e * FF1:(e + 1) * FF1])
                        ins.then_inc(sems["hid_bn"], 1)
                        wait(dve, "hid_bn", u, arg)
                        for e in range(2):
                            ins = v.bn_aggr(hstat[:, t, e], hbn[:, t, e])
                        ins.then_inc(sems["hid_stats"], 1)
                        wait(dve, "hid_stats", u, arg)
                        v.tensor_scalar(hvar[:, t], hstat[:, t, :, 1], EPS, None, ALU.add).then_inc(sems["hid_var"], 1)
                    elif kind == "hid_hat":
                        t = arg % NT
                        wait(dve, "hid_rstd", u, arg)
                        v.scalar_tensor_tensor(hshift[:, t], hstat[:, t, :, 0], -1.0, hrstd[:, t], ALU.mult,
                                               ALU.mult).then_inc(sems["hid_shift"], 1)
                    elif kind == "down1":
                        wait(dve, "down1_full", u, arg)
                        if arg == 0:
                            wait(dve, "comb_ready", u, 0)
                            dve.wait_ge(sems["acc_free"], 1)
                        else:
                            wait(dve, "down1_done", u, arg - 1)
                        for t in range(NT):
                            src, w = ps[:, DN1[arg % 2], t * P:(t + 1) * P], comb[:, par, t, arg:arg + 1]
                            if arg == 0:
                                ins = v.tensor_scalar(acc[:, par, t], src, w, None, ALU.mult)
                            else:
                                ins = v.scalar_tensor_tensor(acc[:, par, t], src, w, acc[:, par, t], ALU.mult, ALU.add)
                        ins.then_inc(sems["down1_done"], 1)
                    elif kind == "out_stats":
                        wait(dve, "down1_done", u, E1 - 1)
                        if UNITS[u.at - 1].kind == "moe1":
                            wait(dve, "out_hat", UNITS[u.at - 1], 0)
                        for t in range(NT):
                            ins = v.bn_stats(out_bn[:, t], acc[:, par, t])
                        ins.then_inc(sems["out_bn"], 1)
                        wait(dve, "out_bn", u, 0)
                        for t in range(NT):
                            ins = v.bn_aggr(out_stat[:, t], out_bn[:, t])
                        ins.then_inc(sems["out_stats"], 1)
                        wait(dve, "out_stats", u, 0)
                        v.tensor_scalar(out_var[:], out_stat[:, :, 1], EPS, None, ALU.add).then_inc(sems["out_var"], 1)
                    elif kind == "out_shift":
                        wait(dve, "out_rstd", u, 0)
                        v.scalar_tensor_tensor(out_shift[:], out_stat[:, :, 0], -1.0, out_rstd[:], ALU.mult,
                                               ALU.mult).then_inc(sems["out_mshift"], 1)
                    elif kind == "out_hat":
                        wait(dve, "out_hat", u, 0)
                        v.tensor_tensor(acc[:, par], acc[:, par], spread_over(spread[:, 2], NT),
                                        ALU.mult).then_inc(sems["out_gain"], 1)
                        wait(dve, "out_gain", u, 0)
                        wait(dve, "out_bias", u, 0)
                        v.tensor_tensor(acc[:, par], acc[:, par], x_bias[:, par], ALU.add).then_inc(sems["out_ready"], 1)

            begin(FIRST)
            steps(-1)
            dve.drain().then_inc(turn_done, 1)
            begin(ORDER)
            with dve.Fori(0, TURNS) as turn:
                start_turn(dve, "dve")
                steps(turn)
                dve.drain().then_inc(turn_done, 1)

        @block.tensor
        def _(pe):
            m = nc.tensor.matmul

            def turn_square(dst, src):
                k = src.shape[0]
                i = ident_b if src.dtype == BF16 else ident
                return nc.tensor.transpose(dst, src, i[0:k, 0:k])

            def split3(dst, w_hi, w_lo, x_hi, x_lo, stop=True):
                m(dst, w_lo, x_hi, start=True, stop=False)
                m(dst, w_hi, x_lo, start=False, stop=False)
                return m(dst, w_hi, x_hi, start=False, stop=stop)

            pe.wait_ge(const_cast, 1)

            def setup(part):
                if part in (CASTS, UPS):
                    return
                bank = SETUP_BANK[part]
                layer = int(part >= K1_A)
                before = [q for q in range(1, part) if SETUP_BANK[q] == bank]
                needs = {JOINED: W1_T, JOINED_BIAS: COLS, K0_A: CTX_T, K1_A: JOINED_BIAS, V1: JOINED_BIAS}.get(part, 0)
                for q in {max(before + [0]), needs} - {0}:
                    wait_part(pe, q)
                if part == W0_T:
                    pe.wait_ge(ld_w, 16 * 4)
                    for i in range(4):
                        ins = turn_square(ps[:, bank, i * P:(i + 1) * P], w_nat[:, i])
                elif part == CTX_T:
                    pe.wait_ge(ld_ctx, 16)
                    for b in range(B):
                        ins = turn_square(ps[:, bank, b * KEYS:(b + 1) * KEYS], ctx_nat[:, b])
                elif part in (K0_A, K0_B, K1_A, K1_B):
                    half = part in (K0_B, K1_B)
                    ins = split3(ps[:, bank, 0:B * KEYS], wqk_hi[:, layer, 1, int(half)], wqk_lo[:, layer, 1, int(half)],
                                 ctx_hi[:], ctx_lo[:])
                elif part in (V0, V1):
                    for b in range(B):
                        ins = m(ps[0:KEYS, bank, b * P:(b + 1) * P], ctx_T[:, b * KEYS:(b + 1) * KEYS], wv[:, layer],
                                start=True, stop=(layer == 0))
                        if layer:
                            ins = m(ps[0:KEYS, bank, b * P:(b + 1) * P], ones[0:1, 0:KEYS], v_bias[:],
                                    start=False, stop=True)
                elif part == COLS:
                    pe.wait_ge(ld_rows, 16 * 12)
                    ins = turn_square(ps[:, bank, 0:29], rows_sb[:])
                elif part == W1_T:
                    pe.wait_ge(ld_w1, 16 * 4)
                    for i in range(3):
                        ins = turn_square(ps[:, bank, i * P:(i + 1) * P], w_nat[:, 4 + i])
                elif part == ROWS:
                    pe.wait_ge(ld_flat, 16 * 5)
                    ins = m(ps[:, bank, :], ones[0:1, :], flat_sb[:].rearrange("p i d -> p (i d)"), start=True, stop=True)
                elif part == JOINED:
                    pe.wait_ge(ld_head, 16 * 3)
                    for i in range(3):
                        ins = m(ps[:, bank, i * P:(i + 1) * P], w_T[:, i], w_head[:, i], start=True, stop=True)
                elif part == JOINED_BIAS:
                    for i in range(2):
                        for half in range(2):
                            for twice in range(2):
                                m(ps[64 * twice:64 * twice + 64, bank, 2 * i + half:2 * i + half + 1],
                                  w_head[:, i, 64 * half:64 * half + 64], cols[:, NB_B + i:NB_B + i + 1],
                                  start=True, stop=True)
                    m(ps[0:1, bank, P:2 * P], cols[:, NB_B + 2:NB_B + 3], w_head[:, 2], start=True, stop=True)
                    ins = m(ps[:, bank, 2 * P:2 * P + 2 * E1], ones[:], router_in[:].rearrange("p i e -> p (i e)"),
                            start=True, stop=True)
                ins.then_inc(setup_full, 1)

            def steps(turn):
                for kind, u, arg in phase["steps"]:
                    par = u.par
                    if kind in SHORT:
                        short("short_free", kind, pe, u, arg, back=1)
                    if kind == "setup":
                        setup(arg)
                    elif kind == "mask_T":
                        wait(pe, "mask_ready", u, 0)
                        for t in range(NT):
                            ins = turn_square(ps[0:KEYS, SH, t * P // 2:(t + 1) * P // 2].bitcast(BF16), mask_q[:, par, t])
                    elif kind == "xhat_T":
                        wait(pe, "xhat_ready", u, 0)
                        for t in range(NT):
                            ins = turn_square(ps[:, SH, t * P:(t + 1) * P], xhat[:, par, t])
                    elif kind == "row_valid":
                        ins = m(ps[:, SH, :], ones_r[:], shift[0:KEYS, par], start=True, stop=True)
                    elif kind == "query":
                        ins = split3(ps[:, SH, :], wqk_hi[:, u.layer, 0, arg], wqk_lo[:, u.layer, 0, arg],
                                     xT_hi[:, par], xT_lo[:, par])
                    elif kind == "values":
                        wait(pe, "values_ready", u, 0)
                        if phase["steps"] is FIRST:
                            pe.wait_ge(pick_made, 1)
                        for n, c in enumerate(VCH[arg]):
                            for v_part in (v_lo, v_hi):
                                ins = m(ps[:, SH, n * P:(n + 1) * P], pick[0:KEYS, 0, c * P:(c + 1) * P], v_part[:],
                                        start=(v_part is v_lo), stop=(v_part is v_hi))
                    elif kind == "gate":
                        ne, gate = (E0, gate0_r) if u.kind == "moe0" else (E1, gate1_r)
                        for t in range(NT):
                            tok, dst = slice(t * P, (t + 1) * P), 2 * ne * t
                            m(ps[:, SH, dst:dst + 2 * ne], xT_hi[:, par, tok], gate[:].rearrange("p i e -> p (i e)"),
                              start=True, stop=False)
                            ins = m(ps[:, SH, dst:dst + ne], xT_lo[:, par, tok], gate[:, 0], start=False, stop=True)
                    elif kind == "peak":
                        t, quarter = divmod(arg, H // QH)
                        half, i = divmod(quarter, 2)
                        if arg == 0:
                            wait(pe, "keys_hi", u, 1)
                            wait(pe, "query_ready", u, 1)
                        if arg >= len(PK[u.at]):
                            wait(pe, "peak_done", u, arg - len(PK[u.at]))
                        elif UNITS[u.at - 1].kind == "attn":
                            wait(pe, "peak_done", UNITS[u.at - 1], NPK - 1)
                        elif UNITS[u.at - 1].kind == "moe0":
                            wait(pe, "silu_done", UNITS[u.at - 2], 2 * E0 - 1)
                        else:
                            wait(pe, "hid_norm", UNITS[u.at - 1], 2 * NT - 1)
                        dst = ps[:, PK[u.at][arg % len(PK[u.at])], 0:QW]
                        m(dst, q_st[:, par, half, t * P:(t + 1) * P], k_st[:, par, half, 0, i * QW:(i + 1) * QW],
                          start=True, stop=False)
                        m(dst, ident_b[:], spread_over(mask_q[:, par, t], QH), start=False, stop=True)\
                            .then_inc(sems["peak_full"], 1)
                    elif kind == "peak_T":
                        wait(pe, "peak_done", u, NPK - 1)
                        for t in range(NT):
                            ins = turn_square(ps[0:H, SH, t * P:(t + 1) * P], neg_max[:, t])
                    elif kind == "scores":
                        half, c = divmod(arg, NCH)
                        chunk = slice(c * P, (c + 1) * P)
                        if arg == 0:
                            wait(pe, "keys_lo", u, 1)
                        if arg >= 2:
                            wait(pe, "exp_done", u, arg - 2)
                        elif u.at and UNITS[u.at - 1].kind == "moe0":
                            wait(pe, "down0_done", UNITS[u.at - 1], E0 - 2 + arg)
                        elif u.at:
                            wait(pe, "exp_done", UNITS[u.at - 1], 2 * NCH - 2 + arg)
                        dst = ps[:, 4 + arg % 2, :]
                        m(dst, k_st[:, par, half, 1, chunk], q_st[:, par, half], start=True, stop=False)
                        m(dst, k_st[:, par, half, 0, chunk], q_st[:, par, half], start=False, stop=False)
                        if arg == 0:
                            short("short_free", "peak_T", pe, u, 0)
                        m(dst, pick[:, half, chunk], shift[:, par], start=False, stop=True)\
                            .then_inc(sems["scores_full"], 1)
                    elif kind == "weigh":
                        half, c = divmod(arg, NCH)
                        wait(pe, "exp_done", u, arg)
                        if arg == 0:
                            short("short_free", "values", pe, u, 1)
                        if arg == NCH and attn_before(u):
                            wait(pe, "norm_done", attn_before(u), NT - 1)
                        m(ps[:, PV[par][half], :], v_st[:, par, half, c], prob[:, arg % 3], start=(c == 0),
                          stop=(c == NCH - 1)).then_inc(sems["weigh_done"], 1)
                    elif kind == "attn_out":
                        wait(pe, "norm_done", u, NT - 1)
                        for t in range(NT):
                            ins = m(ps[:, SH, t * P:(t + 1) * P], heads_T[:, t * P:(t + 1) * P], wo[:, u.layer],
                                    start=True, stop=True)
                    elif kind == "up0":
                        if arg >= 2:
                            wait(pe, "silu_done", u, arg - 2)
                        elif arg == 0 and par == 1:
                            wait(pe, "norm_done", attn_before(u), NT - 1)
                        if arg == 0:
                            short("short_free", "xhat_T", pe, u, 0)
                        w = slice(arg * P, (arg + 1) * P)
                        split3(ps[:, UP0[par] + arg % 2, :], up0_hi[:, w], up0_lo[:, w], xT_hi[:, par], xT_lo[:, par])\
                            .then_inc(sems["up0_full"], 1)
                    elif kind == "down0":
                        wait(pe, "silu_done", u, 2 * arg + 1)
                        if arg >= 2:
                            wait(pe, "down0_done", u, arg - 2)
                        elif UNITS[u.at - 1].kind == "moe0":
                            wait(pe, "down0_done", UNITS[u.at - 1], E0 - 2 + arg)
                        else:
                            wait(pe, "exp_done", UNITS[u.at - 1], 2 * NCH - 2 + arg)
                        for t in range(NT):
                            for half in range(2):
                                ins = m(ps[:, 4 + arg % 2, t * P:(t + 1) * P], hid_T[:, arg % 2, half, t * P:(t + 1) * P],
                                        dn0[:, arg, half], start=(half == 0), stop=(half == 1))
                        ins.then_inc(sems["down0_full"], 1)
                    elif kind == "up1":
                        g2, t = divmod(arg, NT)
                        if arg == 0:
                            short("short_free", "xhat_T", pe, u, 0)
                        if arg >= 3:
                            wait(pe, "hid_norm", u, arg - 3)
                        elif par == 1:
                            wait(pe, "hid_norm", UNITS[u.at - 1], 2 * NT - 1)
                        tok = slice(t * P, (t + 1) * P)
                        w = slice(g2 * 512, (g2 + 1) * 512)
                        split3(ps[:, up1_bank(u, arg), :], xT_hi[:, par, tok], xT_lo[:, par, tok], up1_hi[:, w], up1_lo[:, w])\
                            .then_inc(sems["up1_full"], 1)
                    elif kind == "turn1":
                        e, half = divmod(arg, 2)
                        if arg % 4 == 0:
                            wait(pe, "hid_norm", u, (e // 2) * NT + NT - 1)
                        if arg >= 2:
                            wait(pe, "relu_done", u, arg - 2)
                        elif UNITS[u.at - 1].kind == "moe1":
                            wait(pe, "relu_done", UNITS[u.at - 1], 2 * E1 - 2 + arg)
                        else:
                            wait(pe, "exp_done", UNITS[u.at - 1], 2 * NCH - 2 + arg)
                        at = (e % 2) * FF1 + half * P
                        for t in range(NT):
                            ins = turn_square(ps[:, 4 + arg % 2, t * P:(t + 1) * P], hnorm[:, e // 2, t, at:at + P])
                        ins.then_inc(sems["turn1_full"], 1)
                    elif kind == "down1":
                        wait(pe, "relu_done", u, 2 * arg + 1)
                        if arg >= 2:
                            wait(pe, "down1_done", u, arg - 2)
                        elif UNITS[u.at - 1].kind == "moe1":
                            wait(pe, "down1_done", UNITS[u.at - 1], E1 - 2 + arg)
                        else:
                            wait(pe, "norm_done", attn_before(u), NT - 1)
                        for t in range(NT):
                            for half in range(2):
                                ins = m(ps[:, DN1[arg % 2], t * P:(t + 1) * P], hid_T[:, arg % 2, half, t * P:(t + 1) * P],
                                        dn1[:, arg, half], start=(half == 0), stop=(half == 1))
                        ins.then_inc(sems["down1_full"], 1)
                    if kind in SHORT:
                        ins.then_inc(sems["short_full"], 1)

            begin(FIRST)
            steps(-1)
            pe.drain().then_inc(turn_done, 1)
            begin(ORDER)
            with pe.Fori(0, TURNS) as turn:
                start_turn(pe, "pe")
                steps(turn)
                pe.drain().then_inc(turn_done, 1)


def kernel(**inputs):
    import numpy as np
    import concourse.bacc as bacc
    from concourse.bass_utils import run_bass_kernel_spmd

    nc = bacc.Bacc("TRN2", target_bir_lowering=False, num_devices=1)
    arrays, args = {}, {}
    for name, value in inputs.items():
        arr = np.ascontiguousarray(value)
        arrays[f"in_{name}"] = arr
        args[name] = nc.dram_tensor(f"in_{name}", arr.shape, mybir.dt.from_np(arr.dtype), kind="ExternalInput").ap()
    out = nc.dram_tensor("out_0", (B, S, D), F32, kind="ExternalOutput").ap()
    build(nc, args, out)
    r = run_bass_kernel_spmd(nc, [arrays], core_ids=[0])
    return r.results[0]["out_0"]
```
